# Optimizing a Trainium2 kernel written in Bass

```python
import numpy as np
import jax
import jax.numpy as jnp

def _softmax(x, axis=-1):
    return jax.nn.softmax(x, axis=axis)

def _gelu(x):
    return jax.nn.gelu(x, approximate=True)

def _silu(x):
    return jax.nn.silu(x)

def _sigmoid(x):
    return jax.nn.sigmoid(x)

def _layernorm(x, axis=-1, eps=1e-05):
    m = jnp.mean(x, axis=axis, keepdims=True)
    v = jnp.var(x, axis=axis, keepdims=True)
    return (x - m) / jnp.sqrt(v + eps)

def _scatter_add(tgt, idx, src, axis=0):
    return tgt.at[idx].add(src)

def _segment_sum(src, seg, n):
    return jax.ops.segment_sum(src, seg, n)
kernel_name = 'mk_prb_d1_jaxref_r4_38b7f1'

def setup_inputs(seed: int=0):
    np.random.seed(seed)
    _w = jnp.asarray

    def _L0_attn_setup():
        import jax, jax.numpy as jnp
        import numpy as np
        N_EMBD = 256
        B, T = (8, 512)

        def _wkv_scan(time_decay, time_first, k, v):
            Bn, Tn, Cn = k.shape
            kT = jnp.swapaxes(k, 0, 1)
            vT = jnp.swapaxes(v, 0, 1)
            aa0 = jnp.zeros((Bn, Cn), k.dtype)
            bb0 = jnp.zeros((Bn, Cn), k.dtype)
            pp0 = jnp.full((Bn, Cn), -10000.0, k.dtype)

            def step(carry, kv):
                aa, bb, pp = carry
                kt, vt = kv
                ww = time_first + pp
                p = jnp.maximum(pp, ww)
                e1 = jnp.exp(pp - p)
                e2 = jnp.exp(ww - p)
                wkv_t = (e1 * aa + e2 * vt) / (e1 * bb + e2 + 1e-06)
                ww2 = time_decay + pp
                p2 = jnp.maximum(pp, ww2)
                e1b = jnp.exp(pp - p2)
                e2b = jnp.exp(ww2 - p2)
                aa = e1b * aa + e2b * vt
                bb = e1b * bb + e2b
                return ((aa, bb, p2), wkv_t)
            _, wkvT = jax.lax.scan(step, (aa0, bb0, pp0), (kT, vT))
            return jnp.swapaxes(wkvT, 0, 1)
        key = jax.random.key(seed)
        ks = jax.random.split(key, 7)
        C = N_EMBD
        x = jax.random.normal(ks[0], (B, T, C), dtype=jnp.float32)
        time_decay = jnp.full((C,), -1.0, dtype=jnp.float32)
        time_first = jnp.full((C,), 0.5, dtype=jnp.float32)
        s = 1.0 / np.sqrt(C)
        key_w = jax.random.uniform(ks[1], (C, C), jnp.float32, -s, s)
        value_w = jax.random.uniform(ks[2], (C, C), jnp.float32, -s, s)
        recep_w = jax.random.uniform(ks[3], (C, C), jnp.float32, -s, s)
        out_w = jax.random.uniform(ks[4], (C, C), jnp.float32, -s, s)
        return {'x': x, 'time_decay': time_decay, 'time_first': time_first, 'key_w': key_w, 'value_w': value_w, 'recep_w': recep_w, 'out_w': out_w}
    _L0_attn_in = _L0_attn_setup()

    def _L0_ffn_setup():
        import jax, jax.numpy as jnp
        import numpy as np
        DIM = 256
        INTER = 256
        E = 8
        TOPK = 2
        ROUTE_SCALE = 1.0
        SHARED_INTER = 512
        B, S = (4, 512)

        def _moe_forward(x, gate_w, gate_b, w1, b1, w3, b3, w2, b2, ws1, bs1, ws3, bs3, ws2, bs2):
            Bq, Sq, D = x.shape
            xt = x.reshape(-1, D)
            logits = (xt @ gate_w.T + gate_b).astype(jnp.float32)
            scores = jax.nn.softmax(logits, axis=-1)
            top_w, top_i = jax.lax.top_k(scores, TOPK)
            weights = (top_w * ROUTE_SCALE).astype(x.dtype)
            gate_dense = jnp.sum(jax.nn.one_hot(top_i, E, dtype=x.dtype) * weights[..., None], axis=1)

            def expert(w1e, b1e, w3e, b3e, w2e, b2e):
                h = jax.nn.silu(xt @ w1e.T + b1e) * (xt @ w3e.T + b3e)
                return h @ w2e.T + b2e
            outs = jax.vmap(expert)(w1, b1, w3, b3, w2, b2)
            y = jnp.einsum('etd,te->td', outs, gate_dense)
            z = jax.nn.silu(xt @ ws1.T + bs1) * (xt @ ws3.T + bs3) @ ws2.T + bs2
            return (y + z).reshape(Bq, Sq, D)
        key = jax.random.key(seed)
        ks = jax.random.split(key, 10)

        def w(k, shape, scale=0.02):
            return jax.random.normal(k, shape, jnp.float32) * scale
        return {'x': jax.random.normal(ks[0], (B, S, DIM), jnp.float32), 'gate_w': w(ks[1], (E, DIM)), 'gate_b': jnp.zeros((E,), jnp.float32), 'w1': w(ks[2], (E, INTER, DIM)), 'b1': jnp.zeros((E, INTER), jnp.float32), 'w3': w(ks[3], (E, INTER, DIM)), 'b3': jnp.zeros((E, INTER), jnp.float32), 'w2': w(ks[4], (E, DIM, INTER)), 'b2': jnp.zeros((E, DIM), jnp.float32), 'ws1': w(ks[5], (SHARED_INTER, DIM)), 'bs1': jnp.zeros((SHARED_INTER,), jnp.float32), 'ws3': w(ks[6], (SHARED_INTER, DIM)), 'bs3': jnp.zeros((SHARED_INTER,), jnp.float32), 'ws2': w(ks[7], (DIM, SHARED_INTER)), 'bs2': jnp.zeros((DIM,), jnp.float32)}
    _L0_ffn_in = _L0_ffn_setup()
    _d = {'L0_attn_x': _L0_attn_in['x'], 'L0_attn_time_decay': _L0_attn_in['time_decay'], 'L0_attn_time_first': _L0_attn_in['time_first'], 'L0_attn_key_w': _L0_attn_in['key_w'], 'L0_attn_value_w': _L0_attn_in['value_w'], 'L0_attn_recep_w': _L0_attn_in['recep_w'], 'L0_attn_out_w': _L0_attn_in['out_w'], 'L0_ffn_gate_w': _L0_ffn_in['gate_w'], 'L0_ffn_gate_b': _L0_ffn_in['gate_b'], 'L0_ffn_w1': _L0_ffn_in['w1'], 'L0_ffn_b1': _L0_ffn_in['b1'], 'L0_ffn_w3': _L0_ffn_in['w3'], 'L0_ffn_b3': _L0_ffn_in['b3'], 'L0_ffn_w2': _L0_ffn_in['w2'], 'L0_ffn_b2': _L0_ffn_in['b2'], 'L0_ffn_ws1': _L0_ffn_in['ws1'], 'L0_ffn_bs1': _L0_ffn_in['bs1'], 'L0_ffn_ws3': _L0_ffn_in['ws3'], 'L0_ffn_bs3': _L0_ffn_in['bs3'], 'L0_ffn_ws2': _L0_ffn_in['ws2'], 'L0_ffn_bs2': _L0_ffn_in['bs2']}
    _x0 = _d['L0_attn_x']
    _d['L0_attn_x'] = jax.random.normal(jax.random.fold_in(jax.random.key(seed), 1), (2, 2048, 256), dtype=_x0.dtype)
    del _x0
    return _d

def reference(L0_attn_x, L0_attn_time_decay, L0_attn_time_first, L0_attn_key_w, L0_attn_value_w, L0_attn_recep_w, L0_attn_out_w, L0_ffn_gate_w, L0_ffn_gate_b, L0_ffn_w1, L0_ffn_b1, L0_ffn_w3, L0_ffn_b3, L0_ffn_w2, L0_ffn_b2, L0_ffn_ws1, L0_ffn_bs1, L0_ffn_ws3, L0_ffn_bs3, L0_ffn_ws2, L0_ffn_bs2):

    def _L0_attn_ref(x, time_decay, time_first, key_w, value_w, recep_w, out_w):
        import jax, jax.numpy as jnp
        import numpy as np
        N_EMBD = 256
        B, T = (8, 512)

        def _wkv_scan(time_decay, time_first, k, v):
            Bn, Tn, Cn = k.shape
            kT = jnp.swapaxes(k, 0, 1)
            vT = jnp.swapaxes(v, 0, 1)
            aa0 = jnp.zeros((Bn, Cn), k.dtype)
            bb0 = jnp.zeros((Bn, Cn), k.dtype)
            pp0 = jnp.full((Bn, Cn), -10000.0, k.dtype)

            def step(carry, kv):
                aa, bb, pp = carry
                kt, vt = kv
                ww = time_first + pp
                p = jnp.maximum(pp, ww)
                e1 = jnp.exp(pp - p)
                e2 = jnp.exp(ww - p)
                wkv_t = (e1 * aa + e2 * vt) / (e1 * bb + e2 + 1e-06)
                ww2 = time_decay + pp
                p2 = jnp.maximum(pp, ww2)
                e1b = jnp.exp(pp - p2)
                e2b = jnp.exp(ww2 - p2)
                aa = e1b * aa + e2b * vt
                bb = e1b * bb + e2b
                return ((aa, bb, p2), wkv_t)
            _, wkvT = jax.lax.scan(step, (aa0, bb0, pp0), (kT, vT))
            return jnp.swapaxes(wkvT, 0, 1)
        k = jnp.einsum('btc,dc->btd', x, key_w)
        v = jnp.einsum('btc,dc->btd', x, value_w)
        r = jax.nn.sigmoid(jnp.einsum('btc,dc->btd', x, recep_w))
        wkv = _wkv_scan(time_decay, time_first, k, v)
        return jnp.einsum('btc,dc->btd', r * wkv, out_w)

    def _L0_ffn_ref(x, gate_w, gate_b, w1, b1, w3, b3, w2, b2, ws1, bs1, ws3, bs3, ws2, bs2):
        import jax, jax.numpy as jnp
        import numpy as np
        DIM = 256
        INTER = 256
        E = 8
        TOPK = 2
        ROUTE_SCALE = 1.0
        SHARED_INTER = 512
        B, S = (4, 512)

        def _moe_forward(x, gate_w, gate_b, w1, b1, w3, b3, w2, b2, ws1, bs1, ws3, bs3, ws2, bs2):
            Bq, Sq, D = x.shape
            xt = x.reshape(-1, D)
            logits = (xt @ gate_w.T + gate_b).astype(jnp.float32)
            scores = jax.nn.softmax(logits, axis=-1)
            top_w, top_i = jax.lax.top_k(scores, TOPK)
            weights = (top_w * ROUTE_SCALE).astype(x.dtype)
            gate_dense = jnp.sum(jax.nn.one_hot(top_i, E, dtype=x.dtype) * weights[..., None], axis=1)

            def expert(w1e, b1e, w3e, b3e, w2e, b2e):
                h = jax.nn.silu(xt @ w1e.T + b1e) * (xt @ w3e.T + b3e)
                return h @ w2e.T + b2e
            outs = jax.vmap(expert)(w1, b1, w3, b3, w2, b2)
            y = jnp.einsum('etd,te->td', outs, gate_dense)
            z = jax.nn.silu(xt @ ws1.T + bs1) * (xt @ ws3.T + bs3) @ ws2.T + bs2
            return (y + z).reshape(Bq, Sq, D)
        return _moe_forward(x, gate_w, gate_b, w1, b1, w3, b3, w2, b2, ws1, bs1, ws3, bs3, ws2, bs2)
    x = L0_attn_x
    xn = _layernorm(x, axis=-1)
    x = x + _L0_attn_ref(xn, L0_attn_time_decay, L0_attn_time_first, L0_attn_key_w, L0_attn_value_w, L0_attn_recep_w, L0_attn_out_w) + _L0_ffn_ref(xn, L0_ffn_gate_w, L0_ffn_gate_b, L0_ffn_w1, L0_ffn_b1, L0_ffn_w3, L0_ffn_b3, L0_ffn_w2, L0_ffn_b2, L0_ffn_ws1, L0_ffn_bs1, L0_ffn_ws3, L0_ffn_bs3, L0_ffn_ws2, L0_ffn_bs2)
    return x

_drawn_inputs = setup_inputs


def setup_inputs(seed=0):
    import zlib

    import numpy as np

    out = dict(_drawn_inputs(seed))
    spreads = {'L0_attn_time_decay': (-1.0, 0.6),
     'L0_attn_time_first': (0.5, 0.6),
     'L0_ffn_gate_b': (0.0, 0.549),
     'L0_ffn_b1': (0.0, 0.8),
     'L0_ffn_b3': (0.0, 0.8),
     'L0_ffn_b2': (0.0, 1.03),
     'L0_ffn_bs1': (0.0, 0.8),
     'L0_ffn_bs3': (0.0, 0.8),
     'L0_ffn_bs2': (0.0, 0.372)}
    factors = {'L0_attn_value_w': 4.632,
     'L0_attn_recep_w': 8.0,
     'L0_attn_out_w': 4.587,
     'L0_ffn_w1': 8.0,
     'L0_ffn_w3': 8.0,
     'L0_ffn_w2': 8.0,
     'L0_ffn_ws1': 3.721,
     'L0_ffn_ws3': 4.098}
    for name, (base, spread) in spreads.items():
        noise = np.random.default_rng([zlib.crc32(name.encode()), seed]).standard_normal(out[name].shape)
        drawn = base * np.exp(spread * noise) if base else spread * noise
        out[name] = jnp.asarray(drawn.astype(out[name].dtype))
    for name, factor in factors.items():
        out[name] = (out[name] * factor).astype(out[name].dtype)
    return out
```

```python
from contextlib import ExitStack

import concourse.bass as bass
from concourse import mybir

F32 = mybir.dt.float32
F32R = mybir.dt.float32r
BF16 = mybir.dt.bfloat16
I32 = mybir.dt.int32
ALU = mybir.AluOpType
ACT = mybir.ActivationFunctionType
AX_X = mybir.AxisListType.X
ds = bass.ds

P = 128
B, T, C = 2, 2048, 256
TOK = B * T
E, TOPK = 8, 2
FF, SF = 256, 512
KC = C // P
KS = SF // P
TIMES = 256
STEP = B * TIMES
NSTEP = T // TIMES
Q = STEP // P
NT = TOK // P
HALF = TIMES // P
WALL = 2 * FF + C
TILES = -(-(TOK * TOPK // P + E - 1) // 4) * 4
EPS = 1e-5
PAIRS = TOPK * NT
BATCH = 8


class At:

    def __init__(self, u, r, n):
        self.u, self.r, self.n = u, r, n

    def plus(self, d):
        q, r = divmod(self.r + d, self.n)
        return At(self.u + q if q else self.u, r, self.n)

    @property
    def i(self):
        return self.u * self.n + self.r

    def uses(self, bufs):
        assert self.n % bufs == 0
        return self.u * (self.n // bufs) + self.r // bufs

    def buf(self, bufs):
        return self.r % bufs


def at_least(eng, sem, value):
    if isinstance(value, int) and value <= 0:
        return
    eng.wait_ge(sem, value)


def rounds(eng, n, count, body):
    for r in range(n):
        body(At(0, r, n))
    with eng.Fori(1, count // n - 1) as u:
        for r in range(n):
            body(At(u, r, n))
    for r in range(n):
        body(At(count // n - 1, r, n))


class Own:

    def __init__(self, eng, sem):
        self.eng, self.sem, self.n = eng, sem, 0

    def mark(self, ins):
        ins.then_inc(self.sem, 1)
        self.n += 1

    def wait(self):
        self.eng.wait_ge(self.sem, self.n)

    def link(self, ins):
        self.mark(ins)
        self.wait()


class OwnIn:

    def __init__(self, eng, sem, at, per, done=0):
        self.eng, self.sem, self.base, self.per, self.n = eng, sem, at.i * per + done, per, 0

    def mark(self, ins):
        ins.then_inc(self.sem, 1)
        self.n += 1

    def wait(self):
        self.eng.wait_ge(self.sem, self.base + self.n)

    def link(self, ins):
        self.mark(ins)
        self.wait()

    def close(self):
        assert self.n == self.per, (self.n, self.per)


def build(nc, x, decay, first, wvr, wo, gate_w, gate_b, w_all, b_all, ws13, bs1, bs3, ws2, bs2, out):
    xn_d = nc.dram_tensor("xn_rows", (TOK, C), F32, kind="Internal").ap()
    xT_d = nc.dram_tensor("xn_columns", (P, NSTEP, KC * STEP), F32, kind="Internal").ap()
    y_d = nc.dram_tensor("expert_rows", (TILES * P, C), F32, kind="Internal").ap()

    with ExitStack() as kept:
        def sb(name, shape, dt, stack=kept):
            return stack.enter_context(nc.sbuf_tensor(name, shape, dt))

        ident = sb("ident", [P, P], F32)
        slots = sb("slots", [P, TOPK, NT], I32)
        gates = sb("gates", [P, TOPK, NT], F32)
        tile_tok = sb("tile_tok", [P, TILES], I32)
        tile_exp = sb("tile_exp", [P, TILES], I32)
        raw_vr = sb("raw_vr", [P, KC, 2 * C], F32)
        raw_o = sb("raw_o", [P, KC, C], F32)
        raw_s13 = sb("raw_s13", [P, KC, 2 * SF], F32)
        raw_s2 = sb("raw_s2", [P, KS, C], F32)
        vec_tf = sb("vec_tf", [P, KC], F32)
        vec_td = sb("vec_td", [P, KC], F32)
        vec_b1 = sb("vec_b1", [P, KS], F32)
        vec_b3 = sb("vec_b3", [P, KS], F32)
        row_b2 = sb("row_b2", [P, C], F32)

        with ExitStack() as experts:
            w_hi = sb("w_hi", [P, E, KC, WALL], F32R, experts)
            w_lo = sb("w_lo", [P, E, KC, WALL], F32R, experts)
            bias_hl = sb("bias_hl", [2, E, WALL], F32R, experts)
            ones2 = sb("ones2", [2, P], F32R, experts)
            route(nc, x, gate_w, gate_b, w_all, b_all, xn_d, xT_d, ident, slots, gates, tile_tok,
                  tile_exp, w_hi, w_lo, bias_hl, ones2, raw_s13)
            run_experts(nc, xn_d, y_d, ident, tile_tok, tile_exp, w_hi, w_lo, bias_hl, ones2,
                        [(raw_vr[:], wvr.rearrange("(k p) n -> p k n", p=P)),
                         (raw_o[:], wo.rearrange("(k p) n -> p k n", p=P)),
                         (raw_s13[:], ws13.rearrange("(k p) n -> p k n", p=P)),
                         (raw_s2[:], ws2.rearrange("(k p) n -> p k n", p=P)),
                         (vec_tf[:], first),
                         (vec_td[:], decay),
                         (vec_b1[:], bs1),
                         (vec_b3[:], bs3),
                         (row_b2[:], bs2.rearrange("(a n) -> a n", a=1).broadcast_to([P, C]))])
        mix(nc, x, xT_d, y_d, out, slots, gates, raw_vr, raw_o, raw_s13, raw_s2, vec_tf, vec_td,
            vec_b1, vec_b3, row_b2)


def route(nc, x, gate_w, gate_b, w_all, b_all, xn_d, xT_d, ident, slots, gates, tile_tok,
          tile_exp, w_hi, w_lo, bias_hl, ones2, spare):
    with ExitStack() as ctx:
        def sb(name, shape, dt):
            return ctx.enter_context(nc.sbuf_tensor(name, shape, dt))

        def bank(name, shape):
            return ctx.enter_context(nc.psum_tensor(name, shape, F32))

        def sem(name):
            return ctx.enter_context(nc.semaphore(name))

        xin = [spare[:, b, :].rearrange("p (q c) -> p q c", q=Q) for b in range(2)]
        xn = [sb(f"xn{b}", [P, Q, C], F32) for b in range(2)]
        xT = [sb(f"xT{b}", [P, KC, STEP], F32) for b in range(2)]
        w_raw = [sb(f"w_raw{b}", [P, KC, WALL], F32) for b in range(2)]
        stats = [sb(f"stats{b}", [P, Q, 6], F32) for b in range(2)]
        mv = [sb(f"mv{b}", [P, Q, 2], F32) for b in range(2)]
        var = [sb(f"var{b}", [P, Q], F32) for b in range(2)]
        std = [sb(f"std{b}", [P, Q], F32) for b in range(2)]
        rstd = [sb(f"rstd{b}", [P, Q], F32) for b in range(2)]
        gw = sb("gw", [P, KC, E], F32)
        gb = sb("gb", [P, E], F32)
        BR = E * WALL // P
        b_raw = sb("b_raw", [P, BR], F32)
        b_hi = sb("b_hi", [P, BR], F32R)
        b_lo = sb("b_lo", [P, BR], F32R)
        ones_f = sb("ones_f", [P, P], F32)
        before_f = sb("before_f", [P, P], F32)
        ones = sb("ones", [P, P], BF16)
        before = sb("before", [P, P], BF16)
        lane_i = sb("lane_i", [P, P], I32)
        lane = sb("lane", [P, P], F32)
        token_i = sb("token_i", [P, NT], I32)
        token = sb("token", [P, NT], F32)
        desc_i = sb("desc_i", [P, E], I32)
        desc = sb("desc", [P, E], F32)
        logits = sb("logits", [P, NT, E], F32)
        score = sb("score", [P, NT, E], F32)
        work = sb("work", [P, NT, E], F32)
        work2 = sb("work2", [P, NT, E], F32)
        hot = [sb(f"hot{k}", [P, NT, E], F32) for k in range(TOPK)]
        red = sb("red", [P, NT], F32)
        red2 = sb("red2", [P, NT], F32)
        mask = sb("mask", [P, E, NT], BF16)
        keep = sb("keep", [P, E, NT], F32)
        filled = sb("filled", [P, E, NT], F32)
        place = sb("place", [P, E, NT], F32)
        ntile_i = sb("ntile_i", [P, E], I32)
        ntile = sb("ntile", [P, E], F32)
        last = sb("last", [P, E], F32)
        start = sb("start", [P, E], F32)
        tile_no = sb("tile_no", [P, TILES, E], F32)
        slot_f = sb("slot_f", [P, PAIRS], F32)
        part_i = sb("part_i", [P, 2, PAIRS], I32)
        part = sb("part", [P, 2, PAIRS], F32)
        hot_in = [sb(f"hot_in{b}", [P, BATCH, P], F32R) for b in range(2)]
        hot_tile = sb("hot_tile", [P, BATCH, TILES], F32)
        hot_tok = [sb(f"hot_tok{b}", [P, BATCH, TILES], F32R) for b in range(2)]
        tok_f = sb("tok_f", [P, TILES], F32)

        ps_T = [[bank(f"ps_T{b}{k}", [P, STEP]) for k in range(KC)] for b in range(2)]
        ps_L = [bank(f"ps_L{b}", [P, Q, E]) for b in range(2)]
        ps_cnt = bank("ps_cnt", [P, 2, E * NT])
        ps_tok = bank("ps_tok", [P, TILES])

        s_const = sem("s_const")
        s_pool = sem("s_pool")
        s_small = sem("s_small")
        s_xin = [sem(f"s_xin{b}") for b in range(2)]
        s_w = [sem(f"s_w{b}") for b in range(2)]
        s_whi = sem("s_whi")
        s_wlo = sem("s_wlo")
        s_stat = sem("s_stat")
        s_var = sem("s_var")
        s_go = sem("s_go")
        s_std = sem("s_std")
        s_xn = sem("s_xn")
        s_T = sem("s_T")
        s_xT = sem("s_xT")
        s_L = sem("s_L")
        s_Lc = sem("s_Lc")
        s_xout = [sem(f"s_xout{b}") for b in range(2)]
        s_Tout = [sem(f"s_Tout{b}") for b in range(2)]
        s_bhi = sem("s_bhi")
        s_blo = sem("s_blo")
        s_bias = sem("s_bias")
        s_dve = sem("s_dve")
        s_shift = sem("s_shift")
        s_exp = sem("s_exp")
        s_mask = sem("s_mask")
        s_cnt = sem("s_cnt")
        s_hot = sem("s_hot")
        s_hotmm = sem("s_hotmm")
        s_tok = sem("s_tok")

        xv = x.rearrange("b (i h p) c -> i p b h c", h=HALF, p=P)
        xnv = xn_d.rearrange("(b i h p) c -> i p b h c", b=B, h=HALF, p=P)
        wv = w_all.rearrange("e (k p) n -> e p k n", p=P)

        with nc.Block() as block:

            @block.sync
            def _(sp):
                def load_x(a):
                    at_least(sp, s_xn, a.i - 1)
                    for b in range(B):
                        sp.dma_start(xin[a.buf(2)][:, b * HALF:(b + 1) * HALF, :],
                                     xv[ds(a.i, 1), :, b, :, :].rearrange("o p h c -> p (o h) c")
                                     ).then_inc(s_xin[a.buf(2)], 16)

                def load_w(a):
                    at_least(sp, s_whi, a.i - 1)
                    at_least(sp, s_wlo, a.i - 1)
                    sp.dma_start(w_raw[a.buf(2)][:], wv[ds(a.i, 1)].rearrange("o p k n -> p (o k) n")
                                 ).then_inc(s_w[a.buf(2)], 16)

                load_x(At(0, 0, 2))
                sp.dma_start(gw[:], gate_w).then_inc(s_small, 16)
                sp.dma_start(gb[:], gate_b.rearrange("(a n) -> a n", a=1).broadcast_to([P, E])
                             ).then_inc(s_small, 16)
                sp.dma_start(b_raw[:], b_all.rearrange("(p r) -> p r", p=P)).then_inc(s_small, 16)
                load_x(At(0, 1, 2))
                load_w(At(0, 0, 2))
                load_w(At(0, 1, 2))

                def step(a, more=True):
                    at_least(sp, s_xn, a.i + 1)
                    for b in range(B):
                        sp.dma_start(xnv[ds(a.i, 1), :, b, :, :].rearrange("o p h c -> p (o h) c"),
                                     xn[a.buf(2)][:, b * HALF:(b + 1) * HALF, :]
                                     ).then_inc(s_xout[a.buf(2)], 16)
                    if more:
                        load_x(a.plus(2))
                    at_least(sp, s_xT, a.i + 1)
                    sp.dma_start(xT_d[:, ds(a.i, 1), :].rearrange("p o n -> p (o n)"),
                                 xT[a.buf(2)][:].rearrange("p k n -> p (k n)")
                                 ).then_inc(s_Tout[a.buf(2)], 16)
                    if more:
                        load_w(a.plus(2))

                step(At(0, 0, 2))
                step(At(0, 1, 2))
                with sp.Fori(1, NSTEP // 2 - 1) as u:
                    step(At(u, 0, 2))
                    step(At(u, 1, 2))
                step(At(NSTEP // 2 - 1, 0, 2), False)
                step(At(NSTEP // 2 - 1, 1, 2), False)

                sp.wait_ge(s_bhi, 1)
                sp.wait_ge(s_blo, 1)
                bias = bias_hl[:].rearrange("h e n -> h (e n)").bitcast(F32)
                sp.dma_start(bias[0:1, :].rearrange("o (p r) -> o p r", p=P), b_hi[:].bitcast(F32)).then_inc(s_bias, 16)
                sp.dma_start(bias[1:2, :].rearrange("o (p r) -> o p r", p=P), b_lo[:].bitcast(F32)).then_inc(s_bias, 16)
                for b in range(2):
                    sp.wait_ge(s_xout[b], NSTEP // 2 * 32)
                    sp.wait_ge(s_Tout[b], NSTEP // 2 * 16)
                sp.wait_ge(s_bias, 32)

            @block.gpsimd
            def _(pool):
                own = Own(pool, s_pool)
                nc.gpsimd.memset(ones_f[:], 1.0).then_inc(s_pool, 1)
                own.n += 1
                own.mark(nc.gpsimd.memset(ident[:], 0.0))
                own.wait()
                nc.gpsimd.affine_select(out=ident[:], in_=ident[:], compare_op=ALU.not_equal, fill=1.0,
                                        base=0, pattern=[[-1, P]], channel_multiplier=1).then_inc(s_const, 1)
                nc.gpsimd.affine_select(out=before_f[:], in_=ones_f[:], compare_op=ALU.is_gt, fill=0.0,
                                        base=0, pattern=[[1, P]], channel_multiplier=-1).then_inc(s_const, 1)
                nc.gpsimd.iota(lane_i[:], pattern=[[1, P]], base=0, channel_multiplier=0).then_inc(s_const, 1)
                nc.gpsimd.iota(token_i[:].rearrange("p (i b h) -> p i b h", b=B, h=HALF),
                               pattern=[[TIMES, NSTEP], [T, B], [P, HALF]], base=0,
                               channel_multiplier=1).then_inc(s_const, 1)
                nc.gpsimd.iota(desc_i[:], pattern=[[-1, E]], base=E, channel_multiplier=0).then_inc(s_const, 1)

                def split(a):
                    pool.wait_ge(s_whi, a.i + 1)
                    nc.gpsimd.tensor_tensor(w_lo[:, ds(a.i, 1)].rearrange("p o k n -> p (o k) n"),
                                            w_raw[a.buf(2)][:],
                                            w_hi[:, ds(a.i, 1)].rearrange("p o k n -> p (o k) n").bitcast(F32),
                                            ALU.subtract).then_inc(s_wlo, 1)

                rounds(pool, 2, E, split)

            @block.scalar
            def _(act):
                def root(a):
                    act.wait_ge(s_var, a.i + 1)
                    nc.scalar.activation(std[a.buf(2)][:], var[a.buf(2)][:], ACT.Sqrt).then_inc(s_std, 1)

                def step(a, more=True):
                    if more:
                        root(a.plus(1))
                    act.wait_ge(s_T, a.i + 1)
                    at_least(act, s_Tout[a.buf(2)], a.uses(2) * 16)
                    at_least(act, s_L, a.i - 1)
                    nc.scalar.activation(xT[a.buf(2)][:, 0, :], ps_T[a.buf(2)][0][:], ACT.Copy)
                    nc.scalar.activation(xT[a.buf(2)][:, 1, :], ps_T[a.buf(2)][1][:], ACT.Copy
                                         ).then_inc(s_xT, 1)
                    act.wait_ge(s_w[a.buf(2)], (a.uses(2) + 1) * 16)
                    nc.scalar.activation(w_hi[:, ds(a.i, 1)].rearrange("p o k n -> p (o k) n"),
                                         w_raw[a.buf(2)][:], ACT.Copy).then_inc(s_whi, 1)

                root(At(0, 0, 2))
                step(At(0, 0, 2))
                step(At(0, 1, 2))
                with act.Fori(1, NSTEP // 2 - 1) as u:
                    step(At(u, 0, 2))
                    step(At(u, 1, 2))
                step(At(NSTEP // 2 - 1, 0, 2))
                step(At(NSTEP // 2 - 1, 1, 2), False)
                act.wait_ge(s_shift, 1)
                nc.scalar.activation(score[:], work[:], ACT.Exp).then_inc(s_exp, 1)

            @block.tensor
            def _(pe):
                def turn(a):
                    pe.wait_ge(s_xn, a.i + 1)
                    at_least(pe, s_xT, a.i - 1)
                    for k in range(KC):
                        for q in range(Q):
                            mm = nc.tensor.transpose(ps_T[a.buf(2)][k][:, q * P:(q + 1) * P],
                                                     xn[a.buf(2)][:, q, k * P:(k + 1) * P], ident[:])
                    mm.then_inc(s_T, 1)

                def gate(a):
                    pe.wait_ge(s_xT, a.i + 1)
                    at_least(pe, s_Lc, a.i - 1)
                    for q in range(Q):
                        for k in range(KC):
                            mm = nc.tensor.matmul(ps_L[a.buf(2)][:, q, :],
                                                  xT[a.buf(2)][:, k, q * P:(q + 1) * P], gw[:, k, :],
                                                  start=(k == 0), stop=(k == KC - 1))
                    mm.then_inc(s_L, 1)

                pe.wait_ge(s_const, 5)
                pe.wait_ge(s_small, 48)
                turn(At(0, 0, 2))
                turn(At(0, 1, 2))
                gate(At(0, 0, 2))
                turn(At(1, 0, 2))
                gate(At(0, 1, 2))
                turn(At(1, 1, 2))
                gate(At(1, 0, 2))
                with pe.Fori(2, NSTEP // 2) as u:
                    turn(At(u, 0, 2))
                    gate(At(u - 1, 1, 2))
                    turn(At(u, 1, 2))
                    gate(At(u, 0, 2))
                gate(At(NSTEP // 2 - 1, 1, 2))

                pe.wait_ge(s_mask, 2)
                nc.tensor.matmul(ps_cnt[:, 0, :], before[:], mask[:].rearrange("p e j -> p (e j)"),
                                 start=True, stop=True)
                nc.tensor.matmul(ps_cnt[:, 1, :], ones[:], mask[:].rearrange("p e j -> p (e j)"),
                                 start=True, stop=True).then_inc(s_cnt, 1)
                for n in range(PAIRS // BATCH):
                    pe.wait_ge(s_hot, n + 1)
                    for g in range(BATCH):
                        mm = nc.tensor.matmul(ps_tok[:], hot_in[n % 2][:, g, :], hot_tok[n % 2][:, g, :],
                                              start=(n == 0 and g == 0),
                                              stop=(n == PAIRS // BATCH - 1 and g == BATCH - 1))
                    mm.then_inc(s_hotmm, 1)

            @block.vector
            def _(dve):
                dve.wait_ge(s_const, 5)
                nc.vector.tensor_copy(lane[:], lane_i[:])
                nc.vector.tensor_copy(token[:], token_i[:])
                nc.vector.tensor_copy(desc[:], desc_i[:])
                nc.vector.tensor_copy(ones[:], ones_f[:])
                nc.vector.tensor_copy(ones2[:], ones_f[0:2, :])
                nc.vector.memset(keep[:], 1.0)
                nc.vector.tensor_copy(before[:], before_f[:]).then_inc(s_mask, 1)
                dve.wait_ge(s_mask, 1)
                nc.vector.memset(keep[:, :, 0:1], 0.0)
                PER = 2

                def measure(a):
                    own = OwnIn(dve, s_stat, a, PER)
                    dve.wait_ge(s_xin[a.buf(2)], (a.uses(2) + 1) * 32)
                    for q in range(Q):
                        ins = nc.vector.bn_stats(stats[a.buf(2)][:, q, :], xin[a.buf(2)][:, q, :])
                    own.link(ins)
                    dve.sem_inc(s_go, 1)
                    for q in range(Q):
                        ins = nc.vector.bn_aggr(mv[a.buf(2)][:, q, :], stats[a.buf(2)][:, q, :])
                    own.link(ins)
                    own.close()
                    at_least(dve, s_std, a.i - 1)
                    nc.vector.tensor_scalar(var[a.buf(2)][:], mv[a.buf(2)][:, :, 1], EPS, None, ALU.add
                                            ).then_inc(s_var, 1)

                def norm(a):
                    own = OwnIn(dve, s_dve, a, 1)
                    dve.wait_ge(s_std, a.i + 1)
                    own.link(nc.vector.reciprocal(rstd[a.buf(2)][:], std[a.buf(2)][:]))
                    own.close()
                    at_least(dve, s_T, a.i - 1)
                    at_least(dve, s_xout[a.buf(2)], a.uses(2) * 32)
                    for q in range(Q):
                        ins = nc.vector.tensor_scalar(xn[a.buf(2)][:, q, :], xin[a.buf(2)][:, q, :],
                                                      mv[a.buf(2)][:, q, 0:1], rstd[a.buf(2)][:, q:q + 1],
                                                      ALU.subtract, ALU.mult)
                    ins.then_inc(s_xn, 1)

                def take(a):
                    dve.wait_ge(s_L, a.i + 1)
                    nc.vector.tensor_tensor(logits[:, ds(a.i * Q, Q), :], ps_L[a.buf(2)][:],
                                            gb[:, None, :].broadcast_to([P, Q, E]), ALU.add
                                            ).then_inc(s_Lc, 1)

                dve.wait_ge(s_small, 48)
                nc.vector.tensor_copy(b_hi[:], b_raw[:]).then_inc(s_bhi, 1)
                dve.wait_ge(s_bhi, 1)
                nc.vector.tensor_tensor(b_lo[:], b_raw[:], b_hi[:].bitcast(F32), ALU.subtract).then_inc(s_blo, 1)
                measure(At(0, 0, 2))
                norm(At(0, 0, 2))
                measure(At(0, 1, 2))
                norm(At(0, 1, 2))
                measure(At(1, 0, 2))
                take(At(0, 0, 2))
                with dve.Fori(1, NSTEP // 2 - 1) as u:
                    norm(At(u, 0, 2))
                    measure(At(u, 1, 2))
                    take(At(u - 1, 1, 2))
                    norm(At(u, 1, 2))
                    measure(At(u + 1, 0, 2))
                    take(At(u, 0, 2))
                L = NSTEP // 2 - 1
                norm(At(L, 0, 2))
                measure(At(L, 1, 2))
                take(At(L - 1, 1, 2))
                norm(At(L, 1, 2))
                take(At(L, 0, 2))
                take(At(L, 1, 2))

                def wide(ap):
                    return ap[:, :, None].broadcast_to([P, NT, E])

                own = Own(dve, s_dve)
                own.n = NSTEP
                dve.wait_ge(s_Lc, NSTEP)
                own.link(nc.vector.tensor_reduce(red[:], logits[:], AX_X, ALU.max))
                nc.vector.tensor_tensor(work[:], logits[:], wide(red[:]), ALU.subtract).then_inc(s_shift, 1)
                dve.wait_ge(s_exp, 1)
                own.link(nc.vector.tensor_reduce(red[:], score[:], AX_X, ALU.add))
                own.link(nc.vector.reciprocal(red2[:], red[:]))
                own.link(nc.vector.tensor_tensor(score[:], score[:], wide(red2[:]), ALU.mult))
                cur = score
                for k in range(TOPK):
                    own.link(nc.vector.tensor_reduce(gates[:, k, :], cur[:], AX_X, ALU.max))
                    own.link(nc.vector.tensor_tensor(work2[:], cur[:], wide(gates[:, k, :]), ALU.is_equal))
                    own.link(nc.vector.tensor_tensor(work2[:], work2[:], desc[:, None, :].broadcast_to([P, NT, E]),
                                                     ALU.mult))
                    own.link(nc.vector.tensor_reduce(red[:], work2[:], AX_X, ALU.max))
                    own.link(nc.vector.tensor_tensor(hot[k][:], work2[:], wide(red[:]), ALU.is_equal))
                    if k == 0:
                        own.link(nc.vector.scalar_tensor_tensor(out=work[:], in0=hot[0][:], scalar=-2.0,
                                                                in1=score[:], op0=ALU.mult, op1=ALU.add))
                        cur = work
                nc.vector.tensor_tensor(mask[:].rearrange("p e j -> p j e"), hot[0][:], hot[1][:], ALU.add
                                        ).then_inc(s_mask, 1)
                dve.wait_ge(s_cnt, 1)
                total = ps_cnt[:, 1, :].rearrange("p (e j) -> p e j", e=E)
                prefix = ps_cnt[:, 0, :].rearrange("p (e j) -> p e j", e=E)
                own.link(nc.vector.tensor_tensor_scan(out=filled[:].rearrange("p e j -> p (e j)"),
                                                      data0=keep[:].rearrange("p e j -> p (e j)"),
                                                      data1=ps_cnt[:, 1, :], initial=0.0,
                                                      op0=ALU.mult, op1=ALU.add))
                own.link(nc.vector.tensor_tensor(place[:], filled[:], total, ALU.subtract))
                own.link(nc.vector.tensor_tensor(place[:], place[:], prefix, ALU.add))
                own.link(nc.vector.tensor_scalar(ntile_i[:], filled[:, :, NT - 1], float(P - 1), None, ALU.add))
                own.link(nc.vector.tensor_scalar(ntile_i[:], ntile_i[:], 7, None, ALU.arith_shift_right))
                own.link(nc.vector.tensor_copy(ntile[:], ntile_i[:]))
                own.link(nc.vector.tensor_tensor_scan(out=last[:], data0=ones_f[:, 0:E], data1=ntile[:],
                                                      initial=0.0, op0=ALU.mult, op1=ALU.add))
                own.link(nc.vector.tensor_tensor(start[:], last[:], ntile[:], ALU.subtract))
                own.link(nc.vector.scalar_tensor_tensor(out=place[:], in0=start[:, :, None].broadcast_to([P, E, NT]),
                                                        scalar=float(P), in1=place[:], op0=ALU.mult, op1=ALU.add))
                for k in range(TOPK):
                    own.link(nc.vector.tensor_tensor(work2[:], hot[k][:], place[:].rearrange("p e j -> p j e"),
                                                     ALU.mult))
                    own.link(nc.vector.tensor_reduce(slot_f[:, k * NT:(k + 1) * NT], work2[:], AX_X, ALU.add))
                own.link(nc.vector.tensor_scalar(slot_f[:], slot_f[:], 0.0, float(TILES * P - 1), ALU.max, ALU.min))
                own.link(nc.vector.tensor_copy(slots[:].rearrange("p k j -> p (k j)"), slot_f[:]))
                own.mark(nc.vector.tensor_scalar(part_i[:, 0, :], slots[:].rearrange("p k j -> p (k j)"), 7, None,
                                                 ALU.arith_shift_right))
                own.link(nc.vector.tensor_scalar(part_i[:, 1, :], slots[:].rearrange("p k j -> p (k j)"), P - 1, None,
                                                 ALU.bitwise_and))
                own.link(nc.vector.tensor_copy(part[:], part_i[:]))
                for n in range(PAIRS // BATCH):
                    sl = slice(n * BATCH, (n + 1) * BATCH)
                    tj = (n * BATCH) % NT
                    if n >= 2:
                        dve.wait_ge(s_hotmm, n - 1)
                    own.mark(nc.vector.tensor_tensor(hot_in[n % 2][:],
                                                     part[:, 1, sl][:, :, None].broadcast_to([P, BATCH, P]),
                                                     lane[:, None, :].broadcast_to([P, BATCH, P]), ALU.is_equal))
                    if n >= 1:
                        dve.wait_ge(s_hot, n)
                    own.link(nc.vector.tensor_tensor(hot_tile[:],
                                                     part[:, 0, sl][:, :, None].broadcast_to([P, BATCH, TILES]),
                                                     lane[:, None, 0:TILES].broadcast_to([P, BATCH, TILES]),
                                                     ALU.is_equal))
                    nc.vector.tensor_tensor(hot_tok[n % 2][:], hot_tile[:],
                                            token[:, tj:tj + BATCH][:, :, None].broadcast_to([P, BATCH, TILES]),
                                            ALU.mult).then_inc(s_hot, 1)
                own.link(nc.vector.tensor_tensor(tile_no[:, :, 0:E - 1],
                                                 lane[:, 0:TILES][:, :, None].broadcast_to([P, TILES, E - 1]),
                                                 last[:, None, 0:E - 1].broadcast_to([P, TILES, E - 1]),
                                                 ALU.is_ge))
                own.link(nc.vector.tensor_reduce(tok_f[:], tile_no[:, :, 0:E - 1], AX_X, ALU.add))
                own.link(nc.vector.tensor_copy(tile_exp[:], tok_f[:]))
                dve.wait_ge(s_hotmm, PAIRS // BATCH)
                nc.vector.tensor_scalar(tile_tok[:], ps_tok[:], 0.0, float(TOK - 1), ALU.max, ALU.min
                                        ).then_inc(s_tok, 1)


def run_experts(nc, xn_d, y_d, ident, tile_tok, tile_exp, w_hi, w_lo, bias_hl, ones2, loads):
    with ExitStack() as ctx:
        def sb(name, shape, dt):
            return ctx.enter_context(nc.sbuf_tensor(name, shape, dt))

        def bank(name, shape):
            return ctx.enter_context(nc.psum_tensor(name, shape, F32))

        def sem(name):
            return ctx.enter_context(nc.semaphore(name))

        NG = 4
        picked = [sb(f"picked{b}", [P, 1], I32) for b in range(NG)]
        xg = [sb(f"xg{b}", [P, C], F32) for b in range(NG)]
        x_hi = [sb(f"x_hi{b}", [P, KC, P], F32R) for b in range(2)]
        x_lo = [sb(f"x_lo{b}", [P, KC, P], F32R) for b in range(2)]
        act1 = [sb(f"act1{b}", [P, FF], F32) for b in range(2)]
        hid = [sb(f"hid{b}", [P, FF], F32) for b in range(2)]
        h_hi = [sb(f"h_hi{b}", [P, KC, P], F32R) for b in range(2)]
        h_lo = [sb(f"h_lo{b}", [P, KC, P], F32R) for b in range(2)]
        y = [sb(f"y{b}", [P, C], F32) for b in range(2)]
        ps_x = [bank(f"ps_x{b}", [P, KC, P]) for b in range(2)]
        ps_g = [bank(f"ps_g{b}", [P, 2 * FF]) for b in range(2)]
        ps_h = [bank(f"ps_h{b}", [P, KC, P]) for b in range(2)]
        ps_y = [bank(f"ps_y{b}", [P, C]) for b in range(2)]

        c_idx = sem("c_idx")
        c_go = sem("c_go")
        c_gath = [sem(f"c_gath{b}") for b in range(NG)]
        c_tx = sem("c_tx")
        c_xhi = sem("c_xhi")
        c_xlo = sem("c_xlo")
        c_g = sem("c_g")
        c_silu = sem("c_silu")
        c_h = sem("c_h")
        c_th = sem("c_th")
        c_hhi = sem("c_hhi")
        c_hlo = sem("c_hlo")
        c_y = sem("c_y")
        c_yc = sem("c_yc")
        c_yst = [sem(f"c_yst{b}") for b in range(2)]
        c_ld = sem("c_ld")

        with nc.Block() as block:

            @block.sync
            def _(sp):
                for dst, src in loads:
                    sp.dma_start(dst, src).then_inc(c_ld, 16)

                def store(a):
                    sp.wait_ge(c_yc, a.i + 1)
                    sp.dma_start(y_d[ds(a.i * P, P), :], y[a.buf(2)][:]).then_inc(c_yst[a.buf(2)], 16)

                rounds(sp, 4, TILES, store)
                for b in range(2):
                    sp.wait_ge(c_yst[b], TILES // 2 * 16)
                sp.wait_ge(c_ld, 16 * len(loads))

            @block.gpsimd
            def _(pool):
                def gather(a):
                    at_least(pool, c_tx, a.i - NG + 1)
                    nc.gpsimd.tensor_copy(picked[a.buf(NG)][:], tile_tok[:, ds(a.i, 1)]).then_inc(c_idx, 1)
                    pool.wait_ge(c_idx, a.i + 1)
                    pool.sem_inc(c_go, 1)
                    pool.indirect_dma_start(
                        out=xg[a.buf(NG)][:], out_offset=None, in_=xn_d[:, :],
                        in_offset=bass.IndirectOffsetOnAxis(ap=picked[a.buf(NG)][:, 0:1], axis=0)
                    ).then_inc(c_gath[a.buf(NG)], 16)

                rounds(pool, NG, TILES, gather)

            @block.tensor
            def _(pe):
                def turn_x(a):
                    pe.wait_ge(c_gath[a.buf(NG)], (a.uses(NG) + 1) * 16)
                    at_least(pe, c_xlo, a.i - 1)
                    for k in range(KC):
                        mm = nc.tensor.transpose(ps_x[a.buf(2)][:, k, :], xg[a.buf(NG)][:, k * P:(k + 1) * P],
                                                 ident[:])
                    mm.then_inc(c_tx, 1)

                def expert(a):
                    return pe.value_load(tile_exp[0:1, ds(a.i, 1)], min_val=0, max_val=E - 1)

                def three(out, hi, lo, e, cols):
                    for k in range(KC):
                        for n, (x, w) in enumerate([(hi, w_hi), (hi, w_lo), (lo, w_hi)]):
                            nc.tensor.matmul(out, x[:, k, :],
                                             w[:, ds(e, 1), k, cols].rearrange("p o n -> p (o n)"),
                                             start=(k == 0 and n == 0), stop=False)
                    return nc.tensor.matmul(out, ones2[:],
                                            bias_hl[:, ds(e, 1), cols].rearrange("p o n -> p (o n)"),
                                            start=False, stop=True)

                def up(a):
                    e = expert(a)
                    pe.wait_ge(c_xlo, a.i + 1)
                    at_least(pe, c_h, a.i - 1)
                    three(ps_g[a.buf(2)][:], x_hi[a.buf(2)], x_lo[a.buf(2)], e, slice(0, 2 * FF)).then_inc(c_g, 1)

                def turn_h(a):
                    pe.wait_ge(c_h, a.i + 1)
                    at_least(pe, c_hlo, a.i - 1)
                    for k in range(KC):
                        mm = nc.tensor.transpose(ps_h[a.buf(2)][:, k, :], hid[a.buf(2)][:, k * P:(k + 1) * P],
                                                 ident[:])
                    mm.then_inc(c_th, 1)

                def down(a):
                    e = expert(a)
                    pe.wait_ge(c_hlo, a.i + 1)
                    at_least(pe, c_yc, a.i - 1)
                    three(ps_y[a.buf(2)][:], h_hi[a.buf(2)], h_lo[a.buf(2)], e, slice(2 * FF, WALL)).then_inc(c_y, 1)

                def tile(a, first=False, left=2):
                    if left > 0:
                        up(a.plus(1))
                    turn_h(a)
                    if left > 1:
                        turn_x(a.plus(2))
                    if not first:
                        down(a.plus(-1))

                turn_x(At(0, 0, 4))
                turn_x(At(0, 1, 4))
                up(At(0, 0, 4))
                for r in range(4):
                    tile(At(0, r, 4), first=(r == 0))
                with pe.Fori(1, TILES // 4 - 1) as u:
                    for r in range(4):
                        tile(At(u, r, 4))
                for r in range(4):
                    tile(At(TILES // 4 - 1, r, 4), left=3 - r)
                down(At(TILES // 4 - 1, 3, 4))

            @block.scalar
            def _(act):
                def cut_x(a):
                    act.wait_ge(c_tx, a.i + 1)
                    at_least(act, c_g, a.i - 1)
                    nc.scalar.activation(x_hi[a.buf(2)][:], ps_x[a.buf(2)][:], ACT.Copy).then_inc(c_xhi, 1)

                def silu(a):
                    act.wait_ge(c_g, a.i + 1)
                    at_least(act, c_h, a.i - 1)
                    nc.scalar.activation(act1[a.buf(2)][:], ps_g[a.buf(2)][:, 0:FF], ACT.Silu).then_inc(c_silu, 1)

                def cut_h(a):
                    act.wait_ge(c_th, a.i + 1)
                    at_least(act, c_y, a.i - 1)
                    nc.scalar.activation(h_hi[a.buf(2)][:], ps_h[a.buf(2)][:], ACT.Copy).then_inc(c_hhi, 1)

                def result(a):
                    act.wait_ge(c_y, a.i + 1)
                    at_least(act, c_yst[a.buf(2)], a.uses(2) * 16)
                    nc.scalar.activation(y[a.buf(2)][:], ps_y[a.buf(2)][:], ACT.Copy).then_inc(c_yc, 1)

                def tile(a, first=False, left=2):
                    if left > 0:
                        silu(a.plus(1))
                    cut_h(a)
                    if left > 1:
                        cut_x(a.plus(2))
                    if not first:
                        result(a.plus(-1))

                cut_x(At(0, 0, 4))
                cut_x(At(0, 1, 4))
                silu(At(0, 0, 4))
                for r in range(4):
                    tile(At(0, r, 4), first=(r == 0))
                with act.Fori(1, TILES // 4 - 1) as u:
                    for r in range(4):
                        tile(At(u, r, 4))
                for r in range(4):
                    tile(At(TILES // 4 - 1, r, 4), left=3 - r)
                result(At(TILES // 4 - 1, 3, 4))

            @block.vector
            def _(dve):
                def cut_x(a):
                    dve.wait_ge(c_xhi, a.i + 1)
                    at_least(dve, c_g, a.i - 1)
                    nc.vector.tensor_tensor(x_lo[a.buf(2)][:], ps_x[a.buf(2)][:], x_hi[a.buf(2)][:].bitcast(F32),
                                            ALU.subtract).then_inc(c_xlo, 1)

                def hidden(a):
                    dve.wait_ge(c_silu, a.i + 1)
                    at_least(dve, c_th, a.i - 1)
                    nc.vector.tensor_tensor(hid[a.buf(2)][:], ps_g[a.buf(2)][:, FF:2 * FF], act1[a.buf(2)][:],
                                            ALU.mult).then_inc(c_h, 1)

                def cut_h(a):
                    dve.wait_ge(c_hhi, a.i + 1)
                    at_least(dve, c_y, a.i - 1)
                    nc.vector.tensor_tensor(h_lo[a.buf(2)][:], ps_h[a.buf(2)][:], h_hi[a.buf(2)][:].bitcast(F32),
                                            ALU.subtract).then_inc(c_hlo, 1)

                def tile(a, left=2):
                    if left > 0:
                        hidden(a.plus(1))
                    cut_h(a)
                    if left > 1:
                        cut_x(a.plus(2))

                cut_x(At(0, 0, 4))
                cut_x(At(0, 1, 4))
                hidden(At(0, 0, 4))
                for r in range(4):
                    tile(At(0, r, 4))
                with dve.Fori(1, TILES // 4 - 1) as u:
                    for r in range(4):
                        tile(At(u, r, 4))
                for r in range(4):
                    tile(At(TILES // 4 - 1, r, 4), left=3 - r)


def mix(nc, x, xT_d, y_d, out, slots, gates, raw_vr, raw_o, raw_s13, raw_s2, vec_tf, vec_td,
        vec_b1, vec_b3, row_b2):
    with ExitStack() as ctx:
        def sb(name, shape, dt):
            return ctx.enter_context(nc.sbuf_tensor(name, shape, dt))

        def bank(name, shape):
            return ctx.enter_context(nc.psum_tensor(name, shape, F32))

        def sem(name):
            return ctx.enter_context(nc.semaphore(name))

        vr_hi, vr_lo = (sb(f"vr_{s}", [P, KC, 2 * C], F32R) for s in ("hi", "lo"))
        o_hi, o_lo = (sb(f"o_{s}", [P, KC, C], F32R) for s in ("hi", "lo"))
        s13_hi, s13_lo = (sb(f"s13_{s}", [P, KC, 2 * SF], F32R) for s in ("hi", "lo"))
        s2_hi, s2_lo = (sb(f"s2_{s}", [P, KS, C], F32R) for s in ("hi", "lo"))
        splits = [(raw_vr, vr_hi, vr_lo), (raw_s13, s13_hi, s13_lo), (raw_o, o_hi, o_lo), (raw_s2, s2_hi, s2_lo)]
        xT = [sb(f"col{b}", [P, KC, STEP], F32) for b in range(2)]
        x_hi = [sb(f"col_hi{b}", [P, KC, STEP], F32R) for b in range(2)]
        x_lo = [sb(f"col_lo{b}", [P, KC, STEP], F32R) for b in range(2)]
        res = [sb(f"res{b}", [P, Q, C], F32) for b in range(2)]
        yg = [sb(f"yg{b}", [P, TOPK, Q, C], F32) for b in range(2)]
        picked = [sb(f"rows{b}", [P, TOPK, Q], I32) for b in range(2)]
        NA, NB = KC * B, KC
        state = sb("state", [P, NA + 2 * NB, TIMES + 1], F32)
        sa = state[:, 0:NA, :]
        s_b = state[:, NA:NA + NB, :]
        s_p = state[:, NA + NB:NA + 2 * NB, :]
        grow = sb("grow", [P, KC], F32)
        zero = sb("zero", [P, 1], F32)
        low = sb("low", [P, 2, KC, TIMES], F32)
        high = sb("high", [P, 2, KC, TIMES], F32)
        decays = sb("decays", [P, 2, 2, KC, TIMES], F32)
        den = sb("den", [P, KC, TIMES], F32)
        rden = sb("rden", [P, KC, TIMES], F32)
        coef = sb("coef", [P, 2, KC, TIMES], F32)
        fed = sb("fed", [P, KC, B, TIMES], F32)
        part_a = sb("part_a", [P, KC, B, TIMES], F32)
        part_v = sb("part_v", [P, KC, B, TIMES], F32)
        th = sb("th", [P, KC, B, TIMES], F32)
        rw = sb("rw", [P, KC, B, TIMES], F32)
        a_hi = sb("a_hi", [P, KC, STEP], F32R)
        a_lo = sb("a_lo", [P, KC, STEP], F32R)
        act1 = [sb(f"sact{b}", [P, STEP], F32) for b in range(2)]
        hid = [sb(f"shid{b}", [P, STEP], F32) for b in range(2)]
        s_hi = sb("s_hi", [P, KS, STEP], F32R)
        s_lo = sb("s_lo", [P, KS, STEP], F32R)
        ps_v = bank("ps_v", [P, KC, STEP])
        ps_r = bank("ps_r", [P, KC, STEP])
        ps_w = [bank(f"ps_w{b}", [P, STEP]) for b in range(4)]

        b_xT = [sem(f"b_xT{b}") for b in range(2)]
        b_res = [sem(f"b_res{b}") for b in range(2)]
        b_ost = [sem(f"b_ost{b}") for b in range(2)]
        b_gath = [sem(f"b_gath{b}") for b in range(2)]
        b_idx = sem("b_idx")
        b_go = sem("b_go")
        b_whi = sem("b_whi")
        b_wlo = sem("b_wlo")
        b_xhi = sem("b_xhi")
        b_xlo = sem("b_xlo")
        b_xb = sem("b_xb")
        b_v = sem("b_v")
        b_r = sem("b_r")
        b_tanh = sem("b_tanh")
        b_used = sem("b_used")
        b_vread = sem("b_vread")
        b_rw = sem("b_rw")
        b_ahi = sem("b_ahi")
        b_alo = sem("b_alo")
        b_t1 = sem("b_t1")
        b_exp = sem("b_exp")
        b_z = sem("b_z")
        b_silu = sem("b_silu")
        b_h = sem("b_h")
        b_shi = sem("b_shi")
        b_slo = sem("b_slo")
        b_o = sem("b_o")
        b_fin = sem("b_fin")
        b_a = sem("b_a")
        b_t = sem("b_t")
        b_f = sem("b_f")

        xv = x.rearrange("b (i h p) c -> i p b h c", h=HALF, p=P)
        ov = out.rearrange("b (i h p) c -> i p b h c", h=HALF, p=P)
        LAST = At(NSTEP // 2 - 1, 1, 2)

        def steps(eng, body):
            body(At(0, 0, 2), True, 2)
            body(At(0, 1, 2), False, 2)
            with eng.Fori(1, NSTEP // 2 - 1) as u:
                body(At(u, 0, 2), False, 2)
                body(At(u, 1, 2), False, 2)
            body(At(NSTEP // 2 - 1, 0, 2), False, 1)
            body(At(NSTEP // 2 - 1, 1, 2), False, 0)

        with nc.Block() as block:

            @block.sync
            def _(sp):
                def load_cols(a):
                    at_least(sp, b_xhi, a.i - 1)
                    at_least(sp, b_xlo, a.i - 1)
                    sp.dma_start(xT[a.buf(2)][:].rearrange("p k n -> p (k n)"),
                                 xT_d[:, ds(a.i, 1), :].rearrange("p o n -> p (o n)")).then_inc(b_xT[a.buf(2)], 16)

                def load_rows(a):
                    at_least(sp, b_ost[a.buf(2)], a.uses(2) * 32)
                    for b in range(B):
                        sp.dma_start(res[a.buf(2)][:, b * HALF:(b + 1) * HALF, :],
                                     xv[ds(a.i, 1), :, b, :, :].rearrange("o p h c -> p (o h) c")
                                     ).then_inc(b_res[a.buf(2)], 16)

                load_cols(At(0, 0, 2))
                load_cols(At(0, 1, 2))
                load_rows(At(0, 0, 2))
                load_rows(At(0, 1, 2))

                def step(a, first, left):
                    if left > 1:
                        load_cols(a.plus(2))
                    sp.wait_ge(b_fin, a.i * Q + Q)
                    for b in range(B):
                        sp.dma_start(ov[ds(a.i, 1), :, b, :, :].rearrange("o p h c -> p (o h) c"),
                                     res[a.buf(2)][:, b * HALF:(b + 1) * HALF, :]).then_inc(b_ost[a.buf(2)], 16)
                    if left > 1:
                        load_rows(a.plus(2))

                steps(sp, step)
                for b in range(2):
                    sp.wait_ge(b_ost[b], NSTEP // 2 * 32)

            @block.gpsimd
            def _(pool):
                def gather(a):
                    at_least(pool, b_fin, a.i * Q - Q)
                    nc.gpsimd.tensor_copy(picked[a.buf(2)][:], slots[:, :, ds(a.i * Q, Q)]).then_inc(b_idx, 1)
                    pool.wait_ge(b_idx, a.i + 1)
                    pool.sem_inc(b_go, 1)
                    for k in range(TOPK):
                        for q in range(Q):
                            pool.indirect_dma_start(
                                out=yg[a.buf(2)][:, k, q, :], out_offset=None, in_=y_d[:, :],
                                in_offset=bass.IndirectOffsetOnAxis(ap=picked[a.buf(2)][:, k, q:q + 1], axis=0)
                            ).then_inc(b_gath[a.buf(2)], 16)

                def cut(a):
                    pool.wait_ge(b_xhi, a.i + 1)
                    at_least(pool, b_z, a.i * KS - KS)
                    nc.gpsimd.tensor_tensor(x_lo[a.buf(2)][:], xT[a.buf(2)][:], x_hi[a.buf(2)][:].bitcast(F32),
                                            ALU.subtract).then_inc(b_xlo, 1)

                def bias(a):
                    pool.wait_ge(b_res[a.buf(2)], (a.uses(2) + 1) * 32)
                    nc.gpsimd.tensor_tensor(res[a.buf(2)][:], res[a.buf(2)][:],
                                            row_b2[:, None, :].broadcast_to([P, Q, C]), ALU.add).then_inc(b_xb, 1)

                def step(a, first, left):
                    gather(a)
                    if left > 0:
                        cut(a.plus(1))
                    bias(a)

                cut(At(0, 0, 2))
                steps(pool, step)

            @block.tensor
            def _(pe):
                def three(out, w_hi, w_lo, x_hi, x_lo, start, stop):
                    nc.tensor.matmul(out, w_hi, x_hi, start=start, stop=False)
                    nc.tensor.matmul(out, w_hi, x_lo, start=False, stop=False)
                    return nc.tensor.matmul(out, w_lo, x_hi, start=False, stop=stop)

                def columns(out, hi, lo, n0, xh, xl):
                    for k in range(KC):
                        mm = three(out, hi[:, k, n0:n0 + P], lo[:, k, n0:n0 + P], xh[:, k, :], xl[:, k, :],
                                   k == 0, k == KC - 1)
                    return mm

                def values(a):
                    pe.wait_ge(b_xlo, a.i + 1)
                    at_least(pe, b_vread, a.i)
                    for m in range(KC):
                        mm = columns(ps_v[:, m, :], vr_hi, vr_lo, m * P, x_hi[a.buf(2)], x_lo[a.buf(2)])
                    mm.then_inc(b_v, 1)
                    at_least(pe, b_tanh, a.i)
                    for m in range(KC):
                        mm = columns(ps_r[:, m, :], vr_hi, vr_lo, C + m * P, x_hi[a.buf(2)], x_lo[a.buf(2)])
                    mm.then_inc(b_r, 1)

                def shared(a):
                    for m in range(KS):
                        if m < 2:
                            at_least(pe, b_fin, a.i * Q - Q + 2 * m + 2)
                        else:
                            pe.wait_ge(b_h, a.i * KS + m - 1)
                        columns(ps_w[m % 2 * 2][:], s13_hi, s13_lo, m * P, x_hi[a.buf(2)], x_lo[a.buf(2)])
                        columns(ps_w[m % 2 * 2 + 1][:], s13_hi, s13_lo, SF + m * P, x_hi[a.buf(2)],
                                x_lo[a.buf(2)]).then_inc(b_z, 1)

                def outputs(a):
                    pe.wait_ge(b_alo, a.i + 1)
                    pe.wait_ge(b_slo, a.i * KS + KS)
                    for q in range(Q):
                        cols = slice(q * P, (q + 1) * P)
                        bank_q = ps_w[q][:, 0:C]
                        for k in range(KC):
                            three_rows(bank_q, a_hi, a_lo, k, cols, o_hi, o_lo, k == 0, False)
                        for k in range(KS):
                            mm = three_rows(bank_q, s_hi, s_lo, k, cols, s2_hi, s2_lo, False, k == KS - 1)
                        mm.then_inc(b_o, 1)

                def three_rows(out, hi, lo, k, cols, w_hi, w_lo, start, stop):
                    nc.tensor.matmul(out, hi[:, k, cols], w_hi[:, k, :], start=start, stop=False)
                    nc.tensor.matmul(out, hi[:, k, cols], w_lo[:, k, :], start=False, stop=False)
                    return nc.tensor.matmul(out, lo[:, k, cols], w_hi[:, k, :], start=False, stop=stop)

                def step(a, first, left):
                    values(a)
                    if first:
                        pe.wait_ge(b_whi, 4)
                        pe.wait_ge(b_wlo, 4)
                    else:
                        outputs(a.plus(-1))
                    shared(a)

                pe.wait_ge(b_whi, 1)
                pe.wait_ge(b_wlo, 1)
                steps(pe, step)
                outputs(LAST)

            @block.scalar
            def _(act):
                def cut_x(a):
                    act.wait_ge(b_xT[a.buf(2)], (a.uses(2) + 1) * 16)
                    at_least(act, b_z, a.i * KS - KS)
                    nc.scalar.activation(x_hi[a.buf(2)][:], xT[a.buf(2)][:], ACT.Copy).then_inc(b_xhi, 1)

                def exps(a):
                    act.wait_ge(b_t1, a.i + 1)
                    at_least(act, b_used, a.i)
                    nc.scalar.activation(decays[:, 0], high[:], ACT.Exp, scale=-1.0)
                    nc.scalar.activation(decays[:, 1], low[:], ACT.Exp).then_inc(b_exp, 1)

                def receive(a):
                    act.wait_ge(b_r, a.i + 1)
                    at_least(act, b_rw, a.i)
                    nc.scalar.activation(th[:].rearrange("p k b t -> p k (b t)"), ps_r[:], ACT.Tanh, scale=0.5
                                         ).then_inc(b_tanh, 1)

                def cut_a(a):
                    act.wait_ge(b_rw, a.i + 1)
                    at_least(act, b_o, a.i * Q)
                    nc.scalar.activation(a_hi[:], rw[:].rearrange("p k b t -> p k (b t)"), ACT.Copy
                                         ).then_inc(b_ahi, 1)

                def silu(a, m):
                    act.wait_ge(b_z, a.i * KS + m + 1)
                    at_least(act, b_h, a.i * KS + m - 1)
                    nc.scalar.activation(act1[m % 2][:], ps_w[m % 2 * 2][:], ACT.Silu, bias=vec_b1[:, m:m + 1]
                                         ).then_inc(b_silu, 1)

                def cut_s(a, m):
                    act.wait_ge(b_h, a.i * KS + m + 1)
                    at_least(act, b_o, a.i * Q)
                    nc.scalar.activation(s_hi[:, m, :], hid[m % 2][:], ACT.Copy).then_inc(b_shi, 1)

                def step(a, first, left):
                    receive(a)
                    if left > 0:
                        cut_x(a.plus(1))
                    cut_a(a)
                    if left > 0:
                        exps(a.plus(1))
                    silu(a, 0)
                    silu(a, 1)
                    for m in range(KS):
                        cut_s(a, m)
                        if m + 2 < KS:
                            silu(a, m + 2)

                cut_x(At(0, 0, 2))
                for raw, hi, lo in splits:
                    nc.scalar.activation(hi[:], raw[:], ACT.Copy).then_inc(b_whi, 1)
                exps(At(0, 0, 2))
                steps(act, step)

            @block.vector
            def _(dve):
                def differences(a, first=False):
                    own = OwnIn(dve, b_t, a, 9)
                    if first:
                        own.n += 1
                    else:
                        own.link(nc.vector.tensor_copy(state[:, :, 0:1], state[:, :, TIMES:TIMES + 1]))
                    for c in range(KC):
                        ins = nc.vector.tensor_tensor_scan(out=s_p[:, c, 1:TIMES + 1],
                                                           data0=grow[:, c:c + 1].broadcast_to([P, TIMES]),
                                                           data1=zero[:].broadcast_to([P, TIMES]),
                                                           initial=s_p[:, c, 0:1], op0=ALU.add, op1=ALU.add)
                    own.link(ins)
                    for n, v in enumerate((vec_tf, vec_td)):
                        for c in range(KC):
                            ins = nc.vector.scalar_tensor_tensor(out=low[:, n, c, :], in0=s_p[:, c, 0:TIMES],
                                                                 scalar=v[:, c:c + 1], in1=s_p[:, c, 0:TIMES],
                                                                 op0=ALU.add, op1=ALU.subtract)
                    own.link(ins)
                    own.link(nc.vector.tensor_scalar(high[:], low[:], 0.0, None, ALU.max))
                    nc.vector.tensor_scalar(low[:], low[:], 0.0, None, ALU.min).then_inc(b_t1, 1)
                    return own

                def factors(a, own):
                    dve.wait_ge(b_exp, a.i + 1)
                    for c in range(KC):
                        ins = nc.vector.tensor_tensor_scan(out=s_b[:, c, 1:TIMES + 1], data0=decays[:, 0, 1, c, :],
                                                           data1=decays[:, 1, 1, c, :], initial=s_b[:, c, 0:1],
                                                           op0=ALU.mult, op1=ALU.add)
                    own.link(ins)
                    own.link(nc.vector.tensor_tensor(den[:], decays[:, 0, 0], s_b[:, :, 0:TIMES], ALU.mult))
                    own.link(nc.vector.tensor_tensor(den[:], den[:], decays[:, 1, 0], ALU.add))
                    own.link(nc.vector.tensor_scalar(den[:], den[:], 1e-6, 2.0, ALU.add, ALU.mult))
                    own.link(nc.vector.reciprocal(rden[:], den[:]))
                    own.close()
                    for n in range(2):
                        ins = nc.vector.tensor_tensor(coef[:, n], decays[:, n, 0], rden[:], ALU.mult)
                    ins.then_inc(b_f, 1)

                def wide(ap):
                    return ap[:, :, None, :].broadcast_to([P, KC, B, TIMES])

                def time_mix(a):
                    own = OwnIn(dve, b_a, a, 3)
                    v = ps_v[:].rearrange("p k (b t) -> p k b t", b=B)
                    dve.wait_ge(b_v, a.i + 1)
                    dve.wait_ge(b_f, a.i + 1)
                    own.mark(nc.vector.tensor_tensor(fed[:], v, wide(decays[:, 1, 1]), ALU.mult))
                    nc.vector.tensor_tensor(part_v[:], v, wide(coef[:, 1]), ALU.mult).then_inc(b_vread, 1)
                    own.wait()
                    for c in range(KC):
                        for b in range(B):
                            ins = nc.vector.tensor_tensor_scan(
                                out=sa[:, c * B + b, 1:TIMES + 1], data0=decays[:, 0, 1, c, :], data1=fed[:, c, b, :],
                                initial=sa[:, c * B + b, 0:1], op0=ALU.mult, op1=ALU.add)
                    ins.then_inc(b_used, 1)
                    dve.wait_ge(b_used, a.i + 1)
                    own.link(nc.vector.tensor_tensor(
                        part_a[:], sa[:, :, 0:TIMES].rearrange("p (k b) t -> p k b t", k=KC), wide(coef[:, 0]),
                        ALU.mult))
                    own.link(nc.vector.tensor_tensor(part_a[:], part_a[:], part_v[:], ALU.add))
                    own.close()
                    dve.wait_ge(b_tanh, a.i + 1)
                    at_least(dve, b_ahi, a.i)
                    nc.vector.scalar_tensor_tensor(
                        out=rw[:].rearrange("p k b t -> p (k b t)"), in0=th[:].rearrange("p k b t -> p (k b t)"),
                        scalar=1.0, in1=part_a[:].rearrange("p k b t -> p (k b t)"), op0=ALU.add, op1=ALU.mult
                    ).then_inc(b_rw, 1)

                def sum_up(a):
                    buf = a.buf(2)
                    dve.wait_ge(b_xb, a.i + 1)
                    dve.wait_ge(b_gath[buf], (a.uses(2) + 1) * 16 * TOPK * Q)
                    own = OwnIn(dve, b_slot, a, TOPK)
                    for k in range(TOPK):
                        for q in range(Q):
                            ins = nc.vector.scalar_tensor_tensor(
                                out=res[buf][:, q, :], in0=yg[buf][:, k, q, :],
                                scalar=gates[:, k, ds(a.i * Q + q, 1)], in1=res[buf][:, q, :],
                                op0=ALU.mult, op1=ALU.add)
                        own.link(ins)
                    own.close()
                    for q in range(Q):
                        dve.wait_ge(b_o, a.i * Q + q + 1)
                        nc.vector.tensor_tensor(res[buf][:, q, :], ps_w[q][:, 0:C], res[buf][:, q, :], ALU.add
                                                ).then_inc(b_fin, 1)

                def cut_a(a):
                    dve.wait_ge(b_ahi, a.i + 1)
                    nc.vector.tensor_tensor(a_lo[:], rw[:].rearrange("p k b t -> p k (b t)"), a_hi[:].bitcast(F32),
                                            ALU.subtract).then_inc(b_alo, 1)

                def hidden(a, m):
                    dve.wait_ge(b_silu, a.i * KS + m + 1)
                    at_least(dve, b_shi, a.i * KS + m - 1)
                    at_least(dve, b_slo, a.i * KS + m - 1)
                    nc.vector.scalar_tensor_tensor(out=hid[m % 2][:], in0=ps_w[m % 2 * 2 + 1][:],
                                                   scalar=vec_b3[:, m:m + 1], in1=act1[m % 2][:],
                                                   op0=ALU.add, op1=ALU.mult).then_inc(b_h, 1)

                def cut_s(a, m):
                    dve.wait_ge(b_shi, a.i * KS + m + 1)
                    nc.vector.tensor_tensor(s_lo[:, m, :], hid[m % 2][:], s_hi[:, m, :].bitcast(F32), ALU.subtract
                                            ).then_inc(b_slo, 1)

                def step(a, first, left):
                    time_mix(a)
                    if not first:
                        sum_up(a.plus(-1))
                    cut_a(a)
                    if left > 0:
                        own = differences(a.plus(1))
                    hidden(a, 0)
                    hidden(a, 1)
                    for m in range(KS):
                        cut_s(a, m)
                        if m + 2 < KS:
                            hidden(a, m + 2)
                    if left > 0:
                        factors(a.plus(1), own)

                b_slot = sem("b_slot")
                nc.vector.memset(zero[:], 0.0)
                nc.vector.memset(state[:, 0:NA + NB, 0:1], 0.0)
                nc.vector.memset(s_p[:, :, 0:1], -10000.0)
                nc.vector.tensor_scalar(grow[:], vec_td[:], 0.0, None, ALU.max).then_inc(b_t, 1)
                dve.wait_ge(b_t, 1)
                first_own = differences(At(0, 0, 2), True)
                for n, (raw, hi, lo) in enumerate(splits):
                    dve.wait_ge(b_whi, n + 1)
                    nc.vector.tensor_tensor(lo[:], raw[:], hi[:].bitcast(F32), ALU.subtract).then_inc(b_wlo, 1)
                factors(At(0, 0, 2), first_own)
                steps(dve, step)
                sum_up(LAST)


_OUT = (B, T, C)


def kernel(**inputs):
    import numpy as np
    import concourse.bacc as bacc
    from concourse.bass_utils import run_bass_kernel_spmd as run

    def get(name):
        return np.asarray(inputs[name])

    def cols(name):
        return np.swapaxes(get(name), -1, -2)

    def by_partition(a):
        a = a.reshape(-1, P, *a.shape[1:])
        return np.swapaxes(a, 0, 1)

    arrays = {
        "x": get("L0_attn_x"),
        "decay": by_partition(get("L0_attn_time_decay")),
        "first": by_partition(get("L0_attn_time_first")),
        "wvr": np.concatenate([cols("L0_attn_value_w"), cols("L0_attn_recep_w")], axis=1),
        "wo": cols("L0_attn_out_w"),
        "gate_w": by_partition(cols("L0_ffn_gate_w")),
        "gate_b": get("L0_ffn_gate_b"),
        "w_all": np.concatenate([cols("L0_ffn_w1"), cols("L0_ffn_w3"), cols("L0_ffn_w2")], axis=2),
        "b_all": np.concatenate([get("L0_ffn_b1"), get("L0_ffn_b3"), get("L0_ffn_b2")], axis=1).reshape(-1),
        "ws13": np.concatenate([cols("L0_ffn_ws1"), cols("L0_ffn_ws3")], axis=1),
        "bs1": by_partition(get("L0_ffn_bs1")),
        "bs3": by_partition(get("L0_ffn_bs3")),
        "ws2": cols("L0_ffn_ws2"),
        "bs2": get("L0_ffn_bs2"),
    }
    arrays = {k: np.ascontiguousarray(v) for k, v in arrays.items()}
    nc = bacc.Bacc("TRN2", target_bir_lowering=False, num_devices=1)
    args = [nc.dram_tensor(k, v.shape, mybir.dt.from_np(v.dtype), kind="ExternalInput").ap()
            for k, v in arrays.items()]
    out = nc.dram_tensor("out", _OUT, F32, kind="ExternalOutput").ap()
    build(nc, *args, out)
    r = run(nc, [arrays], core_ids=[0])
    return r.results[0]["out"]
```

```python
from contextlib import ExitStack

import concourse.bass as bass
from concourse import mybir

F32 = mybir.dt.float32
F32R = mybir.dt.float32r
BF16 = mybir.dt.bfloat16
I32 = mybir.dt.int32
ALU = mybir.AluOpType
ACT = mybir.ActivationFunctionType
AX_X = mybir.AxisListType.X
ds = bass.ds

P = 128
B, T, C = 2, 2048, 256
TOK = B * T
E, TOPK = 8, 2
FF, SF = 256, 512
KC = C // P
KS = SF // P
TIMES = 256
STEP = B * TIMES
NSTEP = T // TIMES
Q = STEP // P
NT = TOK // P
HALF = TIMES // P
WALL = 2 * FF + C
TILES = -(-(TOK * TOPK // P + E - 1) // 4) * 4
EPS = 1e-5
PIECE = 128
NPIECE = T // PIECE
PAIRS = TOPK * NT
BATCH = 8


class At:

    def __init__(self, u, r, n):
        self.u, self.r, self.n = u, r, n

    def plus(self, d):
        q, r = divmod(self.r + d, self.n)
        return At(self.u + q if q else self.u, r, self.n)

    @property
    def i(self):
        return self.u * self.n + self.r

    def uses(self, bufs):
        assert self.n % bufs == 0
        return self.u * (self.n // bufs) + self.r // bufs

    def buf(self, bufs):
        return self.r % bufs


def at_least(eng, sem, value):
    if isinstance(value, int) and value <= 0:
        return
    eng.wait_ge(sem, value)


def rounds(eng, n, count, body):
    for r in range(n):
        body(At(0, r, n))
    with eng.Fori(1, count // n - 1) as u:
        for r in range(n):
            body(At(u, r, n))
    for r in range(n):
        body(At(count // n - 1, r, n))


class Own:

    def __init__(self, eng, sem):
        self.eng, self.sem, self.n = eng, sem, 0

    def mark(self, ins):
        ins.then_inc(self.sem, 1)
        self.n += 1

    def wait(self):
        self.eng.wait_ge(self.sem, self.n)

    def link(self, ins):
        self.mark(ins)
        self.wait()


class OwnIn:

    def __init__(self, eng, sem, at, per, done=0):
        self.eng, self.sem, self.base, self.per, self.n = eng, sem, at.i * per + done, per, 0

    def mark(self, ins):
        ins.then_inc(self.sem, 1)
        self.n += 1

    def wait(self):
        self.eng.wait_ge(self.sem, self.base + self.n)

    def link(self, ins):
        self.mark(ins)
        self.wait()

    def close(self):
        assert self.n == self.per, (self.n, self.per)


def build(nc, x, decay, first, wvr, wo, gate_w, gate_b, w_all, b_all, ws13, bs1, bs3, ws2, bs2, out):
    xn_d = nc.dram_tensor("xn_rows", (TOK, C), F32, kind="Internal").ap()
    xT_d = nc.dram_tensor("xn_columns", (P, NSTEP, KC * STEP), F32, kind="Internal").ap()
    tab_d = nc.dram_tensor("mix_tables", (T // PIECE, P, 4, KC, PIECE), F32, kind="Internal").ap()
    y_d = nc.dram_tensor("expert_rows", (TILES * P, C), F32, kind="Internal").ap()

    with ExitStack() as kept:
        def sb(name, shape, dt, stack=kept):
            return stack.enter_context(nc.sbuf_tensor(name, shape, dt))

        ident = sb("ident", [P, P], F32)
        slots = sb("slots", [P, TOPK, NT], I32)
        gates = sb("gates", [P, TOPK, NT], F32)
        tile_tok = sb("tile_tok", [P, TILES], I32)
        tile_exp = sb("tile_exp", [P, TILES], I32)
        raw_vr = sb("raw_vr", [P, KC, 2 * C], F32)
        raw_o = sb("raw_o", [P, KC, C], F32)
        raw_s13 = sb("raw_s13", [P, KC, 2 * SF], F32)
        raw_s2 = sb("raw_s2", [P, KS, C], F32)
        vec_tf = sb("vec_tf", [P, KC], F32)
        vec_td = sb("vec_td", [P, KC], F32)
        vec_b1 = sb("vec_b1", [P, KS], F32)
        vec_b3 = sb("vec_b3", [P, KS], F32)
        row_b2 = sb("row_b2", [P, C], F32)

        with ExitStack() as experts:
            w_hi = sb("w_hi", [P, E, KC, WALL], F32R, experts)
            w_lo = sb("w_lo", [P, E, KC, WALL], F32R, experts)
            bias_hl = sb("bias_hl", [2, E, WALL], F32R, experts)
            ones2 = sb("ones2", [2, P], F32R, experts)
            route(nc, x, first, decay, vec_tf, vec_td, gate_w, gate_b, w_all, b_all, xn_d, xT_d, ident, slots, gates, tile_tok,
                  tile_exp, w_hi, w_lo, bias_hl, ones2, raw_s13)
            run_experts(nc, xn_d, y_d, tab_d, vec_tf, vec_td, ident, tile_tok, tile_exp, w_hi, w_lo, bias_hl, ones2,
                        [(raw_vr[:], wvr.rearrange("(k p) n -> p k n", p=P)),
                         (raw_o[:], wo.rearrange("(k p) n -> p k n", p=P)),
                         (raw_s13[:], ws13.rearrange("(k p) n -> p k n", p=P)),
                         (raw_s2[:], ws2.rearrange("(k p) n -> p k n", p=P)),
                         (vec_b1[:], bs1),
                         (vec_b3[:], bs3),
                         (row_b2[:], bs2.rearrange("(a n) -> a n", a=1).broadcast_to([P, C]))])
        mix(nc, x, xT_d, y_d, tab_d, out, slots, gates, raw_vr, raw_o, raw_s13, raw_s2,
            vec_b1, vec_b3, row_b2)


def route(nc, x, first, decay, vec_tf, vec_td, gate_w, gate_b, w_all, b_all, xn_d, xT_d, ident, slots, gates, tile_tok,
          tile_exp, w_hi, w_lo, bias_hl, ones2, spare):
    with ExitStack() as ctx:
        def sb(name, shape, dt):
            return ctx.enter_context(nc.sbuf_tensor(name, shape, dt))

        def bank(name, shape):
            return ctx.enter_context(nc.psum_tensor(name, shape, F32))

        def sem(name):
            return ctx.enter_context(nc.semaphore(name))

        xin = [spare[:, b, :].rearrange("p (q c) -> p q c", q=Q) for b in range(2)]
        xn = [sb(f"xn{b}", [P, Q, C], F32) for b in range(2)]
        xT = [sb(f"xT{b}", [P, KC, STEP], F32) for b in range(2)]
        w_raw = [sb(f"w_raw{b}", [P, KC, WALL], F32) for b in range(2)]
        stats = [sb(f"stats{b}", [P, Q, 6], F32) for b in range(2)]
        mv = [sb(f"mv{b}", [P, Q, 2], F32) for b in range(2)]
        var = [sb(f"var{b}", [P, Q], F32) for b in range(2)]
        std = [sb(f"std{b}", [P, Q], F32) for b in range(2)]
        rstd = [sb(f"rstd{b}", [P, Q], F32) for b in range(2)]
        gw = sb("gw", [P, KC, E], F32)
        gb = sb("gb", [P, E], F32)
        BR = E * WALL // P
        b_raw = sb("b_raw", [P, BR], F32)
        b_hi = sb("b_hi", [P, BR], F32R)
        b_lo = sb("b_lo", [P, BR], F32R)
        ones_f = sb("ones_f", [P, P], F32)
        before_f = sb("before_f", [P, P], F32)
        ones = sb("ones", [P, P], BF16)
        before = sb("before", [P, P], BF16)
        lane_i = sb("lane_i", [P, P], I32)
        lane = sb("lane", [P, P], F32)
        token_i = sb("token_i", [P, NT], I32)
        token = sb("token", [P, NT], F32)
        desc_i = sb("desc_i", [P, E], I32)
        desc = sb("desc", [P, E], F32)
        logits = sb("logits", [P, NT, E], F32)
        score = sb("score", [P, NT, E], F32)
        work = sb("work", [P, NT, E], F32)
        work2 = sb("work2", [P, NT, E], F32)
        hot = [sb(f"hot{k}", [P, NT, E], F32) for k in range(TOPK)]
        red = sb("red", [P, NT], F32)
        red2 = sb("red2", [P, NT], F32)
        mask = sb("mask", [P, E, NT], BF16)
        keep = sb("keep", [P, E, NT], F32)
        filled = sb("filled", [P, E, NT], F32)
        place = sb("place", [P, E, NT], F32)
        ntile_i = sb("ntile_i", [P, E], I32)
        ntile = sb("ntile", [P, E], F32)
        last = sb("last", [P, E], F32)
        start = sb("start", [P, E], F32)
        tile_no = sb("tile_no", [P, TILES, E], F32)
        slot_f = sb("slot_f", [P, PAIRS], F32)
        part_i = sb("part_i", [P, 2, PAIRS], I32)
        part = sb("part", [P, 2, PAIRS], F32)
        hot_in = [sb(f"hot_in{b}", [P, BATCH, P], F32R) for b in range(2)]
        hot_tile = sb("hot_tile", [P, BATCH, TILES], F32)
        hot_tok = [sb(f"hot_tok{b}", [P, BATCH, TILES], F32R) for b in range(2)]
        tok_f = sb("tok_f", [P, TILES], F32)

        ps_T = [[bank(f"ps_T{b}{k}", [P, STEP]) for k in range(KC)] for b in range(2)]
        ps_L = [bank(f"ps_L{b}", [P, Q, E]) for b in range(2)]
        ps_cnt = bank("ps_cnt", [P, 2, E * NT])
        ps_tok = bank("ps_tok", [P, TILES])

        s_const = sem("s_const")
        s_pool = sem("s_pool")
        s_small = sem("s_small")
        s_xin = [sem(f"s_xin{b}") for b in range(2)]
        s_w = [sem(f"s_w{b}") for b in range(2)]
        s_whi = sem("s_whi")
        s_wlo = sem("s_wlo")
        s_stat = sem("s_stat")
        s_var = sem("s_var")
        s_go = sem("s_go")
        s_std = sem("s_std")
        s_xn = sem("s_xn")
        s_T = sem("s_T")
        s_xT = sem("s_xT")
        s_L = sem("s_L")
        s_Lc = sem("s_Lc")
        s_xout = [sem(f"s_xout{b}") for b in range(2)]
        s_Tout = [sem(f"s_Tout{b}") for b in range(2)]
        s_bhi = sem("s_bhi")
        s_blo = sem("s_blo")
        s_bias = sem("s_bias")
        s_dve = sem("s_dve")
        s_shift = sem("s_shift")
        s_exp = sem("s_exp")
        s_mask = sem("s_mask")
        s_cnt = sem("s_cnt")
        s_hot = sem("s_hot")
        s_hotmm = sem("s_hotmm")
        s_tok = sem("s_tok")

        xv = x.rearrange("b (i h p) c -> i p b h c", h=HALF, p=P)
        xnv = xn_d.rearrange("(b i h p) c -> i p b h c", b=B, h=HALF, p=P)
        wv = w_all.rearrange("e (k p) n -> e p k n", p=P)

        with nc.Block() as block:

            @block.sync
            def _(sp):
                def load_x(a):
                    at_least(sp, s_xn, a.i - 1)
                    for b in range(B):
                        sp.dma_start(xin[a.buf(2)][:, b * HALF:(b + 1) * HALF, :],
                                     xv[ds(a.i, 1), :, b, :, :].rearrange("o p h c -> p (o h) c")
                                     ).then_inc(s_xin[a.buf(2)], 16)

                def load_w(a):
                    at_least(sp, s_whi, a.i - 1)
                    at_least(sp, s_wlo, a.i - 1)
                    sp.dma_start(w_raw[a.buf(2)][:], wv[ds(a.i, 1)].rearrange("o p k n -> p (o k) n")
                                 ).then_inc(s_w[a.buf(2)], 16)

                load_x(At(0, 0, 2))
                sp.dma_start(gw[:], gate_w).then_inc(s_small, 16)
                sp.dma_start(gb[:], gate_b.rearrange("(a n) -> a n", a=1).broadcast_to([P, E])
                             ).then_inc(s_small, 16)
                sp.dma_start(vec_tf[:], first).then_inc(s_small, 16)
                sp.dma_start(vec_td[:], decay).then_inc(s_small, 16)
                sp.dma_start(b_raw[:], b_all.rearrange("(p r) -> p r", p=P)).then_inc(s_small, 16)
                load_x(At(0, 1, 2))

                def step(a, more=True):
                    at_least(sp, s_xn, a.i + 1)
                    for b in range(B):
                        sp.dma_start(xnv[ds(a.i, 1), :, b, :, :].rearrange("o p h c -> p (o h) c"),
                                     xn[a.buf(2)][:, b * HALF:(b + 1) * HALF, :]
                                     ).then_inc(s_xout[a.buf(2)], 16)
                    if more:
                        load_x(a.plus(2))
                    at_least(sp, s_xT, a.i + 1)
                    sp.dma_start(xT_d[:, ds(a.i, 1), :].rearrange("p o n -> p (o n)"),
                                 xT[a.buf(2)][:].rearrange("p k n -> p (k n)")
                                 ).then_inc(s_Tout[a.buf(2)], 16)

                step(At(0, 0, 2))
                step(At(0, 1, 2))
                with sp.Fori(1, NSTEP // 2 - 1) as u:
                    step(At(u, 0, 2))
                    step(At(u, 1, 2))
                step(At(NSTEP // 2 - 1, 0, 2), False)
                step(At(NSTEP // 2 - 1, 1, 2), False)
                rounds(sp, 2, E, load_w)

                sp.wait_ge(s_bhi, 1)
                sp.wait_ge(s_blo, 1)
                bias = bias_hl[:].rearrange("h e n -> h (e n)").bitcast(F32)
                sp.dma_start(bias[0:1, :].rearrange("o (p r) -> o p r", p=P), b_hi[:].bitcast(F32)).then_inc(s_bias, 16)
                sp.dma_start(bias[1:2, :].rearrange("o (p r) -> o p r", p=P), b_lo[:].bitcast(F32)).then_inc(s_bias, 16)
                for b in range(2):
                    sp.wait_ge(s_xout[b], NSTEP // 2 * 32)
                    sp.wait_ge(s_Tout[b], NSTEP // 2 * 16)
                sp.wait_ge(s_bias, 32)

            @block.gpsimd
            def _(pool):
                own = Own(pool, s_pool)
                nc.gpsimd.memset(ones_f[:], 1.0).then_inc(s_pool, 1)
                own.n += 1
                own.mark(nc.gpsimd.memset(ident[:], 0.0))
                own.wait()
                nc.gpsimd.affine_select(out=ident[:], in_=ident[:], compare_op=ALU.not_equal, fill=1.0,
                                        base=0, pattern=[[-1, P]], channel_multiplier=1).then_inc(s_const, 1)
                nc.gpsimd.affine_select(out=before_f[:], in_=ones_f[:], compare_op=ALU.is_gt, fill=0.0,
                                        base=0, pattern=[[1, P]], channel_multiplier=-1).then_inc(s_const, 1)
                nc.gpsimd.iota(lane_i[:], pattern=[[1, P]], base=0, channel_multiplier=0).then_inc(s_const, 1)
                nc.gpsimd.iota(token_i[:].rearrange("p (i b h) -> p i b h", b=B, h=HALF),
                               pattern=[[TIMES, NSTEP], [T, B], [P, HALF]], base=0,
                               channel_multiplier=1).then_inc(s_const, 1)
                nc.gpsimd.iota(desc_i[:], pattern=[[-1, E]], base=E, channel_multiplier=0).then_inc(s_const, 1)

                def split(a):
                    pool.wait_ge(s_whi, a.i + 1)
                    nc.gpsimd.tensor_tensor(w_lo[:, ds(a.i, 1)].rearrange("p o k n -> p (o k) n"),
                                            w_raw[a.buf(2)][:],
                                            w_hi[:, ds(a.i, 1)].rearrange("p o k n -> p (o k) n").bitcast(F32),
                                            ALU.subtract).then_inc(s_wlo, 1)

                rounds(pool, 2, E, split)

            @block.scalar
            def _(act):
                def root(a):
                    act.wait_ge(s_var, a.i + 1)
                    nc.scalar.activation(std[a.buf(2)][:], var[a.buf(2)][:], ACT.Sqrt).then_inc(s_std, 1)

                def step(a, more=True):
                    if more:
                        root(a.plus(1))
                    act.wait_ge(s_T, a.i + 1)
                    at_least(act, s_Tout[a.buf(2)], a.uses(2) * 16)
                    at_least(act, s_L, a.i - 1)
                    nc.scalar.activation(xT[a.buf(2)][:, 0, :], ps_T[a.buf(2)][0][:], ACT.Copy)
                    nc.scalar.activation(xT[a.buf(2)][:, 1, :], ps_T[a.buf(2)][1][:], ACT.Copy
                                         ).then_inc(s_xT, 1)

                def split(a):
                    act.wait_ge(s_w[a.buf(2)], (a.uses(2) + 1) * 16)
                    nc.scalar.activation(w_hi[:, ds(a.i, 1)].rearrange("p o k n -> p (o k) n"),
                                         w_raw[a.buf(2)][:], ACT.Copy).then_inc(s_whi, 1)

                root(At(0, 0, 2))
                step(At(0, 0, 2))
                step(At(0, 1, 2))
                with act.Fori(1, NSTEP // 2 - 1) as u:
                    step(At(u, 0, 2))
                    step(At(u, 1, 2))
                step(At(NSTEP // 2 - 1, 0, 2))
                step(At(NSTEP // 2 - 1, 1, 2), False)
                act.wait_ge(s_shift, 1)
                nc.scalar.activation(score[:], work[:], ACT.Exp).then_inc(s_exp, 1)
                rounds(act, 2, E, split)

            @block.tensor
            def _(pe):
                def turn(a):
                    pe.wait_ge(s_xn, a.i + 1)
                    at_least(pe, s_xT, a.i - 1)
                    for k in range(KC):
                        for q in range(Q):
                            mm = nc.tensor.transpose(ps_T[a.buf(2)][k][:, q * P:(q + 1) * P],
                                                     xn[a.buf(2)][:, q, k * P:(k + 1) * P], ident[:])
                    mm.then_inc(s_T, 1)

                def gate(a):
                    pe.wait_ge(s_xT, a.i + 1)
                    at_least(pe, s_Lc, a.i - 1)
                    for q in range(Q):
                        for k in range(KC):
                            mm = nc.tensor.matmul(ps_L[a.buf(2)][:, q, :],
                                                  xT[a.buf(2)][:, k, q * P:(q + 1) * P], gw[:, k, :],
                                                  start=(k == 0), stop=(k == KC - 1))
                    mm.then_inc(s_L, 1)

                pe.wait_ge(s_const, 5)
                pe.wait_ge(s_small, 80)
                turn(At(0, 0, 2))
                turn(At(0, 1, 2))
                gate(At(0, 0, 2))
                turn(At(1, 0, 2))
                gate(At(0, 1, 2))
                turn(At(1, 1, 2))
                gate(At(1, 0, 2))
                with pe.Fori(2, NSTEP // 2) as u:
                    turn(At(u, 0, 2))
                    gate(At(u - 1, 1, 2))
                    turn(At(u, 1, 2))
                    gate(At(u, 0, 2))
                gate(At(NSTEP // 2 - 1, 1, 2))

                pe.wait_ge(s_mask, 2)
                nc.tensor.matmul(ps_cnt[:, 0, :], before[:], mask[:].rearrange("p e j -> p (e j)"),
                                 start=True, stop=True)
                nc.tensor.matmul(ps_cnt[:, 1, :], ones[:], mask[:].rearrange("p e j -> p (e j)"),
                                 start=True, stop=True).then_inc(s_cnt, 1)
                for n in range(PAIRS // BATCH):
                    pe.wait_ge(s_hot, n + 1)
                    for g in range(BATCH):
                        mm = nc.tensor.matmul(ps_tok[:], hot_in[n % 2][:, g, :], hot_tok[n % 2][:, g, :],
                                              start=(n == 0 and g == 0),
                                              stop=(n == PAIRS // BATCH - 1 and g == BATCH - 1))
                    mm.then_inc(s_hotmm, 1)

            @block.vector
            def _(dve):
                dve.wait_ge(s_const, 5)
                nc.vector.tensor_copy(lane[:], lane_i[:])
                nc.vector.tensor_copy(token[:], token_i[:])
                nc.vector.tensor_copy(desc[:], desc_i[:])
                nc.vector.tensor_copy(ones[:], ones_f[:])
                nc.vector.tensor_copy(ones2[:], ones_f[0:2, :])
                nc.vector.memset(keep[:], 1.0)
                nc.vector.tensor_copy(before[:], before_f[:]).then_inc(s_mask, 1)
                dve.wait_ge(s_mask, 1)
                nc.vector.memset(keep[:, :, 0:1], 0.0)
                PER = 2

                def measure(a):
                    own = OwnIn(dve, s_stat, a, PER)
                    dve.wait_ge(s_xin[a.buf(2)], (a.uses(2) + 1) * 32)
                    for q in range(Q):
                        ins = nc.vector.bn_stats(stats[a.buf(2)][:, q, :], xin[a.buf(2)][:, q, :])
                    own.link(ins)
                    dve.sem_inc(s_go, 1)
                    for q in range(Q):
                        ins = nc.vector.bn_aggr(mv[a.buf(2)][:, q, :], stats[a.buf(2)][:, q, :])
                    own.link(ins)
                    own.close()
                    at_least(dve, s_std, a.i - 1)
                    nc.vector.tensor_scalar(var[a.buf(2)][:], mv[a.buf(2)][:, :, 1], EPS, None, ALU.add
                                            ).then_inc(s_var, 1)

                def norm(a):
                    own = OwnIn(dve, s_dve, a, 1)
                    dve.wait_ge(s_std, a.i + 1)
                    own.link(nc.vector.reciprocal(rstd[a.buf(2)][:], std[a.buf(2)][:]))
                    own.close()
                    at_least(dve, s_T, a.i - 1)
                    at_least(dve, s_xout[a.buf(2)], a.uses(2) * 32)
                    for q in range(Q):
                        ins = nc.vector.tensor_scalar(xn[a.buf(2)][:, q, :], xin[a.buf(2)][:, q, :],
                                                      mv[a.buf(2)][:, q, 0:1], rstd[a.buf(2)][:, q:q + 1],
                                                      ALU.subtract, ALU.mult)
                    ins.then_inc(s_xn, 1)

                def take(a):
                    dve.wait_ge(s_L, a.i + 1)
                    nc.vector.tensor_tensor(logits[:, ds(a.i * Q, Q), :], ps_L[a.buf(2)][:],
                                            gb[:, None, :].broadcast_to([P, Q, E]), ALU.add
                                            ).then_inc(s_Lc, 1)

                dve.wait_ge(s_small, 80)
                nc.vector.tensor_copy(b_hi[:], b_raw[:]).then_inc(s_bhi, 1)
                dve.wait_ge(s_bhi, 1)
                nc.vector.tensor_tensor(b_lo[:], b_raw[:], b_hi[:].bitcast(F32), ALU.subtract).then_inc(s_blo, 1)
                measure(At(0, 0, 2))
                norm(At(0, 0, 2))
                measure(At(0, 1, 2))
                norm(At(0, 1, 2))
                measure(At(1, 0, 2))
                norm(At(1, 0, 2))
                take(At(0, 0, 2))
                measure(At(1, 1, 2))
                with dve.Fori(1, NSTEP // 2 - 1) as u:
                    norm(At(u, 1, 2))
                    take(At(u - 1, 1, 2))
                    measure(At(u + 1, 0, 2))
                    norm(At(u + 1, 0, 2))
                    take(At(u, 0, 2))
                    measure(At(u + 1, 1, 2))
                L = NSTEP // 2 - 1
                norm(At(L, 1, 2))
                take(At(L - 1, 1, 2))
                take(At(L, 0, 2))
                take(At(L, 1, 2))

                def wide(ap):
                    return ap[:, :, None].broadcast_to([P, NT, E])

                own = Own(dve, s_dve)
                own.n = NSTEP
                dve.wait_ge(s_Lc, NSTEP)
                own.link(nc.vector.tensor_reduce(red[:], logits[:], AX_X, ALU.max))
                nc.vector.tensor_tensor(work[:], logits[:], wide(red[:]), ALU.subtract).then_inc(s_shift, 1)
                dve.wait_ge(s_exp, 1)
                own.link(nc.vector.tensor_reduce(red[:], score[:], AX_X, ALU.add))
                own.link(nc.vector.reciprocal(red2[:], red[:]))
                own.link(nc.vector.tensor_tensor(score[:], score[:], wide(red2[:]), ALU.mult))
                cur = score
                for k in range(TOPK):
                    own.link(nc.vector.tensor_reduce(gates[:, k, :], cur[:], AX_X, ALU.max))
                    own.link(nc.vector.tensor_tensor(work2[:], cur[:], wide(gates[:, k, :]), ALU.is_equal))
                    own.link(nc.vector.tensor_tensor(work2[:], work2[:], desc[:, None, :].broadcast_to([P, NT, E]),
                                                     ALU.mult))
                    own.link(nc.vector.tensor_reduce(red[:], work2[:], AX_X, ALU.max))
                    own.link(nc.vector.tensor_tensor(hot[k][:], work2[:], wide(red[:]), ALU.is_equal))
                    if k == 0:
                        own.link(nc.vector.scalar_tensor_tensor(out=work[:], in0=hot[0][:], scalar=-2.0,
                                                                in1=score[:], op0=ALU.mult, op1=ALU.add))
                        cur = work
                nc.vector.tensor_tensor(mask[:].rearrange("p e j -> p j e"), hot[0][:], hot[1][:], ALU.add
                                        ).then_inc(s_mask, 1)
                dve.wait_ge(s_cnt, 1)
                total = ps_cnt[:, 1, :].rearrange("p (e j) -> p e j", e=E)
                prefix = ps_cnt[:, 0, :].rearrange("p (e j) -> p e j", e=E)
                own.link(nc.vector.tensor_tensor_scan(out=filled[:].rearrange("p e j -> p (e j)"),
                                                      data0=keep[:].rearrange("p e j -> p (e j)"),
                                                      data1=ps_cnt[:, 1, :], initial=0.0,
                                                      op0=ALU.mult, op1=ALU.add))
                own.link(nc.vector.tensor_tensor(place[:], filled[:], total, ALU.subtract))
                own.link(nc.vector.tensor_tensor(place[:], place[:], prefix, ALU.add))
                own.link(nc.vector.tensor_scalar(ntile_i[:], filled[:, :, NT - 1], float(P - 1), None, ALU.add))
                own.link(nc.vector.tensor_scalar(ntile_i[:], ntile_i[:], 7, None, ALU.arith_shift_right))
                own.link(nc.vector.tensor_copy(ntile[:], ntile_i[:]))
                own.link(nc.vector.tensor_tensor_scan(out=last[:], data0=ones_f[:, 0:E], data1=ntile[:],
                                                      initial=0.0, op0=ALU.mult, op1=ALU.add))
                own.link(nc.vector.tensor_tensor(start[:], last[:], ntile[:], ALU.subtract))
                own.link(nc.vector.scalar_tensor_tensor(out=place[:], in0=start[:, :, None].broadcast_to([P, E, NT]),
                                                        scalar=float(P), in1=place[:], op0=ALU.mult, op1=ALU.add))
                for k in range(TOPK):
                    own.link(nc.vector.tensor_tensor(work2[:], hot[k][:], place[:].rearrange("p e j -> p j e"),
                                                     ALU.mult))
                    own.link(nc.vector.tensor_reduce(slot_f[:, k * NT:(k + 1) * NT], work2[:], AX_X, ALU.add))
                own.link(nc.vector.tensor_scalar(slot_f[:], slot_f[:], 0.0, float(TILES * P - 1), ALU.max, ALU.min))
                own.link(nc.vector.tensor_copy(slots[:].rearrange("p k j -> p (k j)"), slot_f[:]))
                own.mark(nc.vector.tensor_scalar(part_i[:, 0, :], slots[:].rearrange("p k j -> p (k j)"), 7, None,
                                                 ALU.arith_shift_right))
                own.link(nc.vector.tensor_scalar(part_i[:, 1, :], slots[:].rearrange("p k j -> p (k j)"), P - 1, None,
                                                 ALU.bitwise_and))
                own.link(nc.vector.tensor_copy(part[:], part_i[:]))
                for n in range(PAIRS // BATCH):
                    sl = slice(n * BATCH, (n + 1) * BATCH)
                    tj = (n * BATCH) % NT
                    if n >= 2:
                        dve.wait_ge(s_hotmm, n - 1)
                    own.mark(nc.vector.tensor_tensor(hot_in[n % 2][:],
                                                     part[:, 1, sl][:, :, None].broadcast_to([P, BATCH, P]),
                                                     lane[:, None, :].broadcast_to([P, BATCH, P]), ALU.is_equal))
                    if n >= 1:
                        dve.wait_ge(s_hot, n)
                    own.link(nc.vector.tensor_tensor(hot_tile[:],
                                                     part[:, 0, sl][:, :, None].broadcast_to([P, BATCH, TILES]),
                                                     lane[:, None, 0:TILES].broadcast_to([P, BATCH, TILES]),
                                                     ALU.is_equal))
                    nc.vector.tensor_tensor(hot_tok[n % 2][:], hot_tile[:],
                                            token[:, tj:tj + BATCH][:, :, None].broadcast_to([P, BATCH, TILES]),
                                            ALU.mult).then_inc(s_hot, 1)
                own.link(nc.vector.tensor_tensor(tile_no[:, :, 0:E - 1],
                                                 lane[:, 0:TILES][:, :, None].broadcast_to([P, TILES, E - 1]),
                                                 last[:, None, 0:E - 1].broadcast_to([P, TILES, E - 1]),
                                                 ALU.is_ge))
                own.link(nc.vector.tensor_reduce(tok_f[:], tile_no[:, :, 0:E - 1], AX_X, ALU.add))
                own.link(nc.vector.tensor_copy(tile_exp[:], tok_f[:]))
                dve.wait_ge(s_hotmm, PAIRS // BATCH)
                nc.vector.tensor_scalar(tile_tok[:], ps_tok[:], 0.0, float(TOK - 1), ALU.max, ALU.min
                                        ).then_inc(s_tok, 1)


def run_experts(nc, xn_d, y_d, tab_d, vec_tf, vec_td, ident, tile_tok, tile_exp, w_hi, w_lo, bias_hl, ones2, loads):
    with ExitStack() as ctx:
        def sb(name, shape, dt):
            return ctx.enter_context(nc.sbuf_tensor(name, shape, dt))

        def bank(name, shape):
            return ctx.enter_context(nc.psum_tensor(name, shape, F32))

        def sem(name):
            return ctx.enter_context(nc.semaphore(name))

        NG = 4
        picked = [sb(f"picked{b}", [P, 1], I32) for b in range(NG)]
        xg = [sb(f"xg{b}", [P, C], F32) for b in range(NG)]
        x_hi = [sb(f"x_hi{b}", [P, KC, P], F32R) for b in range(2)]
        x_lo = [sb(f"x_lo{b}", [P, KC, P], F32R) for b in range(2)]
        act1 = [sb(f"act1{b}", [P, FF], F32) for b in range(2)]
        hid = [sb(f"hid{b}", [P, FF], F32) for b in range(2)]
        h_hi = [sb(f"h_hi{b}", [P, KC, P], F32R) for b in range(2)]
        h_lo = [sb(f"h_lo{b}", [P, KC, P], F32R) for b in range(2)]
        y = [sb(f"y{b}", [P, C], F32) for b in range(2)]
        s_p = sb("s_p", [P, KC, PIECE + 1], F32)
        s_b = sb("s_b", [P, KC, PIECE + 1], F32)
        grow = sb("grow", [P, KC], F32)
        zero = sb("zero", [P, 1], F32)
        dif = sb("dif", [P, 2, KC, PIECE], F32)
        sides = sb("sides", [P, 2, 2, KC, PIECE], F32)
        gated = [sb(f"gated{b}", [P, FF], F32) for b in range(2)]
        decays = sb("decays", [P, 2, 2, KC, PIECE], F32)
        den = sb("den", [P, KC, PIECE], F32)
        rden = sb("rden", [P, KC, PIECE], F32)
        coef = sb("coef", [P, 2, KC, PIECE], F32)
        ps_x = [bank(f"ps_x{b}", [P, KC, P]) for b in range(2)]
        ps_g = [bank(f"ps_g{b}", [P, 2 * FF]) for b in range(2)]
        ps_h = [bank(f"ps_h{b}", [P, KC, P]) for b in range(2)]
        ps_y = [bank(f"ps_y{b}", [P, C]) for b in range(2)]

        c_idx = sem("c_idx")
        c_go = sem("c_go")
        c_gath = [sem(f"c_gath{b}") for b in range(NG)]
        c_tx = sem("c_tx")
        c_xhi = sem("c_xhi")
        c_xlo = sem("c_xlo")
        c_g = sem("c_g")
        c_silu = sem("c_silu")
        c_h = sem("c_h")
        c_th = sem("c_th")
        c_hhi = sem("c_hhi")
        c_hlo = sem("c_hlo")
        c_y = sem("c_y")
        c_yc = sem("c_yc")
        c_yst = [sem(f"c_yst{b}") for b in range(2)]
        c_ld = sem("c_ld")
        t_own = sem("t_own")
        t_pool = sem("t_pool")
        t_dif = sem("t_dif")
        t_carry = sem("t_carry")
        t_sides = sem("t_sides")
        c_gate = sem("c_gate")
        t_exp = sem("t_exp")
        t_bb = sem("t_bb")
        t_den = sem("t_den")
        t_rec = sem("t_rec")
        t_coef = sem("t_coef")
        t_est = sem("t_est")
        t_cst = sem("t_cst")

        with nc.Block() as block:

            @block.sync
            def _(sp):
                for dst, src in loads:
                    sp.dma_start(dst, src).then_inc(c_ld, 16)

                def store(a):
                    sp.wait_ge(c_yc, a.i + 1)
                    sp.dma_start(y_d[ds(a.i * P, P), :], y[a.buf(2)][:]).then_inc(c_yst[a.buf(2)], 16)

                def store_table(v, kinds, src, sem_):
                    sp.dma_start(tab_d[ds(v, 1), :, kinds].rearrange("o p n k t -> p (o n) (k t)"),
                                 src.rearrange("p n k t -> p n (k t)")).then_inc(sem_, 16)

                for r in range(4):
                    store(At(0, r, 4))
                with sp.Fori(1, TILES // 4 - 1) as u:
                    v = u - 1
                    store(At(u, 0, 4))
                    sp.wait_ge(t_exp, u)
                    store_table(v, slice(0, 2), decays[:, 1], t_est)
                    store(At(u, 1, 4))
                    store(At(u, 2, 4))
                    store(At(u, 3, 4))
                    sp.wait_ge(t_coef, u)
                    store_table(v, slice(2, 4), coef[:], t_cst)
                for r in range(4):
                    store(At(TILES // 4 - 1, r, 4))
                sp.wait_ge(t_est, NPIECE * 16)
                sp.wait_ge(t_cst, NPIECE * 16)
                for b in range(2):
                    sp.wait_ge(c_yst[b], TILES // 2 * 16)
                sp.wait_ge(c_ld, 16 * len(loads))

            @block.gpsimd
            def _(pool):
                def gather(a):
                    at_least(pool, c_tx, a.i - NG + 1)
                    nc.gpsimd.tensor_copy(picked[a.buf(NG)][:], tile_tok[:, ds(a.i, 1)]).then_inc(c_idx, 1)
                    pool.wait_ge(c_idx, a.i + 1)
                    pool.sem_inc(c_go, 1)
                    pool.indirect_dma_start(
                        out=xg[a.buf(NG)][:], out_offset=None, in_=xn_d[:, :],
                        in_offset=bass.IndirectOffsetOnAxis(ap=picked[a.buf(NG)][:, 0:1], axis=0)
                    ).then_inc(c_gath[a.buf(NG)], 16)

                def denominator(u):
                    own = OwnIn(pool, t_pool, At(u - 1, 0, 1), 2)
                    pool.wait_ge(t_bb, u)
                    own.link(nc.gpsimd.tensor_tensor(den[:], decays[:, 0, 0], s_b[:, :, 0:PIECE], ALU.mult))
                    own.link(nc.gpsimd.tensor_tensor(den[:], den[:], decays[:, 0, 1], ALU.add))
                    own.close()
                    pool.sem_inc(c_go, 1)
                    nc.gpsimd.tensor_scalar(den[:], den[:], 1e-6, 2.0, ALU.add, ALU.mult).then_inc(t_den, 1)

                def factors(u):
                    pool.wait_ge(t_rec, u)
                    if not isinstance(u, int) or u > 1:
                        pool.wait_ge(t_cst, u * 16 - 16)
                    nc.gpsimd.tensor_tensor(coef[:], decays[:, 0], rden[:, None].broadcast_to([P, 2, KC, PIECE]),
                                            ALU.mult).then_inc(t_coef, 1)

                def turn(v, first=False):
                    gather(At(v, 0, 4))
                    if not first:
                        factors(v - 2)
                    gather(At(v, 1, 4))
                    gather(At(v, 2, 4))
                    gather(At(v, 3, 4))
                    denominator(v - 1)

                for r in range(8):
                    gather(At(r // 4, r % 4, 4))
                turn(2, first=True)
                turn(3)
                with pool.Fori(4, TILES // 4) as v:
                    turn(v)
                factors(NPIECE)

            @block.tensor
            def _(pe):
                def turn_x(a):
                    pe.wait_ge(c_gath[a.buf(NG)], (a.uses(NG) + 1) * 16)
                    at_least(pe, c_xlo, a.i - 1)
                    for k in range(KC):
                        mm = nc.tensor.transpose(ps_x[a.buf(2)][:, k, :], xg[a.buf(NG)][:, k * P:(k + 1) * P],
                                                 ident[:])
                    mm.then_inc(c_tx, 1)

                def experts(u, first, last):
                    _, values = nc.values_load_multi_w_load_instructions(
                        tile_exp[0:1, ds(At(u, 0, 4).plus(first).i, last + 1 - first)],
                        engines=[mybir.EngineType.PE], min_val=0, max_val=E - 1)
                    return dict(zip(range(first, last + 1), values))

                def three(out, hi, lo, e, cols):
                    for k in range(KC):
                        for n, (x, w) in enumerate([(hi, w_hi), (hi, w_lo), (lo, w_hi)]):
                            nc.tensor.matmul(out, x[:, k, :],
                                             w[:, ds(e, 1), k, cols].rearrange("p o n -> p (o n)"),
                                             start=(k == 0 and n == 0), stop=False)
                    return nc.tensor.matmul(out, ones2[:],
                                            bias_hl[:, ds(e, 1), cols].rearrange("p o n -> p (o n)"),
                                            start=False, stop=True)

                def up(a, e):
                    pe.wait_ge(c_xlo, a.i + 1)
                    at_least(pe, c_h, a.i - 1)
                    three(ps_g[a.buf(2)][:], x_hi[a.buf(2)], x_lo[a.buf(2)], e, slice(0, 2 * FF)).then_inc(c_g, 1)

                def turn_h(a):
                    pe.wait_ge(c_h, a.i + 1)
                    at_least(pe, c_hlo, a.i - 1)
                    for k in range(KC):
                        mm = nc.tensor.transpose(ps_h[a.buf(2)][:, k, :], hid[a.buf(2)][:, k * P:(k + 1) * P],
                                                 ident[:])
                    mm.then_inc(c_th, 1)

                def down(a, e):
                    pe.wait_ge(c_hlo, a.i + 1)
                    at_least(pe, c_yc, a.i - 1)
                    three(ps_y[a.buf(2)][:], h_hi[a.buf(2)], h_lo[a.buf(2)], e, slice(2 * FF, WALL)).then_inc(c_y, 1)

                def tile(a, es, first=False, left=3):
                    if left > 0:
                        up(a.plus(1), es[a.r + 1])
                    turn_h(a)
                    if left > 2:
                        turn_x(a.plus(3))
                    if not first:
                        down(a.plus(-1), es[a.r - 1])

                turn_x(At(0, 0, 4))
                turn_x(At(0, 1, 4))
                es = experts(0, 0, 4)
                up(At(0, 0, 4), es[0])
                turn_x(At(0, 2, 4))
                for r in range(4):
                    tile(At(0, r, 4), es, first=(r == 0))
                with pe.Fori(1, TILES // 4 - 1) as u:
                    es = experts(u, -1, 4)
                    for r in range(4):
                        tile(At(u, r, 4), es)
                es = experts(TILES // 4 - 1, -1, 3)
                for r in range(4):
                    tile(At(TILES // 4 - 1, r, 4), es, left=3 - r)
                down(At(TILES // 4 - 1, 3, 4), es[3])

            @block.scalar
            def _(act):
                def cut_x(a):
                    act.wait_ge(c_tx, a.i + 1)
                    at_least(act, c_g, a.i - 1)
                    nc.scalar.activation(x_hi[a.buf(2)][:], ps_x[a.buf(2)][:], ACT.Copy).then_inc(c_xhi, 1)

                def silu(a):
                    act.wait_ge(c_g, a.i + 1)
                    at_least(act, c_h, a.i - 1)
                    nc.scalar.activation(act1[a.buf(2)][:], ps_g[a.buf(2)][:, 0:FF], ACT.Tanh, scale=0.5
                                         ).then_inc(c_silu, 1)

                def cut_h(a):
                    act.wait_ge(c_th, a.i + 1)
                    at_least(act, c_y, a.i - 1)
                    nc.scalar.activation(h_hi[a.buf(2)][:], ps_h[a.buf(2)][:], ACT.Copy, scale=0.5).then_inc(c_hhi, 1)

                def result(a):
                    act.wait_ge(c_y, a.i + 1)
                    at_least(act, c_yst[a.buf(2)], a.uses(2) * 16)
                    nc.scalar.activation(y[a.buf(2)][:], ps_y[a.buf(2)][:], ACT.Copy).then_inc(c_yc, 1)

                def tile(a, first=False, left=3):
                    if left > 0:
                        silu(a.plus(1))
                    cut_h(a)
                    if left > 2:
                        cut_x(a.plus(3))
                    if not first:
                        result(a.plus(-1))

                cut_x(At(0, 0, 4))
                cut_x(At(0, 1, 4))
                silu(At(0, 0, 4))
                cut_x(At(0, 2, 4))

                def halves(u):
                    act.wait_ge(t_dif, u + 1)
                    at_least(act, t_exp, u)
                    nc.scalar.activation(sides[:, 0], dif[:], ACT.Relu)
                    nc.scalar.activation(sides[:, 1], dif[:], ACT.Relu, scale=-1.0).then_inc(t_sides, 1)

                def exps(u):
                    act.wait_ge(t_sides, u)
                    if not isinstance(u, int) or u > 1:
                        act.wait_ge(t_est, u * 16 - 16)
                        act.wait_ge(t_coef, u - 1)
                    nc.scalar.activation(decays[:], sides[:].rearrange("p s n k t -> p n s k t"), ACT.Exp, scale=-1.0
                                         ).then_inc(t_exp, 1)

                def turn(u):
                    for r in range(4):
                        tile(At(u, r, 4))
                        if r == 0:
                            exps(u)
                        if r == 2:
                            halves(u)

                for r in range(4):
                    tile(At(0, r, 4), first=(r == 0))
                halves(0)
                turn(1)
                with act.Fori(2, TILES // 4 - 1) as u:
                    turn(u)
                for r in range(4):
                    tile(At(TILES // 4 - 1, r, 4), left=3 - r)
                result(At(TILES // 4 - 1, 3, 4))

            @block.vector
            def _(dve):
                def cut_x(a):
                    dve.wait_ge(c_xhi, a.i + 1)
                    at_least(dve, c_g, a.i - 1)
                    nc.vector.tensor_tensor(x_lo[a.buf(2)][:], ps_x[a.buf(2)][:], x_hi[a.buf(2)][:].bitcast(F32),
                                            ALU.subtract).then_inc(c_xlo, 1)

                def gate(a):
                    dve.wait_ge(c_silu, a.i + 1)
                    nc.vector.scalar_tensor_tensor(out=gated[a.buf(2)][:], in0=act1[a.buf(2)][:], scalar=1.0,
                                                   in1=ps_g[a.buf(2)][:, 0:FF], op0=ALU.add, op1=ALU.mult
                                                   ).then_inc(c_gate, 1)

                def hidden(a):
                    dve.wait_ge(c_gate, a.i + 1)
                    at_least(dve, c_th, a.i - 1)
                    nc.vector.tensor_tensor(hid[a.buf(2)][:], ps_g[a.buf(2)][:, FF:2 * FF], gated[a.buf(2)][:],
                                            ALU.mult).then_inc(c_h, 1)

                def cut_h(a):
                    dve.wait_ge(c_hhi, a.i + 1)
                    at_least(dve, c_y, a.i - 1)
                    nc.vector.scalar_tensor_tensor(out=h_lo[a.buf(2)][:], in0=ps_h[a.buf(2)][:], scalar=0.5,
                                                   in1=h_hi[a.buf(2)][:].bitcast(F32), op0=ALU.mult,
                                                   op1=ALU.subtract).then_inc(c_hlo, 1)

                def tile(a, left=3):
                    if left > 0:
                        gate(a.plus(1))
                    cut_h(a)
                    if left > 0:
                        hidden(a.plus(1))
                    if left > 2:
                        cut_x(a.plus(3))

                def differences(u):
                    own = OwnIn(dve, t_own, At(u, 0, 1), 2)
                    if isinstance(u, int) and u == 0:
                        own.n += 1
                    else:
                        own.link(nc.vector.tensor_copy(s_p[:, :, 0:1], s_p[:, :, PIECE:PIECE + 1]))
                    for c in range(KC):
                        ins = nc.vector.tensor_tensor_scan(out=s_p[:, c, 1:PIECE + 1],
                                                           data0=grow[:, c:c + 1].broadcast_to([P, PIECE]),
                                                           data1=zero[:].broadcast_to([P, PIECE]),
                                                           initial=s_p[:, c, 0:1], op0=ALU.add, op1=ALU.add)
                    own.link(ins)
                    own.close()
                    at_least(dve, t_sides, u)
                    for n, vec in enumerate((vec_tf, vec_td)):
                        for c in range(KC):
                            ins = nc.vector.scalar_tensor_tensor(out=dif[:, n, c, :], in0=s_p[:, c, 0:PIECE],
                                                                 scalar=vec[:, c:c + 1], in1=s_p[:, c, 0:PIECE],
                                                                 op0=ALU.add, op1=ALU.subtract)
                    ins.then_inc(t_dif, 1)

                def scan_b(u):
                    dve.wait_ge(t_exp, u)
                    if not isinstance(u, int) or u > 1:
                        dve.wait_ge(t_den, u - 1)
                        nc.vector.tensor_copy(s_b[:, :, 0:1], s_b[:, :, PIECE:PIECE + 1]).then_inc(t_carry, 1)
                        dve.wait_ge(t_carry, u)
                    for c in range(KC):
                        ins = nc.vector.tensor_tensor_scan(out=s_b[:, c, 1:PIECE + 1], data0=decays[:, 1, 0, c, :],
                                                           data1=decays[:, 1, 1, c, :], initial=s_b[:, c, 0:1],
                                                           op0=ALU.mult, op1=ALU.add)
                    ins.then_inc(t_bb, 1)

                def invert(u):
                    dve.wait_ge(t_den, u)
                    nc.vector.reciprocal(rden[:], den[:]).then_inc(t_rec, 1)

                def turn(u):
                    after = {0: differences, 1: scan_b, 2: invert}
                    for r in range(4):
                        tile(At(u, r, 4))
                        if r in after:
                            after[r](u)

                nc.vector.memset(zero[:], 0.0)
                nc.vector.memset(s_b[:, :, 0:1], 0.0)
                nc.vector.memset(s_p[:, :, 0:1], -10000.0)
                nc.vector.tensor_scalar(grow[:], vec_td[:], 0.0, None, ALU.max).then_inc(t_own, 1)
                dve.wait_ge(t_own, 1)
                nc.vector.sem_inc(t_carry, 1)
                cut_x(At(0, 0, 4))
                cut_x(At(0, 1, 4))
                gate(At(0, 0, 4))
                hidden(At(0, 0, 4))
                cut_x(At(0, 2, 4))
                for r in range(4):
                    tile(At(0, r, 4))
                differences(0)
                turn(1)
                with dve.Fori(2, TILES // 4 - 1) as u:
                    turn(u)
                for r in range(4):
                    tile(At(TILES // 4 - 1, r, 4), left=3 - r)


def mix(nc, x, xT_d, y_d, tab_d, out, slots, gates, raw_vr, raw_o, raw_s13, raw_s2,
        vec_b1, vec_b3, row_b2):
    with ExitStack() as ctx:
        def sb(name, shape, dt):
            return ctx.enter_context(nc.sbuf_tensor(name, shape, dt))

        def bank(name, shape):
            return ctx.enter_context(nc.psum_tensor(name, shape, F32))

        def sem(name):
            return ctx.enter_context(nc.semaphore(name))

        vr_hi, vr_lo = (sb(f"vr_{s}", [P, KC, 2 * C], F32R) for s in ("hi", "lo"))
        o_hi, o_lo = (sb(f"o_{s}", [P, KC, C], F32R) for s in ("hi", "lo"))
        s13_hi, s13_lo = (sb(f"s13_{s}", [P, KC, 2 * SF], F32R) for s in ("hi", "lo"))
        s2_hi, s2_lo = (sb(f"s2_{s}", [P, KS, C], F32R) for s in ("hi", "lo"))
        splits = [(raw_vr, vr_hi, vr_lo), (raw_s13, s13_hi, s13_lo), (raw_o, o_hi, o_lo), (raw_s2, s2_hi, s2_lo)]
        xT = [sb(f"col{b}", [P, KC, STEP], F32) for b in range(2)]
        x_hi = [sb(f"col_hi{b}", [P, KC, STEP], F32R) for b in range(2)]
        x_lo = [sb(f"col_lo{b}", [P, KC, STEP], F32R) for b in range(2)]
        res = [sb(f"res{b}", [P, Q, C], F32) for b in range(2)]
        yg = [sb(f"yg{b}", [P, TOPK, Q, C], F32) for b in range(2)]
        picked = [sb(f"rows{b}", [P, TOPK, Q], I32) for b in range(2)]
        sa = sb("sa", [P, KC * B, TIMES + 1], F32)
        table = [sb(f"table{b}", [P, 4, KC, TIMES], F32) for b in range(2)]
        fed = sb("fed", [P, KC, B, TIMES], F32)
        part_a = sb("part_a", [P, KC, B, TIMES], F32)
        part_v = sb("part_v", [P, KC, B, TIMES], F32)
        th = sb("th", [P, KC, B, TIMES], F32)
        rw = sb("rw", [P, KC, B, TIMES], F32)
        a_hi = sb("a_hi", [P, KC, STEP], F32R)
        a_lo = sb("a_lo", [P, KC, STEP], F32R)
        act1 = [sb(f"sact{b}", [P, STEP], F32) for b in range(2)]
        hid = [sb(f"shid{b}", [P, STEP], F32) for b in range(2)]
        s_hi = sb("s_hi", [P, KS, STEP], F32R)
        s_lo = sb("s_lo", [P, KS, STEP], F32R)
        ps_v = bank("ps_v", [P, KC, STEP])
        ps_r = bank("ps_r", [P, KC, STEP])
        ps_w = [bank(f"ps_w{b}", [P, STEP]) for b in range(4)]

        b_xT = [sem(f"b_xT{b}") for b in range(2)]
        b_res = [sem(f"b_res{b}") for b in range(2)]
        b_ost = [sem(f"b_ost{b}") for b in range(2)]
        b_gath = [sem(f"b_gath{b}") for b in range(2)]
        b_idx = sem("b_idx")
        b_go = sem("b_go")
        b_whi = sem("b_whi")
        b_wlo = sem("b_wlo")
        b_xhi = sem("b_xhi")
        b_xlo = sem("b_xlo")
        b_xb = sem("b_xb")
        b_v = sem("b_v")
        b_r = sem("b_r")
        b_tanh = sem("b_tanh")
        b_rw = sem("b_rw")
        b_ahi = sem("b_ahi")
        b_alo = sem("b_alo")
        b_tab = [sem(f"b_tab{b}") for b in range(2)]
        b_z = sem("b_z")
        b_silu = sem("b_silu")
        b_h = sem("b_h")
        b_shi = sem("b_shi")
        b_slo = sem("b_slo")
        b_o = sem("b_o")
        b_fin = sem("b_fin")
        b_a = sem("b_a")
        b_slot = sem("b_slot")

        xv = x.rearrange("b (i h p) c -> i p b h c", h=HALF, p=P)
        ov = out.rearrange("b (i h p) c -> i p b h c", h=HALF, p=P)
        MIX = 6
        LAST = At(NSTEP // 2 - 1, 1, 2)

        def steps(eng, body):
            body(At(0, 0, 2), True, 2)
            body(At(0, 1, 2), False, 2)
            with eng.Fori(1, NSTEP // 2 - 1) as u:
                body(At(u, 0, 2), False, 2)
                body(At(u, 1, 2), False, 2)
            body(At(NSTEP // 2 - 1, 0, 2), False, 1)
            body(At(NSTEP // 2 - 1, 1, 2), False, 0)

        with nc.Block() as block:

            @block.sync
            def _(sp):
                def load_cols(a):
                    at_least(sp, b_xhi, a.i - 1)
                    at_least(sp, b_xlo, a.i - 1)
                    sp.dma_start(xT[a.buf(2)][:].rearrange("p k n -> p (k n)"),
                                 xT_d[:, ds(a.i, 1), :].rearrange("p o n -> p (o n)")).then_inc(b_xT[a.buf(2)], 16)

                def load_rows(a):
                    at_least(sp, b_ost[a.buf(2)], a.uses(2) * 32)
                    for b in range(B):
                        sp.dma_start(res[a.buf(2)][:, b * HALF:(b + 1) * HALF, :],
                                     xv[ds(a.i, 1), :, b, :, :].rearrange("o p h c -> p (o h) c")
                                     ).then_inc(b_res[a.buf(2)], 16)

                def load_table(a):
                    at_least(sp, b_a, a.i * MIX - MIX)
                    for h in range(TIMES // PIECE):
                        sp.dma_start(
                            table[a.buf(2)][:, :, :, h * PIECE:(h + 1) * PIECE].rearrange("p n k t -> p (n k) t"),
                            tab_d[ds(a.i * (TIMES // PIECE) + h, 1)].rearrange("o p n k t -> p (o n k) t")
                        ).then_inc(b_tab[a.buf(2)], 16)

                load_cols(At(0, 0, 2))
                load_table(At(0, 0, 2))
                load_cols(At(0, 1, 2))
                load_table(At(0, 1, 2))
                load_rows(At(0, 0, 2))
                load_rows(At(0, 1, 2))

                def step(a, first, left):
                    if left > 1:
                        load_cols(a.plus(2))
                        load_table(a.plus(2))
                    sp.wait_ge(b_fin, a.i * Q + Q)
                    for b in range(B):
                        sp.dma_start(ov[ds(a.i, 1), :, b, :, :].rearrange("o p h c -> p (o h) c"),
                                     res[a.buf(2)][:, b * HALF:(b + 1) * HALF, :]).then_inc(b_ost[a.buf(2)], 16)
                    if left > 1:
                        load_rows(a.plus(2))

                steps(sp, step)
                for b in range(2):
                    sp.wait_ge(b_ost[b], NSTEP // 2 * 32)

            @block.gpsimd
            def _(pool):
                def gather(a):
                    at_least(pool, b_fin, a.i * Q - Q)
                    nc.gpsimd.tensor_copy(picked[a.buf(2)][:], slots[:, :, ds(a.i * Q, Q)]).then_inc(b_idx, 1)
                    pool.wait_ge(b_idx, a.i + 1)
                    pool.sem_inc(b_go, 1)
                    for k in range(TOPK):
                        for q in range(Q):
                            pool.indirect_dma_start(
                                out=yg[a.buf(2)][:, k, q, :], out_offset=None, in_=y_d[:, :],
                                in_offset=bass.IndirectOffsetOnAxis(ap=picked[a.buf(2)][:, k, q:q + 1], axis=0)
                            ).then_inc(b_gath[a.buf(2)], 16)

                def cut(a):
                    pool.wait_ge(b_xhi, a.i + 1)
                    at_least(pool, b_z, a.i * KS - KS)
                    nc.gpsimd.tensor_tensor(x_lo[a.buf(2)][:], xT[a.buf(2)][:], x_hi[a.buf(2)][:].bitcast(F32),
                                            ALU.subtract).then_inc(b_xlo, 1)

                def bias(a):
                    pool.wait_ge(b_res[a.buf(2)], (a.uses(2) + 1) * 32)
                    nc.gpsimd.tensor_tensor(res[a.buf(2)][:], res[a.buf(2)][:],
                                            row_b2[:, None, :].broadcast_to([P, Q, C]), ALU.add).then_inc(b_xb, 1)

                def step(a, first, left):
                    gather(a)
                    if left > 0:
                        cut(a.plus(1))
                    bias(a)

                cut(At(0, 0, 2))
                steps(pool, step)

            @block.tensor
            def _(pe):
                def three(out, w_hi, w_lo, x_hi, x_lo, start, stop):
                    nc.tensor.matmul(out, w_hi, x_hi, start=start, stop=False)
                    nc.tensor.matmul(out, w_hi, x_lo, start=False, stop=False)
                    return nc.tensor.matmul(out, w_lo, x_hi, start=False, stop=stop)

                def columns(out, hi, lo, n0, xh, xl):
                    for k in range(KC):
                        mm = three(out, hi[:, k, n0:n0 + P], lo[:, k, n0:n0 + P], xh[:, k, :], xl[:, k, :],
                                   k == 0, k == KC - 1)
                    return mm

                def values(a):
                    pe.wait_ge(b_xlo, a.i + 1)
                    at_least(pe, b_a, a.i * MIX)
                    for m in range(KC):
                        mm = columns(ps_v[:, m, :], vr_hi, vr_lo, m * P, x_hi[a.buf(2)], x_lo[a.buf(2)])
                    mm.then_inc(b_v, 1)
                    at_least(pe, b_tanh, a.i)
                    for m in range(KC):
                        mm = columns(ps_r[:, m, :], vr_hi, vr_lo, C + m * P, x_hi[a.buf(2)], x_lo[a.buf(2)])
                    mm.then_inc(b_r, 1)

                def shared(a):
                    for m in range(KS):
                        if m < 2:
                            at_least(pe, b_fin, a.i * Q - Q + 2 * m + 2)
                        else:
                            pe.wait_ge(b_h, a.i * KS + m - 1)
                        columns(ps_w[m % 2 * 2][:], s13_hi, s13_lo, m * P, x_hi[a.buf(2)], x_lo[a.buf(2)])
                        columns(ps_w[m % 2 * 2 + 1][:], s13_hi, s13_lo, SF + m * P, x_hi[a.buf(2)],
                                x_lo[a.buf(2)]).then_inc(b_z, 1)

                def outputs(a):
                    pe.wait_ge(b_alo, a.i + 1)
                    pe.wait_ge(b_slo, a.i * KS + KS)
                    for q in range(Q):
                        cols = slice(q * P, (q + 1) * P)
                        bank_q = ps_w[q][:, 0:C]
                        for k in range(KC):
                            three_rows(bank_q, a_hi, a_lo, k, cols, o_hi, o_lo, k == 0, False)
                        for k in range(KS):
                            mm = three_rows(bank_q, s_hi, s_lo, k, cols, s2_hi, s2_lo, False, k == KS - 1)
                        mm.then_inc(b_o, 1)

                def three_rows(out, hi, lo, k, cols, w_hi, w_lo, start, stop):
                    nc.tensor.matmul(out, hi[:, k, cols], w_hi[:, k, :], start=start, stop=False)
                    nc.tensor.matmul(out, hi[:, k, cols], w_lo[:, k, :], start=False, stop=False)
                    return nc.tensor.matmul(out, lo[:, k, cols], w_hi[:, k, :], start=False, stop=stop)

                def step(a, first, left):
                    values(a)
                    if first:
                        pe.wait_ge(b_whi, 4)
                        pe.wait_ge(b_wlo, 4)
                    else:
                        outputs(a.plus(-1))
                    shared(a)

                pe.wait_ge(b_whi, 1)
                pe.wait_ge(b_wlo, 1)
                steps(pe, step)
                outputs(LAST)

            @block.scalar
            def _(act):
                def cut_x(a):
                    act.wait_ge(b_xT[a.buf(2)], (a.uses(2) + 1) * 16)
                    at_least(act, b_z, a.i * KS - KS)
                    nc.scalar.activation(x_hi[a.buf(2)][:], xT[a.buf(2)][:], ACT.Copy).then_inc(b_xhi, 1)

                def receive(a):
                    act.wait_ge(b_r, a.i + 1)
                    at_least(act, b_rw, a.i)
                    nc.scalar.activation(th[:].rearrange("p k b t -> p k (b t)"), ps_r[:], ACT.Tanh, scale=0.5
                                         ).then_inc(b_tanh, 1)

                def cut_a(a):
                    act.wait_ge(b_rw, a.i + 1)
                    at_least(act, b_o, a.i * Q)
                    nc.scalar.activation(a_hi[:], rw[:].rearrange("p k b t -> p k (b t)"), ACT.Copy
                                         ).then_inc(b_ahi, 1)

                def silu(a, m):
                    act.wait_ge(b_z, a.i * KS + m + 1)
                    at_least(act, b_h, a.i * KS + m - 1)
                    nc.scalar.activation(act1[m % 2][:], ps_w[m % 2 * 2][:], ACT.Silu, bias=vec_b1[:, m:m + 1]
                                         ).then_inc(b_silu, 1)

                def cut_s(a, m):
                    act.wait_ge(b_h, a.i * KS + m + 1)
                    at_least(act, b_o, a.i * Q)
                    nc.scalar.activation(s_hi[:, m, :], hid[m % 2][:], ACT.Copy).then_inc(b_shi, 1)

                def step(a, first, left):
                    receive(a)
                    if left > 0:
                        cut_x(a.plus(1))
                    cut_a(a)
                    silu(a, 0)
                    silu(a, 1)
                    for m in range(KS):
                        cut_s(a, m)
                        if m + 2 < KS:
                            silu(a, m + 2)

                cut_x(At(0, 0, 2))
                for raw, hi, lo in splits:
                    nc.scalar.activation(hi[:], raw[:], ACT.Copy).then_inc(b_whi, 1)
                steps(act, step)

            @block.vector
            def _(dve):
                def wide(ap):
                    return ap[:, :, None, :].broadcast_to([P, KC, B, TIMES])

                def time_mix(a):
                    own = OwnIn(dve, b_a, a, MIX)
                    tab = table[a.buf(2)]
                    v = ps_v[:].rearrange("p k (b t) -> p k b t", b=B)
                    dve.wait_ge(b_v, a.i + 1)
                    dve.wait_ge(b_tab[a.buf(2)], (a.uses(2) + 1) * 32)
                    own.mark(nc.vector.tensor_tensor(fed[:], v, wide(tab[:, 1]), ALU.mult))
                    own.mark(nc.vector.tensor_tensor(part_v[:], v, wide(tab[:, 3]), ALU.mult))
                    own.wait()
                    for c in range(KC):
                        for b in range(B):
                            ins = nc.vector.tensor_tensor_scan(
                                out=sa[:, c * B + b, 1:TIMES + 1], data0=tab[:, 0, c, :], data1=fed[:, c, b, :],
                                initial=sa[:, c * B + b, 0:1], op0=ALU.mult, op1=ALU.add)
                    own.link(ins)
                    own.link(nc.vector.tensor_tensor(
                        part_a[:], sa[:, :, 0:TIMES].rearrange("p (k b) t -> p k b t", k=KC), wide(tab[:, 2]),
                        ALU.mult))
                    own.mark(nc.vector.tensor_copy(sa[:, :, 0:1], sa[:, :, TIMES:TIMES + 1]))
                    own.link(nc.vector.tensor_tensor(part_a[:], part_a[:], part_v[:], ALU.add))
                    own.close()
                    dve.wait_ge(b_tanh, a.i + 1)
                    at_least(dve, b_ahi, a.i)
                    nc.vector.scalar_tensor_tensor(
                        out=rw[:].rearrange("p k b t -> p (k b t)"), in0=th[:].rearrange("p k b t -> p (k b t)"),
                        scalar=1.0, in1=part_a[:].rearrange("p k b t -> p (k b t)"), op0=ALU.add, op1=ALU.mult
                    ).then_inc(b_rw, 1)

                def sum_up(a):
                    buf = a.buf(2)
                    dve.wait_ge(b_xb, a.i + 1)
                    dve.wait_ge(b_gath[buf], (a.uses(2) + 1) * 16 * TOPK * Q)
                    own = OwnIn(dve, b_slot, a, TOPK)
                    for k in range(TOPK):
                        for q in range(Q):
                            ins = nc.vector.scalar_tensor_tensor(
                                out=res[buf][:, q, :], in0=yg[buf][:, k, q, :],
                                scalar=gates[:, k, ds(a.i * Q + q, 1)], in1=res[buf][:, q, :],
                                op0=ALU.mult, op1=ALU.add)
                        own.link(ins)
                    own.close()
                    for q in range(Q):
                        dve.wait_ge(b_o, a.i * Q + q + 1)
                        nc.vector.tensor_tensor(res[buf][:, q, :], ps_w[q][:, 0:C], res[buf][:, q, :], ALU.add
                                                ).then_inc(b_fin, 1)

                def cut_a(a):
                    dve.wait_ge(b_ahi, a.i + 1)
                    nc.vector.tensor_tensor(a_lo[:], rw[:].rearrange("p k b t -> p k (b t)"), a_hi[:].bitcast(F32),
                                            ALU.subtract).then_inc(b_alo, 1)

                def hidden(a, m):
                    dve.wait_ge(b_silu, a.i * KS + m + 1)
                    at_least(dve, b_shi, a.i * KS + m - 1)
                    at_least(dve, b_slo, a.i * KS + m - 1)
                    nc.vector.scalar_tensor_tensor(out=hid[m % 2][:], in0=ps_w[m % 2 * 2 + 1][:],
                                                   scalar=vec_b3[:, m:m + 1], in1=act1[m % 2][:],
                                                   op0=ALU.add, op1=ALU.mult).then_inc(b_h, 1)

                def cut_s(a, m):
                    dve.wait_ge(b_shi, a.i * KS + m + 1)
                    nc.vector.tensor_tensor(s_lo[:, m, :], hid[m % 2][:], s_hi[:, m, :].bitcast(F32), ALU.subtract
                                            ).then_inc(b_slo, 1)

                def step(a, first, left):
                    time_mix(a)
                    if not first:
                        sum_up(a.plus(-1))
                    cut_a(a)
                    hidden(a, 0)
                    hidden(a, 1)
                    for m in range(KS):
                        cut_s(a, m)
                        if m + 2 < KS:
                            hidden(a, m + 2)

                nc.vector.memset(sa[:, :, 0:1], 0.0)
                for n, (raw, hi, lo) in enumerate(splits):
                    dve.wait_ge(b_whi, n + 1)
                    nc.vector.tensor_tensor(lo[:], raw[:], hi[:].bitcast(F32), ALU.subtract).then_inc(b_wlo, 1)
                steps(dve, step)
                sum_up(LAST)


_OUT = (B, T, C)


def kernel(**inputs):
    import numpy as np
    import concourse.bacc as bacc
    from concourse.bass_utils import run_bass_kernel_spmd as run

    def get(name):
        return np.asarray(inputs[name])

    def cols(name):
        return np.swapaxes(get(name), -1, -2)

    def by_partition(a):
        a = a.reshape(-1, P, *a.shape[1:])
        return np.swapaxes(a, 0, 1)

    arrays = {
        "x": get("L0_attn_x"),
        "decay": by_partition(get("L0_attn_time_decay")),
        "first": by_partition(get("L0_attn_time_first")),
        "wvr": np.concatenate([cols("L0_attn_value_w"), cols("L0_attn_recep_w")], axis=1),
        "wo": cols("L0_attn_out_w"),
        "gate_w": by_partition(cols("L0_ffn_gate_w")),
        "gate_b": get("L0_ffn_gate_b"),
        "w_all": np.concatenate([cols("L0_ffn_w1"), cols("L0_ffn_w3"), cols("L0_ffn_w2")], axis=2),
        "b_all": np.concatenate([get("L0_ffn_b1"), get("L0_ffn_b3"), get("L0_ffn_b2")], axis=1).reshape(-1),
        "ws13": np.concatenate([cols("L0_ffn_ws1"), cols("L0_ffn_ws3")], axis=1),
        "bs1": by_partition(get("L0_ffn_bs1")),
        "bs3": by_partition(get("L0_ffn_bs3")),
        "ws2": cols("L0_ffn_ws2"),
        "bs2": get("L0_ffn_bs2"),
    }
    arrays = {k: np.ascontiguousarray(v) for k, v in arrays.items()}
    nc = bacc.Bacc("TRN2", target_bir_lowering=False, num_devices=1)
    args = [nc.dram_tensor(k, v.shape, mybir.dt.from_np(v.dtype), kind="ExternalInput").ap()
            for k, v in arrays.items()]
    out = nc.dram_tensor("out", _OUT, F32, kind="ExternalOutput").ap()
    build(nc, *args, out)
    r = run(nc, [arrays], core_ids=[0])
    return r.results[0]["out"]
```

```python
from contextlib import ExitStack

import concourse.bass as bass
from concourse import mybir

F32 = mybir.dt.float32
F32R = mybir.dt.float32r
BF16 = mybir.dt.bfloat16
I32 = mybir.dt.int32
ALU = mybir.AluOpType
ACT = mybir.ActivationFunctionType
AX_X = mybir.AxisListType.X
ds = bass.ds

P = 128
B, T, C = 2, 2048, 256
TOK = B * T
E, TOPK = 8, 2
FF, SF = 256, 512
KC = C // P
KS = SF // P
TIMES = 256
STEP = B * TIMES
NSTEP = T // TIMES
Q = STEP // P
NT = TOK // P
HALF = TIMES // P
WALL = 2 * FF + C
TILES = TOK * TOPK // P + E - 1
ROUNDS = -(-TILES // 4)
REST = TILES - 4 * (ROUNDS - 1)
EPS = 1e-5
PIECE = 128
NPIECE = T // PIECE
PAIRS = TOPK * NT
BATCH = 8


class At:

    def __init__(self, u, r, n):
        self.u, self.r, self.n = u, r, n

    def plus(self, d):
        q, r = divmod(self.r + d, self.n)
        return At(self.u + q if q else self.u, r, self.n)

    @property
    def i(self):
        return self.u * self.n + self.r

    def uses(self, bufs):
        assert self.n % bufs == 0
        return self.u * (self.n // bufs) + self.r // bufs

    def buf(self, bufs):
        return self.r % bufs


def at_least(eng, sem, value):
    if isinstance(value, int) and value <= 0:
        return
    eng.wait_ge(sem, value)


class Own:

    def __init__(self, eng, sem):
        self.eng, self.sem, self.n = eng, sem, 0

    def mark(self, ins):
        ins.then_inc(self.sem, 1)
        self.n += 1

    def wait(self):
        self.eng.wait_ge(self.sem, self.n)

    def link(self, ins):
        self.mark(ins)
        self.wait()


class OwnIn:

    def __init__(self, eng, sem, at, per, done=0):
        self.eng, self.sem, self.base, self.per, self.n = eng, sem, at.i * per + done, per, 0

    def mark(self, ins):
        ins.then_inc(self.sem, 1)
        self.n += 1

    def wait(self):
        self.eng.wait_ge(self.sem, self.base + self.n)

    def link(self, ins):
        self.mark(ins)
        self.wait()

    def close(self):
        assert self.n == self.per, (self.n, self.per)


def build(nc, x, decay, first, wvr, wo, gate_w, gate_b, w_all, b_all, ws13, bs1, bs3, ws2, bs2, out):
    xn_d = nc.dram_tensor("xn_rows", (TOK, C), F32, kind="Internal").ap()
    xT_d = nc.dram_tensor("xn_columns", (P, NSTEP, KC * STEP), F32, kind="Internal").ap()
    tab_d = nc.dram_tensor("mix_tables", (T // PIECE, P, 4, KC, PIECE), F32, kind="Internal").ap()
    y_d = nc.dram_tensor("expert_rows", (TILES * P, C), F32, kind="Internal").ap()

    with ExitStack() as kept:
        def sb(name, shape, dt, stack=kept):
            return stack.enter_context(nc.sbuf_tensor(name, shape, dt))

        ident = sb("ident", [P, P], F32)
        slots = sb("slots", [P, TOPK, NT], I32)
        gates = sb("gates", [P, TOPK, NT], F32)
        tile_tok = sb("tile_tok", [P, TILES], I32)
        tile_exp = sb("tile_exp", [P, TILES], I32)
        raw_s13 = sb("raw_s13", [P, KC, 2 * SF], F32)
        raw_s2 = sb("raw_s2", [P, KS, C], F32)
        raw_o = sb("raw_o", [P, KC, C], F32)
        vr_hi, vr_lo = (sb(f"vr_{s}", [P, KC, 2 * C], F32R) for s in ("hi", "lo"))
        col0 = sb("col0", [P, KC, STEP], F32)
        col_hi0 = sb("col_hi0", [P, KC, STEP], F32R)
        col_lo0 = sb("col_lo0", [P, KC, STEP], F32R)
        vec_tf = sb("vec_tf", [P, KC], F32)
        vec_td = sb("vec_td", [P, KC], F32)
        vec_b1 = sb("vec_b1", [P, KS], F32)
        vec_b3 = sb("vec_b3", [P, KS], F32)
        row_b2 = sb("row_b2", [P, C], F32)

        y_stored = [kept.enter_context(nc.semaphore(f"y_stored{b}")) for b in range(2)]

        with ExitStack() as experts:
            w_hi = sb("w_hi", [P, E, KC, WALL], F32R, experts)
            w_lo = sb("w_lo", [P, E, KC, WALL], F32R, experts)
            bias_hl = sb("bias_hl", [2, E, WALL], F32R, experts)
            ones2 = sb("ones2", [2, P], F32R, experts)
            raw_vr = sb("raw_vr", [P, KC, 2 * C], F32, experts)
            route(nc, x, first, decay, vec_tf, vec_td, gate_w, gate_b, w_all, b_all, xn_d, xT_d, ident, slots, gates,
                  tile_tok, tile_exp, w_hi, w_lo, bias_hl, ones2, raw_s13, raw_s2, raw_vr, col0)
            run_experts(nc, xn_d, y_d, y_stored, tab_d, vec_tf, vec_td, ident, tile_tok, tile_exp, w_hi, w_lo, bias_hl,
                        ones2,
                        [(raw_vr, vr_hi, vr_lo), (col0, col_hi0, col_lo0)],
                        [[(col0[:].rearrange("p k n -> p (k n)"), xT_d[:, 0, :]),
                          (vec_b1[:], bs1)],
                         [(raw_vr[:], wvr.rearrange("(k p) n -> p k n", p=P)),
                          (vec_b3[:], bs3)],
                         [(raw_s13[:], ws13.rearrange("(k p) n -> p k n", p=P))],
                         [(raw_o[:], wo.rearrange("(k p) n -> p k n", p=P)),
                          (raw_s2[:], ws2.rearrange("(k p) n -> p k n", p=P)),
                          (row_b2[:], bs2.rearrange("(a n) -> a n", a=1).broadcast_to([P, C]))]])
        mix(nc, x, xT_d, y_d, y_stored, tab_d, out, slots, gates, vr_hi, vr_lo, raw_s13, raw_o, raw_s2,
            col0, col_hi0, col_lo0, vec_b1, vec_b3, row_b2)


def route(nc, x, first, decay, vec_tf, vec_td, gate_w, gate_b, w_all, b_all, xn_d, xT_d, ident, slots, gates,
          tile_tok, tile_exp, w_hi, w_lo, bias_hl, ones2, spare_x, spare_n0, spare_n1, spare_t):
    with ExitStack() as ctx:
        def sb(name, shape, dt):
            return ctx.enter_context(nc.sbuf_tensor(name, shape, dt))

        def bank(name, shape):
            return ctx.enter_context(nc.psum_tensor(name, shape, F32))

        def sem(name):
            return ctx.enter_context(nc.semaphore(name))

        xin = [spare_x[:, b, :].rearrange("p (q c) -> p q c", q=Q) for b in range(2)]
        xn = [spare_n0, spare_n1[:].rearrange("p k n -> p (k n)").rearrange("p (q c) -> p q c", q=Q)]
        xT = [spare_t, sb("xT1", [P, KC, STEP], F32)]
        NW = 4
        w_raw = [t[:].rearrange("p k n -> p (k n)")[:, 0:WALL] for t in (spare_n0, spare_n1, *xT)]
        later = spare_x[:].rearrange("p k n -> p (k n)")
        maps = [later[:, n * NT * E:(n + 1) * NT * E] for n in range(7)]
        stats = [sb(f"stats{b}", [P, Q, 6], F32) for b in range(2)]
        mv = [sb(f"mv{b}", [P, Q, 2], F32) for b in range(2)]
        var = [sb(f"var{b}", [P, Q], F32) for b in range(2)]
        std = [sb(f"std{b}", [P, Q], F32) for b in range(2)]
        rstd = [sb(f"rstd{b}", [P, Q], F32) for b in range(2)]
        gw = sb("gw", [P, KC, E], F32)
        gb = sb("gb", [E, 1], F32)
        gated = [sb(f"gated{b}", [P, STEP], F32) for b in range(2)]
        BR = E * WALL // P
        b_raw = sb("b_raw", [P, BR], F32)
        b_hi = sb("b_hi", [P, BR], F32R)
        b_lo = sb("b_lo", [P, BR], F32R)
        ones_f = sb("ones_f", [P, P], F32)
        before_f = sb("before_f", [P, P], F32)
        ones = sb("ones", [P, P], BF16)
        before = sb("before", [P, P], BF16)
        lane_i = sb("lane_i", [P, P], I32)
        lane = sb("lane", [P, P], F32)
        desc_i = sb("desc_i", [P, E], I32)
        desc = sb("desc", [P, E], F32)
        logits = sb("logits", [P, NT, E], F32)
        score = maps[0].rearrange("p (j e) -> p j e", e=E)
        work = maps[1].rearrange("p (j e) -> p j e", e=E)
        work2 = maps[2].rearrange("p (j e) -> p j e", e=E)
        hot = [maps[3 + k].rearrange("p (j e) -> p j e", e=E) for k in range(TOPK)]
        red = sb("red", [P, NT], F32)
        red2 = sb("red2", [P, NT], F32)
        mask = sb("mask", [P, E, NT], BF16)
        keep = sb("keep", [P, E, NT], F32)
        filled = maps[5].rearrange("p (e j) -> p e j", e=E)
        place = maps[6].rearrange("p (e j) -> p e j", e=E)
        ntile_i = sb("ntile_i", [P, E], I32)
        ntile = sb("ntile", [P, E], F32)
        last = sb("last", [P, E], F32)
        start = sb("start", [P, E], F32)
        last_b = sb("last_b", [P, E], BF16)
        tile_no = sb("tile_no", [P, TILES, E], BF16)
        exp_f = sb("exp_f", [P, TILES], F32)
        slot_f = sb("slot_f", [P, PAIRS], F32)
        part_i = sb("part_i", [P, 2, PAIRS], I32)
        hot_in = [sb(f"hot_in{b}", [P, P, BATCH], BF16) for b in range(2)]
        hot_tile = [sb(f"hot_tile{b}", [P, TILES, BATCH], BF16) for b in range(2)]
        hot_tok = [sb(f"hot_tok{b}", [P, 2, TILES, BATCH], BF16) for b in range(2)]
        lane_b = sb("lane_b", [P, P, BATCH], BF16)
        part_b = sb("part_b", [P, 2, PAIRS], BF16)
        base_b = sb("base_b", [P, NT], BF16)
        base_i = sb("base_i", [P, NT], I32)
        row_i = sb("row_i", [P, 1], I32)
        row = sb("row", [P, 1], F32)
        tok_f = sb("tok_f", [P, TILES], F32)

        ps_T = [[bank(f"ps_T{b}{k}", [P, STEP]) for k in range(KC)] for b in range(2)]
        ps_L = [bank(f"ps_L{b}", [P, Q, P]) for b in range(2)]
        ps_G = [bank(f"ps_G{b}", [E, STEP]) for b in range(2)]
        ps_cnt = ps_T[0][0][:].rearrange("p (h n) -> p h n", h=2)
        ps_tok = ps_T[1][0][:, 0:2 * TILES].rearrange("p (h t) -> p h t", h=2)

        s_const = sem("s_const")
        s_pool = sem("s_pool")
        s_small = sem("s_small")
        s_xin = [sem(f"s_xin{b}") for b in range(2)]
        s_w = [sem(f"s_w{b}") for b in range(NW)]
        s_whi = sem("s_whi")
        s_wlo = sem("s_wlo")
        s_wlod = sem("s_wlod")
        s_stat = sem("s_stat")
        s_var = sem("s_var")
        s_go = sem("s_go")
        s_std = sem("s_std")
        s_xn = sem("s_xn")
        s_T = sem("s_T")
        s_xT = sem("s_xT")
        s_L = sem("s_L")
        s_Lg = sem("s_Lg")
        s_LT = sem("s_LT")
        s_Lc = sem("s_Lc")
        s_xout = [sem(f"s_xout{b}") for b in range(2)]
        s_Tout = [sem(f"s_Tout{b}") for b in range(2)]
        s_bhi = sem("s_bhi")
        s_blo = sem("s_blo")
        s_bias = sem("s_bias")
        s_dve = sem("s_dve")
        s_shift = sem("s_shift")
        s_exp = sem("s_exp")
        s_mask = sem("s_mask")
        s_cnt = sem("s_cnt")
        s_hott = sem("s_hott")
        s_hot = sem("s_hot")
        s_hotk = sem("s_hotk")
        s_hotd = sem("s_hotd")
        s_hotmm = sem("s_hotmm")
        s_tok = sem("s_tok")

        xv = x.rearrange("b (i h p) c -> i p b h c", h=HALF, p=P)
        xnv = xn_d.rearrange("(b i h p) c -> i p b h c", b=B, h=HALF, p=P)
        wv = w_all.rearrange("e (k p) n -> (e k) p n", p=P)
        BY_POOL = NW - 1
        EARLY = NSTEP - 3
        w_parts = [w[:].rearrange("p e k n -> p (e k) n") for w in (w_hi, w_lo)]

        with nc.Block() as block:

            @block.sync
            def _(sp):
                def load_x(a):
                    at_least(sp, s_xn, a.i - 1)
                    for b in range(B):
                        sp.dma_start(xin[a.buf(2)][:, b * HALF:(b + 1) * HALF, :],
                                     xv[ds(a.i, 1), :, b, :, :].rearrange("o p h c -> p (o h) c")
                                     ).then_inc(s_xin[a.buf(2)], 16)

                def load_w(a):
                    if a.buf(NW) < BY_POOL:
                        at_least(sp, s_wlo, a.u * BY_POOL + (a.r + 1 - BY_POOL))
                    else:
                        at_least(sp, s_wlod, a.u)
                    sp.dma_start(w_raw[a.buf(NW)], wv[ds(a.i, 1)].rearrange("o p n -> p (o n)")
                                 ).then_inc(s_w[a.buf(NW)], 16)

                load_x(At(0, 0, 2))
                sp.dma_start(gw[:], gate_w).then_inc(s_small, 16)
                sp.dma_start(gb[:], gate_b.rearrange("(n a) -> n a", a=1)).then_inc(s_small, 16)
                sp.dma_start(vec_tf[:], first).then_inc(s_small, 16)
                sp.dma_start(vec_td[:], decay).then_inc(s_small, 16)
                sp.dma_start(b_raw[:], b_all.rearrange("(p r) -> p r", p=P)).then_inc(s_small, 16)
                load_x(At(0, 1, 2))

                def step(a, more=True):
                    at_least(sp, s_xn, a.i + 1)
                    if more:
                        load_x(a.plus(2))
                    for b in range(B):
                        sp.dma_start(xnv[ds(a.i, 1), :, b, :, :].rearrange("o p h c -> p (o h) c"),
                                     xn[a.buf(2)][:, b * HALF:(b + 1) * HALF, :]
                                     ).then_inc(s_xout[a.buf(2)], 16)
                    at_least(sp, s_xT, a.i + 1)
                    sp.dma_start(xT_d[:, ds(a.i, 1), :].rearrange("p o n -> p (o n)"),
                                 xT[a.buf(2)][:].rearrange("p k n -> p (k n)")
                                 ).then_inc(s_Tout[a.buf(2)], 16)

                step(At(0, 0, 2))
                step(At(0, 1, 2))
                with sp.Fori(1, NSTEP // 2 - 1) as u:
                    step(At(u, 0, 2))
                    step(At(u, 1, 2))
                step(At(NSTEP // 2 - 1, 0, 2), False)
                step(At(NSTEP // 2 - 1, 1, 2), False)
                sp.wait_ge(s_T, NSTEP)
                for b in range(2):
                    sp.wait_ge(s_xout[b], NSTEP // 2 * 32)
                    load_w(At(0, b, NW))
                sp.wait_ge(s_L, NSTEP)
                for b in range(2):
                    sp.wait_ge(s_Tout[b], NSTEP // 2 * 16)
                    load_w(At(0, 2 + b, NW))
                with sp.Fori(1, E * KC // NW) as u:
                    for r in range(NW):
                        load_w(At(u, r, NW))

                sp.wait_ge(s_bhi, 1)
                sp.wait_ge(s_blo, 1)
                bias = bias_hl[:].rearrange("h e n -> h (e n)").bitcast(F32)
                sp.dma_start(bias[0:1, :].rearrange("o (p r) -> o p r", p=P), b_hi[:].bitcast(F32)).then_inc(s_bias, 16)
                sp.dma_start(bias[1:2, :].rearrange("o (p r) -> o p r", p=P), b_lo[:].bitcast(F32)).then_inc(s_bias, 16)
                sp.wait_ge(s_bias, 32)

            @block.gpsimd
            def _(pool):
                own = Own(pool, s_pool)
                nc.gpsimd.memset(ones_f[:], 1.0).then_inc(s_pool, 1)
                own.n += 1
                own.mark(nc.gpsimd.memset(ident[:], 0.0))
                own.wait()
                nc.gpsimd.affine_select(out=ident[:], in_=ident[:], compare_op=ALU.not_equal, fill=1.0,
                                        base=0, pattern=[[-1, P]], channel_multiplier=1).then_inc(s_const, 1)
                nc.gpsimd.affine_select(out=before_f[:], in_=ones_f[:], compare_op=ALU.is_gt, fill=0.0,
                                        base=0, pattern=[[1, P]], channel_multiplier=-1).then_inc(s_const, 1)
                nc.gpsimd.iota(lane_i[:], pattern=[[1, P]], base=0, channel_multiplier=0).then_inc(s_const, 1)
                nc.gpsimd.iota(base_i[:].rearrange("p (i b h) -> p i b h", b=B, h=HALF),
                               pattern=[[TIMES, NSTEP], [T, B], [P, HALF]], base=0,
                               channel_multiplier=0).then_inc(s_const, 1)
                nc.gpsimd.iota(row_i[:], pattern=[[0, 1]], base=0, channel_multiplier=1).then_inc(s_const, 1)
                nc.gpsimd.iota(desc_i[:], pattern=[[-1, E]], base=E, channel_multiplier=0).then_inc(s_const, 1)

                for b in range(2):
                    nc.gpsimd.memset(gated[b][:], 0.0).then_inc(s_const, 1)

                def split(a):
                    pool.wait_ge(s_whi, a.i + 1)
                    hi, lo = (w[:, ds(a.i, 1), :].rearrange("p o n -> p (o n)") for w in w_parts)
                    nc.gpsimd.tensor_tensor(lo, w_raw[a.buf(NW)], hi.bitcast(F32), ALU.subtract).then_inc(s_wlo, 1)

                with pool.Fori(0, E * KC // NW) as u:
                    for r in range(BY_POOL):
                        split(At(u, r, NW))
            @block.scalar
            def _(act):
                def root(a):
                    act.wait_ge(s_var, a.i + 1)
                    nc.scalar.activation(std[a.buf(2)][:], var[a.buf(2)][:], ACT.Sqrt).then_inc(s_std, 1)

                def logit(a):
                    act.wait_ge(s_L, a.i + 1)
                    at_least(act, s_LT, a.i - 1)
                    nc.scalar.activation(gated[a.buf(2)][0:E, :], ps_G[a.buf(2)][:], ACT.Identity, bias=gb[:]
                                         ).then_inc(s_Lg, 1)

                def step(a, more=True, first=False):
                    if more:
                        root(a.plus(1))
                    act.wait_ge(s_T, a.i + 1)
                    at_least(act, s_Tout[a.buf(2)], a.uses(2) * 16)
                    at_least(act, s_L, a.i - 1)
                    nc.scalar.activation(xT[a.buf(2)][:, 0, :], ps_T[a.buf(2)][0][:], ACT.Copy)
                    nc.scalar.activation(xT[a.buf(2)][:, 1, :], ps_T[a.buf(2)][1][:], ACT.Copy
                                         ).then_inc(s_xT, 1)
                    if not first:
                        logit(a.plus(-1))

                def split(a):
                    act.wait_ge(s_w[a.buf(NW)], (a.uses(NW) + 1) * 16)
                    nc.scalar.activation(w_parts[0][:, ds(a.i, 1), :].rearrange("p o n -> p (o n)"),
                                         w_raw[a.buf(NW)], ACT.Copy).then_inc(s_whi, 1)

                act.wait_ge(s_small, 80)
                act.wait_ge(s_const, 8)
                root(At(0, 0, 2))
                step(At(0, 0, 2), first=True)
                step(At(0, 1, 2))
                with act.Fori(1, NSTEP // 2 - 1) as u:
                    step(At(u, 0, 2))
                    step(At(u, 1, 2))
                def exps(n, first_step, last_step):
                    t = slice(first_step * Q, last_step * Q)
                    act.wait_ge(s_shift, n + 1)
                    nc.scalar.activation(score[:, t], work[:, t], ACT.Exp).then_inc(s_exp, 1)

                step(At(NSTEP // 2 - 1, 0, 2))
                exps(0, 0, EARLY)
                step(At(NSTEP // 2 - 1, 1, 2), False)
                logit(At(NSTEP // 2 - 1, 1, 2))
                exps(1, EARLY, NSTEP)
                half = E * KC // 2
                for n in range(half):
                    split(At(0, n, half))
                for n in range(PAIRS // BATCH):
                    if n < half:
                        split(At(1, n, half))
                    act.wait_ge(s_hott, n + 1)
                    if n >= 2:
                        act.wait_ge(s_hotmm, n - 1)
                    nc.scalar.activation(hot_tok[n % 2][:, 0], hot_tile[n % 2][:], ACT.Copy, scale=row[:]
                                         ).then_inc(s_hotk, 1)
                assert half == PAIRS // BATCH

            @block.tensor
            def _(pe):
                def turn(a):
                    pe.wait_ge(s_xn, a.i + 1)
                    at_least(pe, s_xT, a.i - 1)
                    for k in range(KC):
                        for q in range(Q):
                            mm = nc.tensor.transpose(ps_T[a.buf(2)][k][:, q * P:(q + 1) * P],
                                                     xn[a.buf(2)][:, q, k * P:(k + 1) * P], ident[:])
                    mm.then_inc(s_T, 1)

                def gate(a):
                    pe.wait_ge(s_xT, a.i + 1)
                    at_least(pe, s_Lg, a.i - 1)
                    for k in range(KC):
                        mm = nc.tensor.matmul(ps_G[a.buf(2)][:], gw[:, k, :], xT[a.buf(2)][:, k, :],
                                              start=(k == 0), stop=(k == KC - 1))
                    mm.then_inc(s_L, 1)

                def back(a):
                    pe.wait_ge(s_Lg, a.i + 1)
                    at_least(pe, s_Lc, a.i - 1)
                    for q in range(Q):
                        mm = nc.tensor.transpose(ps_L[a.buf(2)][:, q, :], gated[a.buf(2)][:, q * P:(q + 1) * P],
                                                 ident[:])
                    mm.then_inc(s_LT, 1)

                pe.wait_ge(s_const, 6)
                pe.wait_ge(s_small, 80)
                turn(At(0, 0, 2))
                turn(At(0, 1, 2))
                gate(At(0, 0, 2))
                turn(At(1, 0, 2))
                gate(At(0, 1, 2))
                back(At(0, 0, 2))
                turn(At(1, 1, 2))
                gate(At(1, 0, 2))
                back(At(0, 1, 2))
                with pe.Fori(2, NSTEP // 2) as u:
                    turn(At(u, 0, 2))
                    gate(At(u - 1, 1, 2))
                    back(At(u - 1, 0, 2))
                    turn(At(u, 1, 2))
                    gate(At(u, 0, 2))
                    back(At(u - 1, 1, 2))
                gate(At(NSTEP // 2 - 1, 1, 2))
                back(At(NSTEP // 2 - 1, 0, 2))
                back(At(NSTEP // 2 - 1, 1, 2))

                pe.wait_ge(s_mask, 3)
                nc.tensor.matmul(ps_cnt[:, 0, :], before[:], mask[:].rearrange("p e j -> p (e j)"),
                                 start=True, stop=True)
                nc.tensor.matmul(ps_cnt[:, 1, :], ones[:], mask[:].rearrange("p e j -> p (e j)"),
                                 start=True, stop=True).then_inc(s_cnt, 1)
                for n in range(PAIRS // BATCH):
                    pe.wait_ge(s_hot, n + 1)
                    pe.wait_ge(s_hotk, n + 1)
                    pe.wait_ge(s_hotd, n + 1)
                    for g in range(BATCH):
                        mm = nc.tensor.matmul(ps_tok.rearrange("p h t -> p (h t)"), hot_in[n % 2][:, :, g],
                                              hot_tok[n % 2][:, :, :, g].rearrange("p h t -> p (h t)"),
                                              start=(n == 0 and g == 0),
                                              stop=(n == PAIRS // BATCH - 1 and g == BATCH - 1))
                    mm.then_inc(s_hotmm, 1)

            @block.vector
            def _(dve):
                dve.wait_ge(s_const, 6)
                nc.vector.tensor_copy(lane[:], lane_i[:])
                nc.vector.tensor_copy(lane_b[:], lane_i[:, :, None].broadcast_to([P, P, BATCH]))
                nc.vector.tensor_copy(base_b[:], base_i[:])
                nc.vector.tensor_copy(row[:], row_i[:])
                nc.vector.tensor_copy(desc[:], desc_i[:])
                nc.vector.tensor_copy(ones[:], ones_f[:])
                nc.vector.tensor_copy(ones2[:], ones_f[0:2, :])
                nc.vector.memset(keep[:], 1.0)
                nc.vector.tensor_copy(before[:], before_f[:]).then_inc(s_mask, 1)
                dve.wait_ge(s_mask, 1)
                nc.vector.memset(keep[:, :, 0:1], 0.0)
                PER = 2

                def measure(a):
                    own = OwnIn(dve, s_stat, a, PER)
                    dve.wait_ge(s_xin[a.buf(2)], (a.uses(2) + 1) * 32)
                    for q in range(Q):
                        ins = nc.vector.bn_stats(stats[a.buf(2)][:, q, :], xin[a.buf(2)][:, q, :])
                    own.link(ins)
                    dve.sem_inc(s_go, 1)
                    for q in range(Q):
                        ins = nc.vector.bn_aggr(mv[a.buf(2)][:, q, :], stats[a.buf(2)][:, q, :])
                    own.link(ins)
                    own.close()
                    at_least(dve, s_std, a.i - 1)
                    nc.vector.tensor_scalar(var[a.buf(2)][:], mv[a.buf(2)][:, :, 1], EPS, None, ALU.add
                                            ).then_inc(s_var, 1)

                def norm(a):
                    own = OwnIn(dve, s_dve, a, 1)
                    dve.wait_ge(s_std, a.i + 1)
                    own.link(nc.vector.reciprocal(rstd[a.buf(2)][:], std[a.buf(2)][:]))
                    own.close()
                    at_least(dve, s_T, a.i - 1)
                    at_least(dve, s_xout[a.buf(2)], a.uses(2) * 32)
                    for q in range(Q):
                        ins = nc.vector.tensor_scalar(xn[a.buf(2)][:, q, :], xin[a.buf(2)][:, q, :],
                                                      mv[a.buf(2)][:, q, 0:1], rstd[a.buf(2)][:, q:q + 1],
                                                      ALU.subtract, ALU.mult)
                    ins.then_inc(s_xn, 1)

                def take(a):
                    dve.wait_ge(s_LT, a.i + 1)
                    nc.vector.tensor_copy(logits[:, ds(a.i * Q, Q), :], ps_L[a.buf(2)][:, :, 0:E]).then_inc(s_Lc, 1)

                dve.wait_ge(s_small, 80)
                nc.vector.tensor_copy(b_hi[:], b_raw[:]).then_inc(s_bhi, 1)
                dve.wait_ge(s_bhi, 1)
                nc.vector.tensor_tensor(b_lo[:], b_raw[:], b_hi[:].bitcast(F32), ALU.subtract).then_inc(s_blo, 1)
                measure(At(0, 0, 2))
                norm(At(0, 0, 2))
                measure(At(0, 1, 2))
                norm(At(0, 1, 2))
                measure(At(1, 0, 2))
                norm(At(1, 0, 2))
                measure(At(1, 1, 2))
                norm(At(1, 1, 2))
                take(At(0, 0, 2))
                measure(At(2, 0, 2))
                with dve.Fori(2, NSTEP // 2 - 1) as u:
                    norm(At(u, 0, 2))
                    take(At(u - 2, 1, 2))
                    measure(At(u, 1, 2))
                    norm(At(u, 1, 2))
                    take(At(u - 1, 0, 2))
                    measure(At(u + 1, 0, 2))
                L = NSTEP // 2 - 1
                norm(At(L, 0, 2))
                take(At(L - 2, 1, 2))
                measure(At(L, 1, 2))
                norm(At(L, 1, 2))
                take(At(L - 1, 0, 2))

                own = Own(dve, s_dve)
                own.n = NSTEP
                def choose(n, first_step, last_step):
                    t = slice(first_step * Q, last_step * Q)
                    count = (last_step - first_step) * Q

                    def wide(ap):
                        return ap[:, :, None].broadcast_to([P, count, E])

                    dve.wait_ge(s_Lc, last_step)
                    own.link(nc.vector.tensor_reduce(red[:, t], logits[:, t], AX_X, ALU.max))
                    nc.vector.tensor_tensor(work[:, t], logits[:, t], wide(red[:, t]), ALU.subtract
                                            ).then_inc(s_shift, 1)
                    dve.wait_ge(s_exp, n + 1)
                    own.link(nc.vector.tensor_reduce(red[:, t], score[:, t], AX_X, ALU.add))
                    own.link(nc.vector.reciprocal(red2[:, t], red[:, t]))
                    own.link(nc.vector.tensor_tensor(score[:, t], score[:, t], wide(red2[:, t]), ALU.mult))
                    cur = score
                    for k in range(TOPK):
                        own.link(nc.vector.tensor_reduce(gates[:, k, t], cur[:, t], AX_X, ALU.max))
                        own.link(nc.vector.tensor_tensor(work2[:, t], cur[:, t], wide(gates[:, k, t]), ALU.is_equal))
                        own.link(nc.vector.tensor_tensor(work2[:, t], work2[:, t],
                                                         desc[:, None, :].broadcast_to([P, count, E]), ALU.mult))
                        own.link(nc.vector.tensor_reduce(red[:, t], work2[:, t], AX_X, ALU.max))
                        own.link(nc.vector.tensor_tensor(hot[k][:, t], work2[:, t], wide(red[:, t]), ALU.is_equal))
                        if k == 0:
                            own.link(nc.vector.scalar_tensor_tensor(out=work[:, t], in0=hot[0][:, t], scalar=-2.0,
                                                                    in1=score[:, t], op0=ALU.mult, op1=ALU.add))
                            cur = work
                    nc.vector.tensor_tensor(mask[:].rearrange("p e j -> p j e")[:, t], hot[0][:, t], hot[1][:, t],
                                            ALU.add).then_inc(s_mask, 1)

                dve.wait_ge(s_xn, NSTEP)
                choose(0, 0, EARLY)
                for n in range(EARLY, NSTEP):
                    take(At(n // 2, n % 2, 2))
                choose(1, EARLY, NSTEP)
                def split(u):
                    i = NW * u + BY_POOL
                    dve.wait_ge(s_whi, i + 1)
                    hi, lo = (w[:, i, :] for w in w_parts)
                    nc.vector.tensor_tensor(lo, w_raw[BY_POOL], hi.bitcast(F32), ALU.subtract).then_inc(s_wlod, 1)

                SPLIT_AFTER = {0: 1, 3: 2, PAIRS // BATCH - 1: 3}
                split(0)
                dve.wait_ge(s_cnt, 1)
                total = ps_cnt[:, 1, :].rearrange("p (e j) -> p e j", e=E)
                prefix = ps_cnt[:, 0, :].rearrange("p (e j) -> p e j", e=E)
                own.link(nc.vector.tensor_tensor_scan(out=filled[:].rearrange("p e j -> p (e j)"),
                                                      data0=keep[:].rearrange("p e j -> p (e j)"),
                                                      data1=ps_cnt[:, 1, :], initial=0.0,
                                                      op0=ALU.mult, op1=ALU.add))
                own.link(nc.vector.tensor_tensor(place[:], filled[:], total, ALU.subtract))
                own.link(nc.vector.tensor_tensor(place[:], place[:], prefix, ALU.add))
                own.link(nc.vector.tensor_scalar(ntile_i[:], filled[:, :, NT - 1], float(P - 1), None, ALU.add))
                own.link(nc.vector.tensor_scalar(ntile_i[:], ntile_i[:], 7, None, ALU.arith_shift_right))
                own.link(nc.vector.tensor_copy(ntile[:], ntile_i[:]))
                own.link(nc.vector.tensor_tensor_scan(out=last[:], data0=ones_f[:, 0:E], data1=ntile[:],
                                                      initial=0.0, op0=ALU.mult, op1=ALU.add))
                nc.vector.tensor_copy(last_b[:], last[:])
                own.link(nc.vector.tensor_tensor(start[:], last[:], ntile[:], ALU.subtract))
                own.link(nc.vector.scalar_tensor_tensor(out=place[:], in0=start[:, :, None].broadcast_to([P, E, NT]),
                                                        scalar=float(P), in1=place[:], op0=ALU.mult, op1=ALU.add))
                for k in range(TOPK):
                    own.link(nc.vector.tensor_tensor(work2[:], hot[k][:], place[:].rearrange("p e j -> p j e"),
                                                     ALU.mult))
                    own.link(nc.vector.tensor_reduce(slot_f[:, k * NT:(k + 1) * NT], work2[:], AX_X, ALU.add))
                own.link(nc.vector.tensor_scalar(slot_f[:], slot_f[:], 0.0, float(TILES * P - 1), ALU.max, ALU.min))
                own.link(nc.vector.tensor_copy(slots[:].rearrange("p k j -> p (k j)"), slot_f[:]))
                own.mark(nc.vector.tensor_scalar(part_i[:, 0, :], slots[:].rearrange("p k j -> p (k j)"), 7, None,
                                                 ALU.arith_shift_right))
                own.link(nc.vector.tensor_scalar(part_i[:, 1, :], slots[:].rearrange("p k j -> p (k j)"), P - 1, None,
                                                 ALU.bitwise_and))
                own.link(nc.vector.tensor_copy(part_b[:], part_i[:]))
                for n in range(PAIRS // BATCH):
                    sl = slice(n * BATCH, (n + 1) * BATCH)
                    if n >= 2:
                        dve.wait_ge(s_hotk, n - 1)
                        dve.wait_ge(s_hotd, n - 1)
                    nc.vector.tensor_tensor(hot_tile[n % 2][:],
                                            part_b[:, 0, sl][:, None, :].broadcast_to([P, TILES, BATCH]),
                                            lane_b[:, 0:TILES, :], ALU.is_equal).then_inc(s_hott, 1)
                    if n == 3:
                        own.mark(nc.vector.tensor_tensor(
                            tile_no[:, :, 0:E - 1], lane_b[:, 0:TILES, 0:E - 1],
                            last_b[:, None, 0:E - 1].broadcast_to([P, TILES, E - 1]), ALU.is_ge))
                    if n == 4:
                        own.wait()
                        own.mark(nc.vector.tensor_reduce(exp_f[:], tile_no[:, :, 0:E - 1], AX_X, ALU.add))
                    if n == 5:
                        own.wait()
                        nc.vector.tensor_copy(tile_exp[:], exp_f[:])
                    if n >= 2:
                        dve.wait_ge(s_hotmm, n - 1)
                    nc.vector.tensor_tensor(hot_in[n % 2][:], part_b[:, 1, sl][:, None, :].broadcast_to([P, P, BATCH]),
                                            lane_b[:], ALU.is_equal).then_inc(s_hot, 1)
                    dve.wait_ge(s_hott, n + 1)
                    tj = n * BATCH % NT
                    nc.vector.tensor_tensor(hot_tok[n % 2][:, 1], hot_tile[n % 2][:],
                                            base_b[:, tj:tj + BATCH][:, None, :].broadcast_to([P, TILES, BATCH]),
                                            ALU.mult).then_inc(s_hotd, 1)
                    if n in SPLIT_AFTER:
                        split(SPLIT_AFTER[n])
                dve.wait_ge(s_hotmm, PAIRS // BATCH)
                own.link(nc.vector.tensor_copy(tok_f[:], ps_tok[:, 0, :]))
                own.link(nc.vector.tensor_tensor(tok_f[:], ps_tok[:, 1, :], tok_f[:], ALU.add))
                nc.vector.tensor_scalar(tile_tok[:], tok_f[:], 0.0, float(TOK - 1), ALU.max, ALU.min
                                        ).then_inc(s_tok, 1)


def run_experts(nc, xn_d, y_d, y_stored, tab_d, vec_tf, vec_td, ident, tile_tok, tile_exp, w_hi, w_lo, bias_hl, ones2,
                cuts, loads):
    with ExitStack() as ctx:
        def sb(name, shape, dt):
            return ctx.enter_context(nc.sbuf_tensor(name, shape, dt))

        def bank(name, shape):
            return ctx.enter_context(nc.psum_tensor(name, shape, F32))

        def sem(name):
            return ctx.enter_context(nc.semaphore(name))

        NG = 4
        picked = [sb(f"picked{b}", [P, 1], I32) for b in range(NG)]
        xg = [sb(f"xg{b}", [P, C], F32) for b in range(NG)]
        x_hi = [sb(f"x_hi{b}", [P, KC, P], F32R) for b in range(2)]
        x_lo = [sb(f"x_lo{b}", [P, KC, P], F32R) for b in range(2)]
        act1 = [sb(f"act1{b}", [P, FF], F32) for b in range(2)]
        hid = [sb(f"hid{b}", [P, FF], F32) for b in range(2)]
        h_hi = [sb(f"h_hi{b}", [P, KC, P], F32R) for b in range(2)]
        h_lo = [sb(f"h_lo{b}", [P, KC, P], F32R) for b in range(2)]
        y = [sb(f"y{b}", [P, C], F32) for b in range(2)]
        s_p = sb("s_p", [P, KC, PIECE + 1], F32)
        s_b = sb("s_b", [P, KC, PIECE + 1], F32)
        grow = sb("grow", [P, KC], F32)
        zero = sb("zero", [P, 1], F32)
        dif = sb("dif", [P, 2, KC, PIECE], F32)
        sides = sb("sides", [P, 2, 2, KC, PIECE], F32)
        decays = sb("decays", [P, 2, 2, KC, PIECE], F32)
        den = sb("den", [P, KC, PIECE], F32)
        rden = sb("rden", [P, KC, PIECE], F32)
        coef = sb("coef", [P, 2, KC, PIECE], F32)
        ps_x = [bank(f"ps_x{b}", [P, KC, P]) for b in range(2)]
        ps_g = [bank(f"ps_g{b}", [P, 2 * FF]) for b in range(2)]
        ps_h = [bank(f"ps_h{b}", [P, KC, P]) for b in range(2)]
        ps_y = [bank(f"ps_y{b}", [P, C]) for b in range(2)]

        c_idx = sem("c_idx")
        c_go = sem("c_go")
        c_gath = [sem(f"c_gath{b}") for b in range(NG)]
        c_tx = sem("c_tx")
        c_xhi = sem("c_xhi")
        c_xlo = sem("c_xlo")
        c_g = sem("c_g")
        c_silu = sem("c_silu")
        c_h = sem("c_h")
        c_th = sem("c_th")
        c_hhi = sem("c_hhi")
        c_hlo = sem("c_hlo")
        c_y = sem("c_y")
        c_yc = sem("c_yc")
        c_ld = sem("c_ld")
        c_whi = sem("c_whi")
        c_wlo = sem("c_wlo")
        t_own = sem("t_own")
        t_pool = sem("t_pool")
        t_dif = sem("t_dif")
        t_carry = sem("t_carry")
        t_sides = sem("t_sides")
        c_gate = sem("c_gate")
        t_exp = sem("t_exp")
        t_exp_f = sem("t_exp_f")
        t_bb = sem("t_bb")
        t_den = sem("t_den")
        t_rec = sem("t_rec")
        t_coef = sem("t_coef")
        t_est = sem("t_est")
        t_cst = sem("t_cst")

        with nc.Block() as block:

            @block.sync
            def _(sp):
                def store(a):
                    sp.wait_ge(c_yc, a.i + 1)
                    sp.dma_start(y_d[ds(a.i * P, P), :], y[a.buf(2)][:]).then_inc(y_stored[a.buf(2)], 16)

                def store_table(v, kinds, src, sem_):
                    sp.dma_start(tab_d[ds(v, 1), :, kinds].rearrange("o p n k t -> p (o n) (k t)"),
                                 src.rearrange("p n k t -> p n (k t)")).then_inc(sem_, 16)

                for r in range(4):
                    store(At(0, r, 4))
                    for dst, src in loads[r]:
                        sp.dma_start(dst, src).then_inc(c_ld, 16)
                with sp.Fori(1, ROUNDS - 1) as u:
                    v = u - 1
                    store(At(u, 0, 4))
                    sp.wait_ge(t_exp, u)
                    store_table(v, slice(0, 2), decays[:, 1], t_est)
                    store(At(u, 1, 4))
                    store(At(u, 2, 4))
                    store(At(u, 3, 4))
                    sp.wait_ge(t_coef, u)
                    store_table(v, slice(2, 4), coef[:], t_cst)
                for r in range(REST):
                    store(At(ROUNDS - 1, r, 4))
                sp.wait_ge(t_est, NPIECE * 16)
                sp.wait_ge(t_cst, NPIECE * 16)

            @block.gpsimd
            def _(pool):
                def gather(a):
                    at_least(pool, c_tx, a.i - NG + 1)
                    nc.gpsimd.tensor_copy(picked[a.buf(NG)][:], tile_tok[:, ds(a.i, 1)]).then_inc(c_idx, 1)
                    pool.wait_ge(c_idx, a.i + 1)
                    pool.sem_inc(c_go, 1)
                    pool.indirect_dma_start(
                        out=xg[a.buf(NG)][:], out_offset=None, in_=xn_d[:, :],
                        in_offset=bass.IndirectOffsetOnAxis(ap=picked[a.buf(NG)][:, 0:1], axis=0)
                    ).then_inc(c_gath[a.buf(NG)], 16)

                def denominator(u):
                    own = OwnIn(pool, t_pool, At(u - 1, 0, 1), 2)
                    pool.wait_ge(t_bb, u)
                    pool.wait_ge(t_exp_f, u)
                    own.link(nc.gpsimd.tensor_tensor(den[:], decays[:, 0, 0], s_b[:, :, 0:PIECE], ALU.mult))
                    own.link(nc.gpsimd.tensor_tensor(den[:], den[:], decays[:, 0, 1], ALU.add))
                    own.close()
                    pool.sem_inc(c_go, 1)
                    nc.gpsimd.tensor_scalar(den[:], den[:], 1e-6, 2.0, ALU.add, ALU.mult).then_inc(t_den, 1)

                def factors(u):
                    pool.wait_ge(t_rec, u)
                    if not isinstance(u, int) or u > 1:
                        pool.wait_ge(t_cst, u * 16 - 16)
                    nc.gpsimd.tensor_tensor(coef[:], decays[:, 0], rden[:, None].broadcast_to([P, 2, KC, PIECE]),
                                            ALU.mult).then_inc(t_coef, 1)

                def turn(v, first=False, count=4):
                    gather(At(v, 0, 4))
                    if not first:
                        factors(v - 2)
                    for r in range(1, count):
                        gather(At(v, r, 4))
                    denominator(v - 1)

                for r in range(8):
                    gather(At(r // 4, r % 4, 4))
                turn(2, first=True)
                turn(3)
                with pool.Fori(4, ROUNDS - 1) as v:
                    turn(v)
                turn(ROUNDS - 1, count=REST)
                factors(NPIECE)
                for n, (raw, hi, lo) in enumerate(cuts):
                    pool.wait_ge(c_whi, n + 1)
                    nc.gpsimd.tensor_tensor(lo[:], raw[:], hi[:].bitcast(F32), ALU.subtract).then_inc(c_wlo, 1)

            @block.tensor
            def _(pe):
                def turn_x(a):
                    pe.wait_ge(c_gath[a.buf(NG)], (a.uses(NG) + 1) * 16)
                    at_least(pe, c_xlo, a.i - 1)
                    for k in range(KC):
                        mm = nc.tensor.transpose(ps_x[a.buf(2)][:, k, :], xg[a.buf(NG)][:, k * P:(k + 1) * P],
                                                 ident[:])
                    mm.then_inc(c_tx, 1)

                def experts(u, first, last):
                    _, values = nc.values_load_multi_w_load_instructions(
                        tile_exp[0:1, ds(At(u, 0, 8).plus(first).i, last + 1 - first)],
                        engines=[mybir.EngineType.PE], min_val=0, max_val=E - 1)
                    return dict(zip(range(first, last + 1), values))

                def three(out, hi, lo, e, cols):
                    for k in range(KC):
                        for n, (x, w) in enumerate([(hi, w_hi), (hi, w_lo), (lo, w_hi)]):
                            nc.tensor.matmul(out, x[:, k, :],
                                             w[:, ds(e, 1), k, cols].rearrange("p o n -> p (o n)"),
                                             start=(k == 0 and n == 0), stop=False)
                    return nc.tensor.matmul(out, ones2[:],
                                            bias_hl[:, ds(e, 1), cols].rearrange("p o n -> p (o n)"),
                                            start=False, stop=True)

                def up(a, e):
                    pe.wait_ge(c_xlo, a.i + 1)
                    at_least(pe, c_h, a.i - 1)
                    three(ps_g[a.buf(2)][:], x_hi[a.buf(2)], x_lo[a.buf(2)], e, slice(0, 2 * FF)).then_inc(c_g, 1)

                def turn_h(a):
                    pe.wait_ge(c_h, a.i + 1)
                    at_least(pe, c_hlo, a.i - 1)
                    for k in range(KC):
                        mm = nc.tensor.transpose(ps_h[a.buf(2)][:, k, :], hid[a.buf(2)][:, k * P:(k + 1) * P],
                                                 ident[:])
                    mm.then_inc(c_th, 1)

                def down(a, e):
                    pe.wait_ge(c_hlo, a.i + 1)
                    at_least(pe, c_yc, a.i - 1)
                    three(ps_y[a.buf(2)][:], h_hi[a.buf(2)], h_lo[a.buf(2)], e, slice(2 * FF, WALL)).then_inc(c_y, 1)

                LAST = (TILES - 1) // 8
                COUNT = TILES - 8 * LAST
                NUMBERS = {0: (-1, 2), 1: (3, 3), 2: (4, 5), 4: (6, 7), 6: (8, 9)}

                def turn(u, first=False, last=False):
                    es = {}
                    count = COUNT if last else 8
                    for r in range(count):
                        a = At(u, r, 8)
                        if r in NUMBERS:
                            lo, hi = NUMBERS[r]
                            lo, hi = max(lo, 0) if first else lo, min(hi, count - 1) if last else hi
                            if lo <= hi:
                                es.update(experts(u, lo, hi))
                        turn_h(a)
                        if not last or r + 3 < count:
                            turn_x(a.plus(3))
                        if not first or r > 0:
                            down(a.plus(-1), es[r - 1])
                        if not last or r + 2 < count:
                            up(a.plus(2), es[r + 2])
                    if last:
                        down(At(u, count - 1, 8), es[count - 1])

                turn_x(At(0, 0, 8))
                turn_x(At(0, 1, 8))
                es = experts(0, 0, 1)
                up(At(0, 0, 8), es[0])
                turn_x(At(0, 2, 8))
                up(At(0, 1, 8), es[1])
                turn(0, first=True)
                with pe.Fori(1, LAST) as u:
                    turn(u)
                turn(LAST, last=True)

            @block.scalar
            def _(act):
                def cut_x(a):
                    act.wait_ge(c_tx, a.i + 1)
                    at_least(act, c_g, a.i - 1)
                    nc.scalar.activation(x_hi[a.buf(2)][:], ps_x[a.buf(2)][:], ACT.Copy).then_inc(c_xhi, 1)

                def silu(a):
                    act.wait_ge(c_g, a.i + 1)
                    at_least(act, c_h, a.i - 1)
                    nc.scalar.activation(act1[a.buf(2)][:], ps_g[a.buf(2)][:, 0:FF], ACT.Tanh, scale=0.5
                                         ).then_inc(c_silu, 1)

                def cut_h(a):
                    act.wait_ge(c_th, a.i + 1)
                    at_least(act, c_y, a.i - 1)
                    nc.scalar.activation(h_hi[a.buf(2)][:], ps_h[a.buf(2)][:], ACT.Copy, scale=0.5).then_inc(c_hhi, 1)

                def result(a):
                    act.wait_ge(c_y, a.i + 1)
                    at_least(act, y_stored[a.buf(2)], a.uses(2) * 16)
                    nc.scalar.activation(y[a.buf(2)][:], ps_y[a.buf(2)][:], ACT.Copy).then_inc(c_yc, 1)

                def tile(a, first=False, left=3):
                    if left > 0:
                        silu(a.plus(1))
                    cut_h(a)
                    if left > 2:
                        cut_x(a.plus(3))
                    if not first:
                        result(a.plus(-1))

                cut_x(At(0, 0, 4))
                cut_x(At(0, 1, 4))
                silu(At(0, 0, 4))
                cut_x(At(0, 2, 4))

                def halves(u):
                    act.wait_ge(t_dif, u + 1)
                    at_least(act, t_exp_f, u)
                    at_least(act, t_exp, u)
                    nc.scalar.activation(sides[:, 0], dif[:], ACT.Relu)
                    nc.scalar.activation(sides[:, 1], dif[:], ACT.Relu, scale=-1.0).then_inc(t_sides, 1)

                def exps_decay(u):
                    act.wait_ge(t_sides, u)
                    if not isinstance(u, int) or u > 1:
                        act.wait_ge(t_est, u * 16 - 16)
                        act.wait_ge(t_bb, u - 1)
                    nc.scalar.activation(decays[:, 1], sides[:, :, 1], ACT.Exp, scale=-1.0).then_inc(t_exp, 1)

                def exps_first(u):
                    if not isinstance(u, int) or u > 1:
                        act.wait_ge(t_coef, u - 1)
                    nc.scalar.activation(decays[:, 0], sides[:, :, 0], ACT.Exp, scale=-1.0).then_inc(t_exp_f, 1)

                def turn(u):
                    for r in range(4):
                        tile(At(u, r, 4))
                        if r == 0:
                            exps_decay(u)
                        if r == 1:
                            exps_first(u)
                        if r == 3:
                            halves(u)

                for r in range(4):
                    tile(At(0, r, 4), first=(r == 0))
                halves(0)
                turn(1)
                with act.Fori(2, ROUNDS - 1) as u:
                    turn(u)
                act.wait_ge(c_ld, sum(map(len, loads)) * 16)
                for r in range(REST):
                    for raw, hi, _ in cuts[r:r + 1]:
                        nc.scalar.activation(hi[:], raw[:], ACT.Copy).then_inc(c_whi, 1)
                    tile(At(ROUNDS - 1, r, 4), left=REST - 1 - r)
                result(At(ROUNDS - 1, REST - 1, 4))

            @block.vector
            def _(dve):
                def cut_x(a):
                    dve.wait_ge(c_xhi, a.i + 1)
                    at_least(dve, c_g, a.i - 1)
                    nc.vector.tensor_tensor(x_lo[a.buf(2)][:], ps_x[a.buf(2)][:], x_hi[a.buf(2)][:].bitcast(F32),
                                            ALU.subtract).then_inc(c_xlo, 1)

                def gate(a):
                    dve.wait_ge(c_silu, a.i + 1)
                    nc.vector.scalar_tensor_tensor(out=act1[a.buf(2)][:], in0=act1[a.buf(2)][:], scalar=1.0,
                                                   in1=ps_g[a.buf(2)][:, 0:FF], op0=ALU.add, op1=ALU.mult
                                                   ).then_inc(c_gate, 1)

                def hidden(a):
                    dve.wait_ge(c_gate, a.i + 1)
                    at_least(dve, c_th, a.i - 1)
                    nc.vector.tensor_tensor(hid[a.buf(2)][:], ps_g[a.buf(2)][:, FF:2 * FF], act1[a.buf(2)][:],
                                            ALU.mult).then_inc(c_h, 1)

                def cut_h(a):
                    dve.wait_ge(c_hhi, a.i + 1)
                    at_least(dve, c_y, a.i - 1)
                    nc.vector.scalar_tensor_tensor(out=h_lo[a.buf(2)][:], in0=ps_h[a.buf(2)][:], scalar=0.5,
                                                   in1=h_hi[a.buf(2)][:].bitcast(F32), op0=ALU.mult,
                                                   op1=ALU.subtract).then_inc(c_hlo, 1)

                def tile(a, left=3):
                    if left > 0:
                        gate(a.plus(1))
                    cut_h(a)
                    if left > 0:
                        hidden(a.plus(1))
                    if left > 2:
                        cut_x(a.plus(3))

                def differences(u):
                    own = OwnIn(dve, t_own, At(u, 0, 1), 2)
                    if isinstance(u, int) and u == 0:
                        own.n += 1
                    else:
                        own.link(nc.vector.tensor_copy(s_p[:, :, 0:1], s_p[:, :, PIECE:PIECE + 1]))
                    for c in range(KC):
                        ins = nc.vector.tensor_tensor_scan(out=s_p[:, c, 1:PIECE + 1],
                                                           data0=grow[:, c:c + 1].broadcast_to([P, PIECE]),
                                                           data1=zero[:].broadcast_to([P, PIECE]),
                                                           initial=s_p[:, c, 0:1], op0=ALU.add, op1=ALU.add)
                    own.link(ins)
                    own.close()
                    at_least(dve, t_sides, u)
                    difference(0)
                    difference(1)

                def difference(i):
                    n, c = divmod(i, KC)
                    vec = (vec_tf, vec_td)[n]
                    ins = nc.vector.scalar_tensor_tensor(out=dif[:, n, c, :], in0=s_p[:, c, 0:PIECE],
                                                         scalar=vec[:, c:c + 1], in1=s_p[:, c, 0:PIECE],
                                                         op0=ALU.add, op1=ALU.subtract)
                    if i == 2 * KC - 1:
                        ins.then_inc(t_dif, 1)

                def scan_b(u):
                    dve.wait_ge(t_exp, u)
                    if not isinstance(u, int) or u > 1:
                        dve.wait_ge(t_den, u - 1)
                        nc.vector.tensor_copy(s_b[:, :, 0:1], s_b[:, :, PIECE:PIECE + 1]).then_inc(t_carry, 1)
                        dve.wait_ge(t_carry, u)
                    for c in range(KC):
                        ins = nc.vector.tensor_tensor_scan(out=s_b[:, c, 1:PIECE + 1], data0=decays[:, 1, 0, c, :],
                                                           data1=decays[:, 1, 1, c, :], initial=s_b[:, c, 0:1],
                                                           op0=ALU.mult, op1=ALU.add)
                    ins.then_inc(t_bb, 1)

                def invert(u, c):
                    dve.wait_ge(t_den, u)
                    ins = nc.vector.reciprocal(rden[:, c, :], den[:, c, :])
                    if c == KC - 1:
                        ins.then_inc(t_rec, 1)

                def turn(u):
                    for r in range(4):
                        tile(At(u, r, 4))
                        if r == 0:
                            differences(u)
                        if r == 1:
                            scan_b(u)
                            difference(2)
                        if r == 2:
                            difference(3)
                            invert(u, 0)
                        if r == 3:
                            invert(u, 1)

                nc.vector.memset(zero[:], 0.0)
                nc.vector.memset(s_b[:, :, 0:1], 0.0)
                nc.vector.memset(s_p[:, :, 0:1], -10000.0)
                nc.vector.tensor_scalar(grow[:], vec_td[:], 0.0, None, ALU.max).then_inc(t_own, 1)
                dve.wait_ge(t_own, 1)
                nc.vector.sem_inc(t_carry, 1)
                cut_x(At(0, 0, 4))
                cut_x(At(0, 1, 4))
                gate(At(0, 0, 4))
                hidden(At(0, 0, 4))
                cut_x(At(0, 2, 4))
                for r in range(4):
                    tile(At(0, r, 4))
                    if r == 1:
                        differences(0)
                    if r == 2:
                        difference(2)
                        difference(3)
                turn(1)
                with dve.Fori(2, ROUNDS - 1) as u:
                    turn(u)
                for r in range(REST):
                    tile(At(ROUNDS - 1, r, 4), left=REST - 1 - r)


def mix(nc, x, xT_d, y_d, y_stored, tab_d, out, slots, gates, vr_hi, vr_lo, raw_s13, raw_o, raw_s2,
        col0, col_hi0, col_lo0, vec_b1, vec_b3, row_b2):
    with ExitStack() as ctx:
        def sb(name, shape, dt):
            return ctx.enter_context(nc.sbuf_tensor(name, shape, dt))

        def bank(name, shape):
            return ctx.enter_context(nc.psum_tensor(name, shape, F32))

        def sem(name):
            return ctx.enter_context(nc.semaphore(name))

        s13_hi, s13_lo = (sb(f"s13_{s}", [P, KC, 2 * SF], F32R) for s in ("hi", "lo"))
        o_hi, o_lo = (sb(f"o_{s}", [P, KC, C], F32R) for s in ("hi", "lo"))
        s2_hi, s2_lo = (sb(f"s2_{s}", [P, KS, C], F32R) for s in ("hi", "lo"))
        splits = ((raw_s13, s13_hi, s13_lo), (raw_o, o_hi, o_lo), (raw_s2, s2_hi, s2_lo))
        xT = [col0, sb("col1", [P, KC, STEP], F32)]
        x_hi = [col_hi0, sb("col_hi1", [P, KC, STEP], F32R)]
        x_lo = [col_lo0, sb("col_lo1", [P, KC, STEP], F32R)]
        res = [sb(f"res{b}", [P, Q, C], F32) for b in range(2)]
        yg = [sb(f"yg{b}", [P, TOPK, Q, C], F32) for b in range(2)]
        picked = [sb(f"rows{b}", [P, TOPK, Q], I32) for b in range(2)]
        sa = sb("sa", [P, KC * B, TIMES + 1], F32)
        table = [sb(f"table{b}", [P, 4, KC, TIMES], F32) for b in range(2)]
        fed = sb("fed", [P, KC, B, TIMES], F32)
        part_a = sb("part_a", [P, KC, B, TIMES], F32)
        part_v = sb("part_v", [P, KC, B, TIMES], F32)
        th = sb("th", [P, KC, B, TIMES], F32)
        rw = sb("rw", [P, KC, B, TIMES], F32)
        a_hi = sb("a_hi", [P, KC, STEP], F32R)
        a_lo = sb("a_lo", [P, KC, STEP], F32R)
        act1 = [sb(f"sact{b}", [P, STEP], F32) for b in range(2)]
        hid = [sb(f"shid{b}", [P, STEP], F32) for b in range(2)]
        s_hi = sb("s_hi", [P, KS, STEP], F32R)
        s_lo = sb("s_lo", [P, KS, STEP], F32R)
        ps_v = bank("ps_v", [P, KC, STEP])
        ps_r = bank("ps_r", [P, KC, STEP])
        ps_w = [bank(f"ps_w{b}", [P, STEP]) for b in range(4)]

        b_xT = [sem(f"b_xT{b}") for b in range(2)]
        b_res = [sem(f"b_res{b}") for b in range(2)]
        b_ost = [sem(f"b_ost{b}") for b in range(2)]
        b_gath = [sem(f"b_gath{b}") for b in range(2)]
        b_idx = sem("b_idx")
        b_go = sem("b_go")
        b_whi = sem("b_whi")
        b_wlo = sem("b_wlo")
        b_xhi = sem("b_xhi")
        b_xlo = sem("b_xlo")
        b_xb = sem("b_xb")
        b_v = sem("b_v")
        b_r = sem("b_r")
        b_tanh = sem("b_tanh")
        b_rw = sem("b_rw")
        b_ahi = sem("b_ahi")
        b_alo = sem("b_alo")
        b_tab = [sem(f"b_tab{b}") for b in range(2)]
        b_z = sem("b_z")
        b_silu = sem("b_silu")
        b_h = sem("b_h")
        b_shi = sem("b_shi")
        b_slo = sem("b_slo")
        b_o = sem("b_o")
        b_fin = sem("b_fin")
        b_a = sem("b_a")
        b_slot = sem("b_slot")

        xv = x.rearrange("b (i h p) c -> i p b h c", h=HALF, p=P)
        ov = out.rearrange("b (i h p) c -> i p b h c", h=HALF, p=P)
        MIX = 6
        LAST = At(NSTEP // 2 - 1, 1, 2)

        def steps(eng, body):
            body(At(0, 0, 2), True, 2)
            body(At(0, 1, 2), False, 2)
            with eng.Fori(1, NSTEP // 2 - 1) as u:
                body(At(u, 0, 2), False, 2)
                body(At(u, 1, 2), False, 2)
            body(At(NSTEP // 2 - 1, 0, 2), False, 1)
            body(At(NSTEP // 2 - 1, 1, 2), False, 0)

        with nc.Block() as block:

            @block.sync
            def _(sp):
                def load_cols(a):
                    at_least(sp, b_xhi, a.i - 2)
                    at_least(sp, b_xlo, a.i - 2)
                    sp.dma_start(xT[a.buf(2)][:].rearrange("p k n -> p (k n)"),
                                 xT_d[:, ds(a.i, 1), :].rearrange("p o n -> p (o n)")).then_inc(b_xT[a.buf(2)], 16)

                def load_rows(a):
                    at_least(sp, b_ost[a.buf(2)], a.uses(2) * 32)
                    for b in range(B):
                        sp.dma_start(res[a.buf(2)][:, b * HALF:(b + 1) * HALF, :],
                                     xv[ds(a.i, 1), :, b, :, :].rearrange("o p h c -> p (o h) c")
                                     ).then_inc(b_res[a.buf(2)], 16)

                def load_table(a):
                    at_least(sp, b_a, a.i * MIX - MIX)
                    for h in range(TIMES // PIECE):
                        sp.dma_start(
                            table[a.buf(2)][:, :, :, h * PIECE:(h + 1) * PIECE].rearrange("p n k t -> p (n k) t"),
                            tab_d[ds(a.i * (TIMES // PIECE) + h, 1)].rearrange("o p n k t -> p (o n k) t")
                        ).then_inc(b_tab[a.buf(2)], 16)

                load_table(At(0, 0, 2))
                load_cols(At(0, 1, 2))
                load_table(At(0, 1, 2))
                load_rows(At(0, 0, 2))
                load_rows(At(0, 1, 2))

                def step(a, first, left):
                    if left > 1:
                        load_cols(a.plus(2))
                        load_table(a.plus(2))
                    for b in range(B):
                        sp.wait_ge(b_fin, a.i * Q + (b + 1) * HALF)
                        sp.dma_start(ov[ds(a.i, 1), :, b, :, :].rearrange("o p h c -> p (o h) c"),
                                     res[a.buf(2)][:, b * HALF:(b + 1) * HALF, :]).then_inc(b_ost[a.buf(2)], 16)
                    if left > 1:
                        load_rows(a.plus(2))

                steps(sp, step)
                for b in range(2):
                    sp.wait_ge(b_ost[b], NSTEP // 2 * 32)

            @block.gpsimd
            def _(pool):
                def gather(a):
                    at_least(pool, b_slot, a.i * TOPK - TOPK)
                    nc.gpsimd.tensor_copy(picked[a.buf(2)][:], slots[:, :, ds(a.i * Q, Q)]).then_inc(b_idx, 1)
                    pool.wait_ge(b_idx, a.i + 1)
                    pool.sem_inc(b_go, 1)
                    for k in range(TOPK):
                        for q in range(Q):
                            pool.indirect_dma_start(
                                out=yg[a.buf(2)][:, k, q, :], out_offset=None, in_=y_d[:, :],
                                in_offset=bass.IndirectOffsetOnAxis(ap=picked[a.buf(2)][:, k, q:q + 1], axis=0)
                            ).then_inc(b_gath[a.buf(2)], 16)

                def cut(a):
                    pool.wait_ge(b_xhi, a.i)
                    at_least(pool, b_z, a.i * KS - KS)
                    nc.gpsimd.tensor_tensor(x_lo[a.buf(2)][:], xT[a.buf(2)][:], x_hi[a.buf(2)][:].bitcast(F32),
                                            ALU.subtract).then_inc(b_xlo, 1)

                def bias(a):
                    pool.wait_ge(b_res[a.buf(2)], (a.uses(2) + 1) * 32)
                    nc.gpsimd.tensor_tensor(res[a.buf(2)][:], res[a.buf(2)][:],
                                            row_b2[:, None, :].broadcast_to([P, Q, C]), ALU.add).then_inc(b_xb, 1)

                def step(a, first, left):
                    bias(a)
                    if left > 0:
                        cut(a.plus(1))
                        gather(a.plus(1))

                for b in range(2):
                    pool.wait_ge(y_stored[b], (TILES + 1 - b) // 2 * 16)
                gather(At(0, 0, 2))
                steps(pool, step)

            @block.tensor
            def _(pe):
                def three(out, w_hi, w_lo, x_hi, x_lo, start, stop):
                    nc.tensor.matmul(out, w_hi, x_hi, start=start, stop=False)
                    nc.tensor.matmul(out, w_hi, x_lo, start=False, stop=False)
                    return nc.tensor.matmul(out, w_lo, x_hi, start=False, stop=stop)

                def columns(out, hi, lo, n0, xh, xl):
                    for k in range(KC):
                        mm = three(out, hi[:, k, n0:n0 + P], lo[:, k, n0:n0 + P], xh[:, k, :], xl[:, k, :],
                                   k == 0, k == KC - 1)
                    return mm

                def values(a):
                    at_least(pe, b_xlo, a.i)
                    at_least(pe, b_a, a.i * MIX - MIX + 2)
                    for m in range(KC):
                        mm = columns(ps_v[:, m, :], vr_hi, vr_lo, m * P, x_hi[a.buf(2)], x_lo[a.buf(2)])
                    mm.then_inc(b_v, 1)
                    at_least(pe, b_tanh, a.i)
                    for m in range(KC):
                        mm = columns(ps_r[:, m, :], vr_hi, vr_lo, C + m * P, x_hi[a.buf(2)], x_lo[a.buf(2)])
                    mm.then_inc(b_r, 1)

                def shared(a):
                    for m in range(KS):
                        if m < 2:
                            at_least(pe, b_fin, a.i * Q - Q + 2 * m + 2)
                        else:
                            pe.wait_ge(b_h, a.i * KS + m - 1)
                        columns(ps_w[m % 2 * 2][:], s13_hi, s13_lo, m * P, x_hi[a.buf(2)], x_lo[a.buf(2)])
                        columns(ps_w[m % 2 * 2 + 1][:], s13_hi, s13_lo, SF + m * P, x_hi[a.buf(2)],
                                x_lo[a.buf(2)]).then_inc(b_z, 1)

                def outputs(a, last=False):
                    def mixed(q):
                        for k in range(KC):
                            three_rows(ps_w[q][:, 0:C], a_hi, a_lo, k, slice(q * P, (q + 1) * P), o_hi, o_lo,
                                       k == 0, False)

                    def hidden(q, m):
                        return three_rows(ps_w[q][:, 0:C], s_hi, s_lo, m, slice(q * P, (q + 1) * P), s2_hi, s2_lo,
                                          False, m == KS - 1)

                    pe.wait_ge(b_alo, a.i + 1)
                    early = 2 if last else 0
                    if last:
                        pe.wait_ge(b_h, a.i * KS + KS - 1)
                        for q in range(early):
                            mixed(q)
                        for m in range(KS - 1):
                            pe.wait_ge(b_slo, a.i * KS + m + 1)
                            for q in range(early):
                                hidden(q, m)
                    pe.wait_ge(b_slo, a.i * KS + KS)
                    for q in range(Q):
                        if q < early:
                            mm = hidden(q, KS - 1)
                        else:
                            mixed(q)
                            for m in range(KS):
                                mm = hidden(q, m)
                        mm.then_inc(b_o, 1)

                def three_rows(out, hi, lo, k, cols, w_hi, w_lo, start, stop):
                    nc.tensor.matmul(out, hi[:, k, cols], w_hi[:, k, :], start=start, stop=False)
                    nc.tensor.matmul(out, hi[:, k, cols], w_lo[:, k, :], start=False, stop=False)
                    return nc.tensor.matmul(out, lo[:, k, cols], w_hi[:, k, :], start=False, stop=stop)

                def step(a, first, left):
                    values(a)
                    if first:
                        pe.wait_ge(b_wlo, 1)
                    else:
                        outputs(a.plus(-1))
                    shared(a)
                    if first:
                        pe.wait_ge(b_wlo, 3)

                steps(pe, step)
                outputs(LAST, last=True)

            @block.scalar
            def _(act):
                def cut_x(a):
                    act.wait_ge(b_xT[a.buf(2)], (a.uses(2) + a.buf(2)) * 16)
                    at_least(act, b_z, a.i * KS - KS)
                    nc.scalar.activation(x_hi[a.buf(2)][:], xT[a.buf(2)][:], ACT.Copy).then_inc(b_xhi, 1)

                def receive(a):
                    act.wait_ge(b_r, a.i + 1)
                    at_least(act, b_rw, a.i)
                    nc.scalar.activation(th[:].rearrange("p k b t -> p k (b t)"), ps_r[:], ACT.Tanh, scale=0.5
                                         ).then_inc(b_tanh, 1)

                def cut_a(a):
                    act.wait_ge(b_rw, a.i + 1)
                    at_least(act, b_o, a.i * Q)
                    nc.scalar.activation(a_hi[:], rw[:].rearrange("p k b t -> p k (b t)"), ACT.Copy
                                         ).then_inc(b_ahi, 1)

                def silu(a, m):
                    act.wait_ge(b_z, a.i * KS + m + 1)
                    at_least(act, b_h, a.i * KS + m - 1)
                    nc.scalar.activation(act1[m % 2][:], ps_w[m % 2 * 2][:], ACT.Silu, bias=vec_b1[:, m:m + 1]
                                         ).then_inc(b_silu, 1)

                def cut_s(a, m):
                    act.wait_ge(b_h, a.i * KS + m + 1)
                    at_least(act, b_o, a.i * Q)
                    nc.scalar.activation(s_hi[:, m, :], hid[m % 2][:], ACT.Copy).then_inc(b_shi, 1)

                def step(a, first, left):
                    receive(a)
                    if left > 0:
                        cut_x(a.plus(1))
                    second = isinstance(a.i, int) and a.i == 1
                    if second:
                        silu(a, 0)
                    if not first:
                        cut_a(a)
                    if not second:
                        silu(a, 0)
                    silu(a, 1)
                    if first:
                        cut_a(a)
                    for m in range(KS):
                        cut_s(a, m)
                        if m + 2 < KS:
                            silu(a, m + 2)

                for raw, hi, _ in splits:
                    nc.scalar.activation(hi[:], raw[:], ACT.Copy).then_inc(b_whi, 1)
                steps(act, step)

            @block.vector
            def _(dve):
                def wide(ap):
                    return ap[:, :, None, :].broadcast_to([P, KC, B, TIMES])

                def time_mix(a, first, second):
                    own = OwnIn(dve, b_a, a, MIX)
                    tab = table[a.buf(2)]
                    v = ps_v[:].rearrange("p k (b t) -> p k b t", b=B)
                    dve.wait_ge(b_v, a.i + 1)
                    dve.wait_ge(b_tab[a.buf(2)], (a.uses(2) + 1) * 32)
                    own.mark(nc.vector.tensor_tensor(fed[:], v, wide(tab[:, 1]), ALU.mult))
                    own.mark(nc.vector.tensor_tensor(part_v[:], v, wide(tab[:, 3]), ALU.mult))
                    own.wait()
                    for c in range(KC):
                        for b in range(B):
                            ins = nc.vector.tensor_tensor_scan(
                                out=sa[:, c * B + b, 1:TIMES + 1], data0=tab[:, 0, c, :], data1=fed[:, c, b, :],
                                initial=sa[:, c * B + b, 0:1], op0=ALU.mult, op1=ALU.add)
                    own.link(ins)
                    if first:
                        hidden(a, 0)
                    if second:
                        add_outputs(a.plus(-1), 0, 2)
                    own.link(nc.vector.tensor_tensor(
                        part_a[:], sa[:, :, 0:TIMES].rearrange("p (k b) t -> p k b t", k=KC), wide(tab[:, 2]),
                        ALU.mult))
                    if second:
                        add_outputs(a.plus(-1), 2, Q)
                    own.mark(nc.vector.tensor_copy(sa[:, :, 0:1], sa[:, :, TIMES:TIMES + 1]))
                    own.link(nc.vector.tensor_tensor(part_a[:], part_a[:], part_v[:], ALU.add))
                    own.close()

                def receive(a):
                    dve.wait_ge(b_tanh, a.i + 1)
                    at_least(dve, b_ahi, a.i)
                    nc.vector.scalar_tensor_tensor(
                        out=rw[:].rearrange("p k b t -> p (k b t)"), in0=th[:].rearrange("p k b t -> p (k b t)"),
                        scalar=1.0, in1=part_a[:].rearrange("p k b t -> p (k b t)"), op0=ALU.add, op1=ALU.mult
                    ).then_inc(b_rw, 1)

                def experts(a, g):
                    buf, k = a.buf(2), g // 2
                    if g == 0:
                        dve.wait_ge(b_xb, a.i + 1)
                        dve.wait_ge(b_gath[buf], (a.uses(2) + 1) * 16 * TOPK * Q)
                    if g == 2:
                        dve.wait_ge(b_slot, a.i * TOPK + 1)
                    for q in (g % 2 * 2, g % 2 * 2 + 1):
                        ins = nc.vector.scalar_tensor_tensor(
                            out=res[buf][:, q, :], in0=yg[buf][:, k, q, :],
                            scalar=gates[:, k, ds(a.i * Q + q, 1)], in1=res[buf][:, q, :],
                            op0=ALU.mult, op1=ALU.add)
                    if g % 2:
                        ins.then_inc(b_slot, 1)

                def add_outputs(a, q0=0, q1=Q):
                    dve.wait_ge(b_slot, a.i * TOPK + TOPK)
                    for q in range(q0, q1):
                        dve.wait_ge(b_o, a.i * Q + q + 1)
                        nc.vector.tensor_tensor(res[a.buf(2)][:, q, :], ps_w[q][:, 0:C], res[a.buf(2)][:, q, :], ALU.add
                                                ).then_inc(b_fin, 1)

                def cut_a(a):
                    dve.wait_ge(b_ahi, a.i + 1)
                    nc.vector.tensor_tensor(a_lo[:], rw[:].rearrange("p k b t -> p k (b t)"), a_hi[:].bitcast(F32),
                                            ALU.subtract).then_inc(b_alo, 1)

                def hidden(a, m):
                    dve.wait_ge(b_silu, a.i * KS + m + 1)
                    at_least(dve, b_shi, a.i * KS + m - 1)
                    at_least(dve, b_slo, a.i * KS + m - 1)
                    nc.vector.scalar_tensor_tensor(out=hid[m % 2][:], in0=ps_w[m % 2 * 2 + 1][:],
                                                   scalar=vec_b3[:, m:m + 1], in1=act1[m % 2][:],
                                                   op0=ALU.add, op1=ALU.mult).then_inc(b_h, 1)

                def cut_s(a, m):
                    dve.wait_ge(b_shi, a.i * KS + m + 1)
                    nc.vector.tensor_tensor(s_lo[:, m, :], hid[m % 2][:], s_hi[:, m, :].bitcast(F32), ALU.subtract
                                            ).then_inc(b_slo, 1)

                def step(a, first, left):
                    second = isinstance(a.i, int) and a.i == 1
                    time_mix(a, first, second)
                    if first:
                        hidden(a, 1)
                    receive(a)
                    if first:
                        experts(a, 0)
                    elif second:
                        hidden(a, 0)
                    else:
                        add_outputs(a.plus(-1))
                    cut_a(a)
                    if not first:
                        if not second:
                            hidden(a, 0)
                        experts(a, 0)
                        hidden(a, 1)
                    for m in range(KS):
                        cut_s(a, m)
                        if m < 2:
                            if not first:
                                experts(a, m + 1)
                            hidden(a, m + 2)
                        if m == (1 if left > 0 else KS - 1) and not first:
                            experts(a, 3)
                    if first:
                        for g in range(1, TOPK * 2):
                            experts(a, g)

                nc.vector.memset(sa[:, :, 0:1], 0.0)
                for n, (raw, hi, lo) in enumerate(splits):
                    dve.wait_ge(b_whi, n + 1)
                    nc.vector.tensor_tensor(lo[:], raw[:], hi[:].bitcast(F32), ALU.subtract).then_inc(b_wlo, 1)
                steps(dve, step)
                add_outputs(LAST)


_OUT = (B, T, C)


def kernel(**inputs):
    import numpy as np
    import concourse.bacc as bacc
    from concourse.bass_utils import run_bass_kernel_spmd as run

    def get(name):
        return np.asarray(inputs[name])

    def cols(name):
        return np.swapaxes(get(name), -1, -2)

    def by_partition(a):
        a = a.reshape(-1, P, *a.shape[1:])
        return np.swapaxes(a, 0, 1)

    arrays = {
        "x": get("L0_attn_x"),
        "decay": by_partition(get("L0_attn_time_decay")),
        "first": by_partition(get("L0_attn_time_first")),
        "wvr": np.concatenate([cols("L0_attn_value_w"), cols("L0_attn_recep_w")], axis=1),
        "wo": cols("L0_attn_out_w"),
        "gate_w": by_partition(cols("L0_ffn_gate_w")),
        "gate_b": get("L0_ffn_gate_b"),
        "w_all": np.concatenate([cols("L0_ffn_w1"), cols("L0_ffn_w3"), cols("L0_ffn_w2")], axis=2),
        "b_all": np.concatenate([get("L0_ffn_b1"), get("L0_ffn_b3"), get("L0_ffn_b2")], axis=1).reshape(-1),
        "ws13": np.concatenate([cols("L0_ffn_ws1"), cols("L0_ffn_ws3")], axis=1),
        "bs1": by_partition(get("L0_ffn_bs1")),
        "bs3": by_partition(get("L0_ffn_bs3")),
        "ws2": cols("L0_ffn_ws2"),
        "bs2": get("L0_ffn_bs2"),
    }
    arrays = {k: np.ascontiguousarray(v) for k, v in arrays.items()}
    nc = bacc.Bacc("TRN2", target_bir_lowering=False, num_devices=1)
    args = [nc.dram_tensor(k, v.shape, mybir.dt.from_np(v.dtype), kind="ExternalInput").ap()
            for k, v in arrays.items()]
    out = nc.dram_tensor("out", _OUT, F32, kind="ExternalOutput").ap()
    build(nc, *args, out)
    r = run(nc, [arrays], core_ids=[0])
    return r.results[0]["out"]
```
